# Optimizing a Trainium2 kernel written in Bass

```python
import numpy as np
import jax
import jax.numpy as jnp

def _softmax(x, axis=-1):
    return jax.nn.softmax(x, axis=axis)
def _gelu(x):
    return jax.nn.gelu(x, approximate=True)
def _silu(x):
    return jax.nn.silu(x)
def _sigmoid(x):
    return jax.nn.sigmoid(x)
def _layernorm(x, axis=-1, eps=1e-5):
    m = jnp.mean(x, axis=axis, keepdims=True)
    v = jnp.var(x, axis=axis, keepdims=True)
    return (x - m) / jnp.sqrt(v + eps)
def _scatter_add(tgt, idx, src, axis=0):
    return tgt.at[idx].add(src)
def _segment_sum(src, seg, n):
    return jax.ops.segment_sum(src, seg, n)

kernel_name = 'mk_conv_preact_d2_conv_nchw192_c01b93'

def setup_inputs(seed: int = 0):
    np.random.seed(seed)
    _w = jnp.asarray
    def _rec_inputs():
        import jax
        import jax.numpy as jnp
        _gk = jax.random.key(seed)
        x = -0.0002221 + 1 * jax.random.normal(jax.random.fold_in(_gk, 1), (32, 192, 64, 64), jnp.float32)
        return x
    x = _rec_inputs()
    def _L0_conv_setup():
        import jax, jax.numpy as jnp
        import numpy as np
        DIM = 192
        RES = 64
        NUM_HEADS = 4
        H_SP, W_SP = (RES, 4)
        SCALE = (DIM // NUM_HEADS) ** (-0.5)

        def conv2d(x, w, b, pad, groups=1):
            y = jax.lax.conv_general_dilated(x, w, window_strides=(1, 1), padding=[(pad, pad), (pad, pad)], dimension_numbers=('NCHW', 'OIHW', 'NCHW'), feature_group_count=groups)
            return y + b[None, :, None, None]

        def img2windows(img, H_sp, W_sp):
            B, C, H, W = img.shape
            x = img.reshape(B, C, H // H_sp, H_sp, W // W_sp, W_sp)
            return jnp.transpose(x, (0, 2, 4, 3, 5, 1)).reshape(-1, H_sp * W_sp, C)

        def windows2img(w, H_sp, W_sp, H, W):
            Bw = w.shape[0]
            B = Bw // (H // H_sp * (W // W_sp))
            x = w.reshape(B, H // H_sp, W // W_sp, H_sp, W_sp, -1)
            return jnp.transpose(x, (0, 5, 1, 3, 2, 4)).reshape(B, -1, H, W)

        def im2cswin(x):
            w = img2windows(x, H_SP, W_SP)
            Bw, L, C = w.shape
            return jnp.transpose(w.reshape(Bw, L, NUM_HEADS, C // NUM_HEADS), (0, 2, 1, 3))
        key = jax.random.key(seed)
        ks = jax.random.split(key, 11)
        s = 0.02
        return {'x': jax.random.normal(ks[0], (32, DIM, RES, RES), jnp.float32), 'w_qk': jax.random.normal(ks[1], (2 * DIM, DIM, 1, 1), jnp.float32) * s, 'b_qk': jnp.zeros((2 * DIM,), jnp.float32), 'w_q5': jax.random.normal(ks[2], (DIM, 1, 5, 5), jnp.float32) * s, 'b_q5': jnp.zeros((DIM,), jnp.float32), 'w_k5': jax.random.normal(ks[3], (DIM, 1, 5, 5), jnp.float32) * s, 'b_k5': jnp.zeros((DIM,), jnp.float32), 'w_v': jax.random.normal(ks[4], (DIM, DIM, 1, 1), jnp.float32) * s, 'b_v': jnp.zeros((DIM,), jnp.float32), 'w_cape': jax.random.normal(ks[5], (DIM, 1, 5, 5), jnp.float32) * s, 'b_cape': jnp.zeros((DIM,), jnp.float32)}
    _L0_conv_all = _L0_conv_setup()
    _L0_conv_in = {k: v for k, v in _L0_conv_all.items() if k in ('w_qk', 'b_qk', 'w_q5', 'b_q5', 'w_k5', 'b_k5', 'w_v', 'b_v', 'w_cape', 'b_cape', )}
    del _L0_conv_all

    def _L1_conv_setup():
        import math
        import jax, jax.numpy as jnp
        import numpy as np

        def _positionalencoding2d(d_model, height, width):
            pe = np.zeros((d_model, height, width), dtype=np.float32)
            dm = d_model // 2
            div_term = np.exp(np.arange(0.0, dm, 2.0) * -(math.log(10000.0) / dm))
            pos_w = np.arange(0.0, width)[:, None]
            pos_h = np.arange(0.0, height)[:, None]
            sw = np.sin(pos_w * div_term).T[:, None, :]
            cw = np.cos(pos_w * div_term).T[:, None, :]
            sh = np.sin(pos_h * div_term).T[:, :, None]
            ch = np.cos(pos_h * div_term).T[:, :, None]
            pe[0:dm:2] = np.repeat(sw, height, axis=1)
            pe[1:dm:2] = np.repeat(cw, height, axis=1)
            pe[dm::2] = np.repeat(sh, width, axis=2)
            pe[dm + 1::2] = np.repeat(ch, width, axis=2)
            return pe

        def _distance_tensor(k):
            i = np.arange(k, dtype=np.float32) + 0.5 - k / 2.0
            d = np.sqrt(i[:, None] ** 2 + i[None, :] ** 2)
            return d.astype(np.float32)
        B, DIM, H, W = (64, 192, 56, 56)
        K, FEMB, FORD = (55, 32, 64)
        key = jax.random.key(seed)
        ks = jax.random.split(key, 5)
        x = jax.random.normal(ks[0], (B, DIM, H, W), dtype=jnp.float32)
        z = jnp.asarray(_positionalencoding2d(FEMB, K, K))[None]
        distance_map = jnp.asarray(_distance_tensor(K))[None, None]
        fast, slow, target = (0.3, 1.5, 0.01)
        max_d, min_d = (math.log(target) / fast, math.log(target) / slow)
        deltas = (jnp.linspace(min_d, max_d, DIM, dtype=jnp.float32) / K)[None, :, None, None]
        s1 = 1.0 / math.sqrt(FEMB)
        s2 = 1.0 / math.sqrt(FORD)
        W1 = jax.random.normal(ks[1], (FORD, FEMB), dtype=jnp.float32) * s1
        W2 = jax.random.normal(ks[2], (FORD, FORD), dtype=jnp.float32) * s2
        W3 = jax.random.normal(ks[3], (DIM, FORD), dtype=jnp.float32) * s2
        b1 = jnp.zeros((FORD,), jnp.float32)
        b2 = jnp.zeros((FORD,), jnp.float32)
        f1 = jnp.ones((1, FORD, 1, 1), jnp.float32)
        f2 = jnp.ones((1, FORD, 1, 1), jnp.float32)
        shift = jnp.zeros((1, DIM, 1, 1), jnp.float32)
        bias = jax.random.normal(ks[4], (1, DIM, 1, 1), dtype=jnp.float32)
        return {'x': x, 'z': z, 'W1': W1, 'b1': b1, 'f1': f1, 'W2': W2, 'b2': b2, 'f2': f2, 'W3': W3, 'deltas': deltas, 'shift': shift, 'bias': bias, 'distance_map': distance_map}
    _L1_conv_all = _L1_conv_setup()
    _L1_conv_in = {k: v for k, v in _L1_conv_all.items() if k in ('z', 'W1', 'b1', 'f1', 'W2', 'b2', 'f2', 'W3', 'deltas', 'shift', 'bias', 'distance_map', )}
    del _L1_conv_all

    return {
        "x": x,
        "L0_conv_w_qk": _L0_conv_in["w_qk"],
        "L0_conv_b_qk": _L0_conv_in["b_qk"],
        "L0_conv_w_q5": _L0_conv_in["w_q5"],
        "L0_conv_b_q5": _L0_conv_in["b_q5"],
        "L0_conv_w_k5": _L0_conv_in["w_k5"],
        "L0_conv_b_k5": _L0_conv_in["b_k5"],
        "L0_conv_w_v": _L0_conv_in["w_v"],
        "L0_conv_b_v": _L0_conv_in["b_v"],
        "L0_conv_w_cape": _L0_conv_in["w_cape"],
        "L0_conv_b_cape": _L0_conv_in["b_cape"],
        "L1_conv_z": _L1_conv_in["z"],
        "L1_conv_W1": _L1_conv_in["W1"],
        "L1_conv_b1": _L1_conv_in["b1"],
        "L1_conv_f1": _L1_conv_in["f1"],
        "L1_conv_W2": _L1_conv_in["W2"],
        "L1_conv_b2": _L1_conv_in["b2"],
        "L1_conv_f2": _L1_conv_in["f2"],
        "L1_conv_W3": _L1_conv_in["W3"],
        "L1_conv_deltas": _L1_conv_in["deltas"],
        "L1_conv_shift": _L1_conv_in["shift"],
        "L1_conv_bias": _L1_conv_in["bias"],
        "L1_conv_distance_map": _L1_conv_in["distance_map"],
    }

def reference(x, L0_conv_w_qk, L0_conv_b_qk, L0_conv_w_q5, L0_conv_b_q5, L0_conv_w_k5, L0_conv_b_k5, L0_conv_w_v, L0_conv_b_v, L0_conv_w_cape, L0_conv_b_cape, L1_conv_z, L1_conv_W1, L1_conv_b1, L1_conv_f1, L1_conv_W2, L1_conv_b2, L1_conv_f2, L1_conv_W3, L1_conv_deltas, L1_conv_shift, L1_conv_bias, L1_conv_distance_map):
    import jax
    import jax.numpy as jnp
    def _L0_conv_ref(x, w_qk, b_qk, w_q5, b_q5, w_k5, b_k5, w_v, b_v, w_cape, b_cape):
        import jax, jax.numpy as jnp
        import numpy as np
        DIM = 192
        RES = 64
        NUM_HEADS = 4
        H_SP, W_SP = (RES, 4)
        SCALE = (DIM // NUM_HEADS) ** (-0.5)

        def conv2d(x, w, b, pad, groups=1):
            y = jax.lax.conv_general_dilated(x, w, window_strides=(1, 1), padding=[(pad, pad), (pad, pad)], dimension_numbers=('NCHW', 'OIHW', 'NCHW'), feature_group_count=groups)
            return y + b[None, :, None, None]

        def img2windows(img, H_sp, W_sp):
            B, C, H, W = img.shape
            x = img.reshape(B, C, H // H_sp, H_sp, W // W_sp, W_sp)
            return jnp.transpose(x, (0, 2, 4, 3, 5, 1)).reshape(-1, H_sp * W_sp, C)

        def windows2img(w, H_sp, W_sp, H, W):
            Bw = w.shape[0]
            B = Bw // (H // H_sp * (W // W_sp))
            x = w.reshape(B, H // H_sp, W // W_sp, H_sp, W_sp, -1)
            return jnp.transpose(x, (0, 5, 1, 3, 2, 4)).reshape(B, -1, H, W)

        def im2cswin(x):
            w = img2windows(x, H_SP, W_SP)
            Bw, L, C = w.shape
            return jnp.transpose(w.reshape(Bw, L, NUM_HEADS, C // NUM_HEADS), (0, 2, 1, 3))
        B, C, H, W = x.shape
        qk = conv2d(x, w_qk, b_qk, pad=0)
        q, k = jnp.split(qk, 2, axis=1)
        v = conv2d(x, w_v, b_v, pad=0)
        cape = conv2d(v, w_cape, b_cape, pad=2, groups=DIM)
        q = im2cswin(conv2d(q, w_q5, b_q5, pad=2, groups=DIM) + cape)
        k = im2cswin(conv2d(k, w_k5, b_k5, pad=2, groups=DIM) + cape)
        vw = im2cswin(v)
        q = q * SCALE
        attn = jnp.einsum('whqd,whkd->whqk', q, k)
        attn = jax.nn.softmax(attn, axis=-1)
        out = jnp.einsum('whqk,whkd->whqd', attn, vw)
        Bw = out.shape[0]
        out = jnp.transpose(out, (0, 2, 1, 3)).reshape(Bw, H_SP * W_SP, C)
        return windows2img(out, H_SP, W_SP, H, W) + cape

    def _L1_conv_ref(x, z, W1, b1, f1, W2, b2, f2, W3, deltas, shift, bias, distance_map):
        import math
        import jax, jax.numpy as jnp
        import numpy as np

        def _positionalencoding2d(d_model, height, width):
            pe = np.zeros((d_model, height, width), dtype=np.float32)
            dm = d_model // 2
            div_term = np.exp(np.arange(0.0, dm, 2.0) * -(math.log(10000.0) / dm))
            pos_w = np.arange(0.0, width)[:, None]
            pos_h = np.arange(0.0, height)[:, None]
            sw = np.sin(pos_w * div_term).T[:, None, :]
            cw = np.cos(pos_w * div_term).T[:, None, :]
            sh = np.sin(pos_h * div_term).T[:, :, None]
            ch = np.cos(pos_h * div_term).T[:, :, None]
            pe[0:dm:2] = np.repeat(sw, height, axis=1)
            pe[1:dm:2] = np.repeat(cw, height, axis=1)
            pe[dm::2] = np.repeat(sh, width, axis=2)
            pe[dm + 1::2] = np.repeat(ch, width, axis=2)
            return pe

        def _distance_tensor(k):
            i = np.arange(k, dtype=np.float32) + 0.5 - k / 2.0
            d = np.sqrt(i[:, None] ** 2 + i[None, :] ** 2)
            return d.astype(np.float32)
        h = jnp.einsum('bchw,oc->bohw', z, W1) + b1[None, :, None, None]
        h = jnp.sin(f1 * h)
        h = jnp.einsum('bchw,oc->bohw', h, W2) + b2[None, :, None, None]
        h = jnp.sin(f2 * h)
        k = jnp.einsum('bchw,oc->bohw', h, W3)
        decay = jnp.exp(-distance_map * jnp.abs(deltas))
        k = k * (decay + shift)
        B, C, H, W = x.shape
        Kh, Kw = (k.shape[-2], k.shape[-1])
        s = (H + Kh - 1, W + Kw - 1)
        xf = jnp.fft.rfft2(x, s)
        kf = jnp.fft.rfft2(k[0], s)
        y = jnp.fft.irfft2(xf * kf[None], s)
        y = y[..., Kh // 2:Kh // 2 + H, Kw // 2:Kw // 2 + W]
        return y + bias * x

    def _gn(v, G=32, eps=1e-5):
        B_, C_, H_, W_ = v.shape
        g = v.reshape(B_, G, C_ // G, H_, W_)
        m = jnp.mean(g, axis=(2, 3, 4), keepdims=True)
        s = jnp.var(g, axis=(2, 3, 4), keepdims=True)
        return ((g - m) / jnp.sqrt(s + eps)).reshape(v.shape)

    def _ln_c(v, eps=1e-6):
        m = jnp.mean(v, axis=1, keepdims=True)
        s = jnp.var(v, axis=1, keepdims=True)
        return (v - m) / jnp.sqrt(s + eps)

    def _ln_t(v, eps=1e-5):
        m = jnp.mean(v, axis=-1, keepdims=True)
        s = jnp.var(v, axis=-1, keepdims=True)
        return (v - m) / jnp.sqrt(s + eps)

    def _to_tokens(v):
        B_, C_, H_, W_ = v.shape
        return v.reshape(B_, C_, H_ * W_).transpose(0, 2, 1)
    def _from_tokens(t, like):
        B_, C_, H_, W_ = like.shape
        return t.transpose(0, 2, 1).reshape(B_, C_, H_, W_)

    x = x + _L0_conv_ref(_gn(x), L0_conv_w_qk, L0_conv_b_qk, L0_conv_w_q5, L0_conv_b_q5, L0_conv_w_k5, L0_conv_b_k5, L0_conv_w_v, L0_conv_b_v, L0_conv_w_cape, L0_conv_b_cape)
    x = x + _L1_conv_ref(_gn(x), L1_conv_z, L1_conv_W1, L1_conv_b1, L1_conv_f1, L1_conv_W2, L1_conv_b2, L1_conv_f2, L1_conv_W3, L1_conv_deltas, L1_conv_shift, L1_conv_bias, L1_conv_distance_map)
    return x


_drawn_inputs = setup_inputs


def setup_inputs(seed=0):
    import zlib

    import numpy as np

    out = dict(_drawn_inputs(seed))
    spreads = {'L0_conv_b_qk': (0.0, 0.8),
     'L0_conv_b_q5': (0.0, 0.8),
     'L0_conv_b_k5': (0.0, 0.8),
     'L0_conv_b_v': (0.0, 0.1),
     'L0_conv_b_cape': (0.0, 0.1),
     'L1_conv_b1': (0.0, 0.1),
     'L1_conv_f1': (1.0, 0.2),
     'L1_conv_b2': (0.0, 0.1),
     'L1_conv_f2': (1.0, 0.2),
     'L1_conv_shift': (0.0, 0.1)}
    factors = {'L0_conv_w_qk': 8.0, 'L0_conv_w_q5': 8.0, 'L0_conv_w_k5': 8.0}
    for name, (base, spread) in spreads.items():
        noise = np.random.default_rng([zlib.crc32(name.encode()), seed]).standard_normal(out[name].shape)
        drawn = base * np.exp(spread * noise) if base else spread * noise
        out[name] = jnp.asarray(drawn.astype(out[name].dtype))
    for name, factor in factors.items():
        out[name] = (out[name] * factor).astype(out[name].dtype)
    return out
```

```python
from contextlib import ExitStack

import concourse.bass as bass
from concourse import mybir


F32 = mybir.dt.float32
F32R = mybir.dt.float32r
ALU = mybir.AluOpType
ACT = mybir.ActivationFunctionType
AX = mybir.AxisListType

P = 128
IMAGES, CHANNELS, HEIGHT, WIDTH = 32, 192, 64, 64
PW = 2
WP = WIDTH // PW
WH = WP // 2
HALVES = 2 * IMAGES
C8 = 8
CG = CHANNELS // C8
KC = 2
KP = CHANNELS // KC
QKV = 3 * CHANNELS
NORM_GROUPS = 32
PER_NORM = CHANNELS // NORM_GROUPS
NORM_COUNT = PER_NORM * HEIGHT * WIDTH
EPS = 1e-5
HEADS = 4
HD = CHANNELS // HEADS
HP = 64
TOKENS = 2 * P
WINDOWS = IMAGES * WP // 2
SCALE = HD ** -0.5

K5, PAD5 = 5, 2
K55, PAD55 = 55, 27
HID, EMB = 64, 32


def toeplitz(k, pad):
    far = (pad + 1) // PW
    u = PW * (2 * far + 1)
    return far, u, (2 * HEIGHT - 1) * u + 2


FAR5, U5, LEN5 = toeplitz(K5, PAD5)
FAR55, U55, LEN55 = toeplitz(K55, PAD55)


def view(ap, offset, dims):
    return bass.AP(tensor=ap.tensor, offset=ap.offset + offset, ap=[ap.ap[0], *dims])


def matmul3(pe, out, w_hi, w_lo, x_hi, x_lo, start, stop):
    pe.matmul(out, w_hi, x_hi, start=start, stop=False)
    pe.matmul(out, w_hi, x_lo, start=False, stop=False)
    return pe.matmul(out, w_lo, x_hi, start=False, stop=stop)


def filter_phase(nc, a, kpad):
    inv2pi, magic = 0.15915494309189535, 12582912.0
    c1, c2 = 6.28125, 0.0019353071795864769
    pi = 3.1415925
    n_pix = K55 * K55
    rows = [(r, min(8, K55 - r)) for r in range(0, K55, 8)]
    with ExitStack() as ctx:
        sb = lambda n, s, d=F32: ctx.enter_context(nc.sbuf_tensor(n, s, d))
        sem = lambda n: ctx.enter_context(nc.semaphore(n))
        z = sb("f_z", [EMB, n_pix])
        w1 = sb("f_w1", [EMB, HID])
        w2 = sb("f_w2", [HID, HID])
        w3 = sb("f_w3", [HID, CHANNELS])
        hid = sb("f_hid", [HID, 4])
        chan = sb("f_chan", [KP, 3, KC])
        dist = sb("f_dist", [KP, n_pix])
        slope = sb("f_slope", [KP, KC])
        decay = sb("f_decay", [KP, KC, n_pix])
        arg = sb("f_arg", [HID, n_pix])
        turns = sb("f_turns", [HID, n_pix])
        h1 = sb("f_h1", [HID, n_pix])
        h2 = sb("f_h2", [HID, n_pix])
        padded = sb("f_padded", [KP, KC, LEN55])
        ps = ctx.enter_context(nc.psum_tensor("f_ps", [P, 8, 512], F32))
        loaded, cleared, products, steps, funcs, stored = (
            sem(n) for n in ("f_loaded", "f_cleared", "f_products", "f_steps", "f_funcs", "f_stored"))
        LOADS = 7
        block = ctx.enter_context(nc.Block())

        @block.sync
        def _(sp):
            for dst, src in ((z[:, :], a["z"]), (w1[:, :], a["w1t"]), (w2[:, :], a["w2t"]),
                             (w3[:, :], a["w3t"]), (hid[:, :], a["hid"]), (chan[:, :, :], a["chan"]),
                             (dist[:, :], a["dist"].partition_broadcast(KP))):
                sp.dma_start(dst, src).then_inc(loaded, 16)
            sp.wait_ge(steps, 28)
            for k in range(KC):
                sp.dma_start(kpad[k * KP:(k + 1) * KP, :], padded[:, k, :]).then_inc(stored, 16)
            sp.wait_ge(stored, 16 * KC)

        @block.gpsimd
        def _(pool):
            pool.memset(padded[:, :, :], 0.0).then_inc(cleared, 1)

        @block.tensor
        def _(pe):
            pe.wait_ge(loaded, 16 * LOADS)
            for i, (r, n) in enumerate(rows):
                m = pe.matmul(ps[0:HID, i, 0:n * K55], w1[:, :], z[:, r * K55:(r + n) * K55],
                              start=True, stop=True)
            m.then_inc(products, 1)
            pe.wait_ge(funcs, 3)
            for i, (r, n) in enumerate(rows):
                m = pe.matmul(ps[0:HID, i, 0:n * K55], w2[:, :], h1[:, r * K55:(r + n) * K55],
                              start=True, stop=True)
            m.then_inc(products, 1)
            pe.wait_ge(funcs, 4)
            for k in range(KC):
                if k:
                    pe.wait_ge(steps, 20)
                for i, (r, n) in enumerate(rows):
                    m = pe.matmul(ps[0:KP, i, 0:n * K55], w3[:, k * KP:(k + 1) * KP],
                                  h2[:, r * K55:(r + n) * K55], start=True, stop=True)
                m.then_inc(products, 1)

        @block.scalar
        def _(act):
            act.wait_ge(steps, 1)
            for k in range(KC):
                act.activation(decay[:, k, :], dist[:, :], ACT.Exp, scale=slope[:, k:k + 1]).then_inc(funcs, 1)
            act.wait_ge(steps, 7)
            act.activation(h1[:, :], turns[:, :], ACT.Sin).then_inc(funcs, 1)
            act.wait_ge(steps, 13)
            act.activation(h2[:, :], turns[:, :], ACT.Sin).then_inc(funcs, 1)

        @block.vector
        def _(dve):
            done = [0]

            def step(ins):
                done[0] += 1
                ins.then_inc(steps, 1)
                dve.wait_ge(steps, done[0])

            dve.wait_ge(loaded, 16 * LOADS)
            step(dve.scalar_tensor_tensor(slope[:, :], chan[:, 0, :], -1.0, chan[:, 0, :], ALU.mult, ALU.min))
            for layer in range(2):
                dve.wait_ge(products, layer + 1)
                if layer:
                    dve.wait_ge(funcs, 3)
                for i, (r, n) in enumerate(rows):
                    m = dve.tensor_scalar(arg[:, r * K55:(r + n) * K55], ps[0:HID, i, 0:n * K55],
                                          hid[:, 2 * layer:2 * layer + 1], hid[:, 2 * layer + 1:2 * layer + 2],
                                          ALU.add, ALU.mult)
                step(m)
                step(dve.tensor_scalar(turns[:, :], arg[:, :], inv2pi, magic, ALU.mult, ALU.add))
                step(dve.tensor_scalar(turns[:, :], turns[:, :], magic, None, ALU.subtract))
                step(dve.scalar_tensor_tensor(arg[:, :], turns[:, :], -c1, arg[:, :], ALU.mult, ALU.add))
                step(dve.scalar_tensor_tensor(arg[:, :], turns[:, :], -c2, arg[:, :], ALU.mult, ALU.add))
                step(dve.tensor_scalar(turns[:, :], arg[:, :], pi, -pi, ALU.min, ALU.max))
            dve.wait_ge(cleared, 1)
            for k in range(KC):
                dve.wait_ge(products, 3 + k)
                for i, (r, n) in enumerate(rows):
                    dst = view(padded[:, k, :], (HEIGHT - 1 - PAD55 + r) * U55 + 2, [[U55, n], [1, K55]])
                    step(dve.scalar_tensor_tensor(
                        dst, decay[:, k, r * K55:(r + n) * K55].rearrange("p (a b) -> p a b", b=K55),
                        chan[:, 1, k:k + 1], ps[0:KP, i, 0:n * K55].rearrange("p (a b) -> p a b", b=K55),
                        ALU.add, ALU.mult))
            centre = (HEIGHT - 1 - PAD55 + PAD55) * U55 + 2 + PAD55
            assert done[0] == 27, done[0]
            for k in range(KC):
                m = dve.tensor_tensor(padded[:, k, centre:centre + 1], padded[:, k, centre:centre + 1],
                                      chan[:, 2, k:k + 1], ALU.add)
            step(m)


def stats0_phase(nc, a, rstd, shift):
    TILES = IMAGES * KC
    FM = 512
    NS = HEIGHT * WIDTH // FM
    SUB = 2 * NS
    with ExitStack() as ctx:
        sb = lambda n, s, d=F32: ctx.enter_context(nc.sbuf_tensor(n, s, d))
        sem = lambda n: ctx.enter_context(nc.semaphore(n))
        xt = sb("s_x", [KP, 4, HEIGHT * WIDTH])
        st = sb("s_stats", [KP, TILES, NS * 6])
        mask = sb("s_mask", [KP, KP])
        mean = sb("s_mean", [KP, TILES])
        dev = sb("s_dev", [KP, TILES, SUB])
        var = sb("s_var", [KP, TILES])
        t = sb("s_t", [KP, TILES])
        ps = ctx.enter_context(nc.psum_tensor("s_ps", [P, 2, 512], F32))
        landed = [sem(f"s_landed{i}") for i in range(4)]
        used, masked, steps, summed, rooted = (sem(n) for n in ("s_used", "s_masked", "s_steps", "s_summed", "s_rooted"))
        block = ctx.enter_context(nc.Block())

        @block.sync
        def _(sp):
            sp.dma_start(mask[:, :], a["mask"]).then_inc(masked, 16)
            sp.sem_inc(used, 4)
            with sp.Fori(0, IMAGES // 2) as m:
                i = m * 2
                for j in range(4):
                    sp.wait_ge(used, i * 2 + (j + 1))
                    src = a["x_ch"][bass.ds(i + j // 2, 1), (j % 2) * KP:(j % 2 + 1) * KP, :, :]
                    sp.dma_start(xt[:, j, :], src.rearrange("o c w n -> (o c) (w n)")).then_inc(landed[j], 16)

        @block.vector
        def _(dve):
            with dve.Fori(0, IMAGES // 2) as m:
                i = m * 2
                for j in range(4):
                    dve.wait_ge(landed[j], i * 8 + 16)
                    for s in range(NS):
                        m = dve.bn_stats(st[:, bass.ds(i * 2 + j, 1), s * 6:s * 6 + 6], xt[:, j, s * FM:(s + 1) * FM])
                    m.then_inc(used, 1)
            dve.wait_ge(used, TILES + 4)
            done = [0]

            def step(ins):
                done[0] += 1
                ins.then_inc(steps, 1)
                dve.wait_ge(steps, done[0])

            flat = st[:, :, :].rearrange("p t s -> p (t s)")
            part = lambda o: view(flat, o, [[NS * 6, TILES], [3, SUB]])
            wide = lambda v: view(v, 0, [[1, TILES], [0, SUB]])
            step(dve.tensor_reduce(t[:, :], part(1), AX.X, ALU.add))
            dve.wait_ge(summed, 1)
            step(dve.tensor_scalar(mean[:, :], ps[0:KP, 0, 0:TILES], 1.0 / (PER_NORM * SUB), None, ALU.mult))
            step(dve.tensor_tensor(dev[:, :, :], part(1), wide(mean[:, :]), ALU.subtract))
            step(dve.tensor_tensor(dev[:, :, :], dev[:, :, :], dev[:, :, :], ALU.mult))
            step(dve.scalar_tensor_tensor(dev[:, :, :], dev[:, :, :], FM / 2.0, part(2), ALU.mult, ALU.add))
            step(dve.tensor_reduce(t[:, :], dev[:, :, :], AX.X, ALU.add))
            dve.wait_ge(summed, 2)
            step(dve.tensor_scalar(var[:, :], ps[0:KP, 1, 0:TILES], 1.0 / NORM_COUNT, EPS, ALU.mult, ALU.add))
            dve.wait_ge(rooted, 1)
            step(dve.reciprocal(rstd[:, :], t[:, :]))
            newton(dve, step, rstd[:, :], var[:, :], t[:, :])
            step(dve.scalar_tensor_tensor(shift[:, :], mean[:, :], -1.0, rstd[:, :], ALU.mult, ALU.mult))

        @block.tensor
        def _(pe):
            pe.wait_ge(masked, 16)
            for n, after in enumerate((1, 6)):
                pe.wait_ge(steps, after)
                pe.matmul(ps[0:KP, n, 0:TILES], mask[:, :], t[:, :], start=True, stop=True).then_inc(summed, 1)

        @block.scalar
        def _(act):
            act.wait_ge(steps, 7)
            act.activation(t[:, :], var[:, :], ACT.Sqrt).then_inc(rooted, 1)


def newton(dve, step, y, v, t):
    step(dve.tensor_tensor(t, y, y, ALU.mult))
    step(dve.tensor_tensor(t, t, v, ALU.mult))
    step(dve.tensor_scalar(t, t, -0.5, 1.5, ALU.mult, ALU.add))
    step(dve.tensor_tensor(y, y, t, ALU.mult))


def project_phase(nc, a, rstd, shift, qkv):
    PX = WH * P
    NC = QKV // 2
    SLOTS = 4
    with ExitStack() as ctx:
        sb = lambda n, s, d=F32: ctx.enter_context(nc.sbuf_tensor(n, s, d))
        sem = lambda n: ctx.enter_context(nc.semaphore(n))
        x = [sb(f"a_x{i}", [KP, KC, PX]) for i in range(2)]
        xh = [sb(f"a_xh{i}", [KP + 1, KC, PX], F32R) for i in range(2)]
        xl = [sb(f"a_xl{i}", [KP, KC, PX], F32R) for i in range(2)]
        w = sb("a_w", [KP + 1, KC, QKV])
        wh = sb("a_wh", [KP + 1, KC, QKV], F32R)
        wl = sb("a_wl", [KP + 1, KC, QKV], F32R)
        tok = [sb(f"a_tok{i}", [P, QKV, WH]) for i in range(2)]
        ps = ctx.enter_context(nc.psum_tensor("a_ps", [P, SLOTS, 2, 512], F32))
        w_landed, w_split, ones = sem("a_w_landed"), sem("a_w_split"), sem("a_ones")
        x_landed = [sem(f"a_x_landed{i}") for i in range(2)]
        x_free, normed, hi, lo, parts_free, prod, prod_free = (
            sem(n) for n in ("a_x_free", "a_normed", "a_hi", "a_lo", "a_parts_free", "a_prod", "a_prod_free"))
        stored = [sem(f"a_stored{i}") for i in range(2)]
        block = ctx.enter_context(nc.Block())

        @block.sync
        def _(sp):
            sp.dma_start(w[:, :, :], a["w_qkv"]).then_inc(w_landed, 16)
            sp.sem_inc(x_free, 2)
            with sp.Fori(0, IMAGES) as i:
                for h in range(2):
                    sp.wait_ge(x_free, i * 2 + (h + 1))
                    src = a["x_ch"][bass.ds(i, 1), :, h, :]
                    sp.dma_start(x[h][:, :, :], src.rearrange("o (k c) n -> c (o k) n", k=KC)).then_inc(x_landed[h], 16)

        @block.gpsimd
        def _(pool):
            for h in range(2):
                pool.memset(xh[h][KP:KP + 1, :, :].bitcast(F32), 1.0).then_inc(ones, 1)

        @block.vector
        def _(dve):
            dve.wait_ge(w_split, 1)
            dve.tensor_tensor(wl[:, :, :], w[:, :, :], wh[:, :, :].bitcast(F32), ALU.subtract).then_inc(w_split, 1)
            with dve.Fori(0, IMAGES) as i:
                for h in range(2):
                    dve.wait_ge(x_landed[h], i * 16 + 16)
                    for k in range(KC):
                        dve.tensor_scalar(x[h][:, k, :], x[h][:, k, :], rstd[:, bass.ds(i * KC + k, 1)],
                                          shift[:, bass.ds(i * KC + k, 1)], ALU.mult, ALU.add).then_inc(normed, 1)
                    dve.wait_ge(hi, i * 2 + (h + 1))
                    dve.wait_ge(parts_free, i * 2 + (h + 1))
                    m = dve.tensor_tensor(xl[h][:, :, :], x[h][:, :, :], xh[h][0:KP, :, :].bitcast(F32), ALU.subtract)
                    m.then_inc(lo, 1)
                    dve.wait_ge(lo, i * 2 + (h + 1))
                    dve.sem_inc(x_free, 1)

        @block.scalar
        def _(act):
            act.wait_ge(w_landed, 16)
            act.activation(wh[:, :, :], w[:, :, :], ACT.Copy).then_inc(w_split, 1)
            act.sem_inc(prod_free, SLOTS)
            for h in range(2):
                act.sem_inc(stored[h], 48)

            def split(i, h):
                act.wait_ge(normed, i * 4 + 2 * (h + 1))
                act.wait_ge(parts_free, i * 2 + (h + 1))
                act.activation(xh[h][0:KP, :, :], x[h][:, :, :], ACT.Copy).then_inc(hi, 1)

            def take(i, h, n0, n1):
                for n in range(n0, n1):
                    act.wait_ge(prod, i * 32 + (h * WH + n + 1))
                    dst = tok[h][:, :, n].rearrange("p (a c) -> p a c", a=2)
                    act.activation(dst, ps[:, n % SLOTS, :, 0:NC], ACT.Copy).then_inc(prod_free, 1)

            def image(i, last):
                for h in range(2):
                    act.wait_ge(stored[h], i * 48 + 48)
                    take(i, h, 0, WH // 2)
                    if h == 0:
                        split(i, 1)
                    elif not last:
                        split(i + 1, 0)
                    take(i, h, WH // 2, WH)
                    act.wait_ge(prod_free, i * 32 + ((h + 1) * WH + SLOTS))
                    for s in range(3):
                        dst = qkv[s][:, :, bass.ds(i, 1), h, :].rearrange("g p o n -> p (g o) n")
                        src = tok[h][:, s * CHANNELS:(s + 1) * CHANNELS, :].rearrange("p (g c) w -> p g (c w)", c=C8)
                        act.dma_start(dst, src).then_inc(stored[h], 16)

            split(0, 0)
            with act.Fori(0, IMAGES - 1) as i:
                image(i, False)
            image(IMAGES - 1, True)
            for h in range(2):
                act.wait_ge(stored[h], 48 * (IMAGES + 1))

        @block.tensor
        def _(pe):
            pe.sem_inc(parts_free, 2)
            pe.wait_ge(w_split, 2)
            pe.wait_ge(ones, 2)
            with pe.Fori(0, IMAGES) as i:
                for h in range(2):
                    pe.wait_ge(hi, i * 2 + (h + 1))
                    pe.wait_ge(lo, i * 2 + (h + 1))
                    for n in range(WH):
                        pe.wait_ge(prod_free, i * 32 + (h * WH + n + 1))
                        px = slice(n * P, (n + 1) * P)
                        for c in range(2):
                            out = ps[:, n % SLOTS, c, 0:NC]
                            oc = slice(c * NC, (c + 1) * NC)
                            for k in range(KC):
                                r = KP + k
                                pe.matmul(out, xh[h][0:r, k, px], wh[0:r, k, oc], start=k == 0, stop=False)
                                pe.matmul(out, xh[h][0:r, k, px], wl[0:r, k, oc], start=False, stop=False)
                                m = pe.matmul(out, xl[h][:, k, px], wh[0:KP, k, oc], start=False, stop=k == 1)
                        m.then_inc(prod, 1)
                        if n == WH - 1:
                            pe.wait_ge(prod, i * 32 + (h + 1) * WH)
                            pe.sem_inc(parts_free, 1)


def depthwise_phase(nc, a, qkv, qkc):
    BH = IMAGES // 2
    TILE = BH * 2 * C8 * WH
    N = BH * WP
    S = 3
    STEPS = 2 * C8
    ORDER = (2, 0, 1)
    with ExitStack() as ctx:
        sb = lambda n, s, d=F32: ctx.enter_context(nc.sbuf_tensor(n, s, d))
        sem = lambda n: ctx.enter_context(nc.semaphore(n))
        raw = [sb(f"b_raw{i}", [P, S, TILE]) for i in range(2)]
        t5 = [sb(f"b_t{i}", [P, S, HEIGHT * U5]) for i in range(2)]
        th = [sb(f"b_th{i}", [P, S, U5 * HEIGHT], F32R) for i in range(2)]
        tl = [sb(f"b_tl{i}", [P, S, U5 * HEIGHT], F32R) for i in range(2)]
        xh = [sb(f"b_xh{i}", [P, S, N], F32R) for i in range(2)]
        xl = [sb(f"b_xl{i}", [P, S, N], F32R) for i in range(2)]
        bias = sb("b_bias", [P, S, CHANNELS])
        ps = ctx.enter_context(nc.psum_tensor("b_ps", [P, 2, S, 512], F32))
        landed = [sem(f"b_landed{i}") for i in range(2)]
        stored = [sem(f"b_stored{i}") for i in range(2)]
        t_landed = [sem(f"b_t_landed{i}") for i in range(2)]
        passed, b_landed, t_free, hi, lo, parts_free, prod, cape, done = (
            sem(n) for n in ("b_passed", "b_b_landed", "b_t_free", "b_hi", "b_lo", "b_parts_free", "b_prod", "b_cape", "b_done"))
        block = ctx.enter_context(nc.Block())

        def channel(tile, s, c):
            return view(raw[tile][:, s, :], c * WH, [[C8 * WH, 2], [1, WH], [2 * C8 * WH, BH]])

        def in_order(ap):
            return ap.rearrange("p (a w b) -> p a w b", a=2, w=WH)

        @block.sync
        def _(sp):
            sp.dma_start(bias[:, :, :].rearrange("p s c -> p (s c)"),
                         a["bias5"].partition_broadcast(P)).then_inc(b_landed, 16)
            for i in range(2):
                sp.sem_inc(stored[i], 48)

            def load(g, i):
                sp.wait_ge(stored[i], g * 48 + 48)
                for s in range(S):
                    src = qkv[s][bass.ds(g, 1), :, i * BH:(i + 1) * BH, :, :].rearrange("o p b h n -> (o p) (b h n)")
                    sp.dma_start(raw[i][:, s, :], src).then_inc(landed[i], 16)

            def store(g, i):
                sp.wait_ge(done, g * (4 * STEPS) + (i + 1) * 4 * C8 + 8)
                sp.sem_inc(passed, 1)
                for s in range(S):
                    dst = qkc[s][bass.ds(g, 1), :, i * BH:(i + 1) * BH, :, :].rearrange("o p b h n -> (o p) (b h n)")
                    sp.dma_start(dst, raw[i][:, s, :]).then_inc(stored[i], 16)

            load(0, 0)
            with sp.Fori(0, CG - 1) as g:
                load(g, 1)
                store(g, 0)
                load(g + 1, 0)
                store(g, 1)
            load(CG - 1, 1)
            store(CG - 1, 0)
            store(CG - 1, 1)
            for i in range(2):
                sp.wait_ge(stored[i], 48 * (CG + 1))

        @block.gpsimd
        def _(pool):
            pool.sem_inc(t_free, 2)
            with pool.Fori(0, CG) as g:
                for j in range(STEPS):
                    pool.wait_ge(t_free, g * STEPS + (j + 1))
                    pool.sem_inc(passed, 1)
                    row = a["w5"][:, bass.ds(g * C8 + j % C8, 1), :]
                    for s in range(S):
                        src = row[s]
                        src = bass.AP(tensor=src.tensor, offset=src.offset, ap=[[1, PW], [U5, HEIGHT], [1, HEIGHT * U5]])
                        pool.dma_start(t5[j % 2][:, s, :], src).then_inc(t_landed[j % 2], 16)

        @block.scalar
        def _(act):
            act.wait_ge(b_landed, 16)

            def split(g, j):
                i, p = j // C8, j % 2
                if j % C8 == 0:
                    act.wait_ge(landed[i], g * 48 + 48)
                act.wait_ge(parts_free, g * STEPS + (j + 1))
                for s in ORDER:
                    act.activation(in_order(xh[p][:, s, :]), channel(i, s, j % C8), ACT.Copy).then_inc(hi, 1)
                act.wait_ge(t_landed[p], g * (48 * C8) + 48 * (j // 2 + 1))
                src = view(t5[p][:, 0, :], HEIGHT * U5 - 1, [[HEIGHT * U5, S], [-1, U5], [-U5, HEIGHT]])
                act.activation(th[p][:, :, :].rearrange("p s (u h) -> p s u h", u=U5), src, ACT.Copy).then_inc(hi, 1)

            def take(g, j):
                act.wait_ge(prod, g * (S * STEPS) + (S * j + 1))
                act.sem_inc(passed, 1)
                act.activation(channel(j // C8 % 2, 2, j % C8), in_order(ps[:, j % 2, 0, :]), ACT.Identity,
                               bias=bias[:, 2, bass.ds(g * C8 + j % C8, 1)]).then_inc(cape, 1)

            def group(g, first):
                for j in range(STEPS):
                    split(g, j)
                    if j:
                        take(g, j - 1)
                    elif not first:
                        take(g - 1, STEPS - 1)

            group(0, True)
            with act.Fori(1, CG) as g:
                group(g, False)
            take(CG - 1, STEPS - 1)

        @block.vector
        def _(dve):
            dve.sem_inc(done, 8)
            dve.wait_ge(b_landed, 16)

            def split(g, j):
                i, p = j // C8, j % 2
                n = g * (4 * STEPS) + 4 * j
                for k, s in enumerate(ORDER):
                    dve.wait_ge(hi, n + (k + 1))
                    dve.tensor_tensor(in_order(xl[p][:, s, :]), channel(i, s, j % C8),
                                      in_order(xh[p][:, s, :]).bitcast(F32), ALU.subtract).then_inc(lo, 1)
                dve.wait_ge(hi, n + 4)
                src = view(t5[p][:, 0, :], HEIGHT * U5 - 1, [[HEIGHT * U5, S], [-1, U5], [-U5, HEIGHT]])
                dve.tensor_tensor(tl[p][:, :, :].rearrange("p s (u h) -> p s u h", u=U5), src,
                                  th[p][:, :, :].bitcast(F32).rearrange("p s (u h) -> p s u h", u=U5),
                                  ALU.subtract).then_inc(lo, 1)
                dve.wait_ge(lo, n + 4)
                dve.sem_inc(t_free, 1)

            def take(g, j):
                i, c = j // C8, j % C8
                dve.wait_ge(cape, g * STEPS + (j + 1))
                for s in (0, 1):
                    dve.wait_ge(prod, g * (S * STEPS) + (S * j + s + 2))
                    for h in range(2):
                        half = slice(h * WH * BH, (h + 1) * WH * BH)
                        at = lambda s: view(raw[i][:, s, :], (h * C8 + c) * WH, [[1, WH], [2 * C8 * WH, BH]])
                        dve.scalar_tensor_tensor(
                            at(s), ps[:, j % 2, 1 + s, half].rearrange("p (w b) -> p w b", w=WH),
                            bias[:, s, bass.ds(g * C8 + c, 1)], at(2), ALU.add, ALU.add).then_inc(done, 1)

            def group(g, first):
                for j in range(STEPS):
                    split(g, j)
                    if j:
                        take(g, j - 1)
                    elif not first:
                        take(g - 1, STEPS - 1)

            group(0, True)
            with dve.Fori(1, CG) as g:
                group(g, False)
            take(CG - 1, STEPS - 1)

        @block.tensor
        def _(pe):
            pe.sem_inc(parts_free, 2)
            with pe.Fori(0, (CG * STEPS) // 2) as m:
                n = m * 2
                for p in range(2):
                    pe.wait_ge(lo, n * 4 + 4 * (p + 1))
                    pe.wait_ge(done, n * 4 + 4 * (p + 1))
                    for k, s in enumerate(ORDER):
                        for d in (0, -1, 1):
                            wt = slice((2 * d + 2 * FAR5) * HEIGHT, (2 * d + 2 * FAR5 + 2) * HEIGHT)
                            o0, o1 = max(0, d) * BH, (WP + min(0, d)) * BH
                            m = matmul3(pe, ps[:, p, k, o0:o1], th[p][:, s, wt], tl[p][:, s, wt],
                                        xh[p][:, s, o0 - d * BH:o1 - d * BH], xl[p][:, s, o0 - d * BH:o1 - d * BH],
                                        start=d == 0, stop=d == 1)
                        m.then_inc(prod, 1)
                    pe.wait_ge(prod, n * S + S * (p + 1))
                    pe.sem_inc(parts_free, 1)


def attention_phase(nc, a, qkv, qkc, x1, stats):
    HALF = CG * C8 * WH
    HW = WH // 2
    PARTS = HW - 1
    with ExitStack() as ctx:
        sb = lambda n, s, d=F32: ctx.enter_context(nc.sbuf_tensor(n, s, d))
        sem = lambda n: ctx.enter_context(nc.semaphore(n))
        rqk = [sb(f"c_rqk{i}", [P, 2, HALF]) for i in range(2)]
        rv = [sb(f"c_rv{i}", [P, HALF]) for i in range(2)]
        rcx = [sb(f"c_rcx{i}", [P, 2, HALF]) for i in range(2)]
        x1t = [sb(f"c_x1t{i}", [P, HALF]) for i in range(2)]
        qk = [sb(f"c_qk{i}", [P, 2, 2, HEADS * HP]) for i in range(2)]
        vs = [sb(f"c_v{i}", [P, 2, HEADS, HP]) for i in range(2)]
        qkh = [sb(f"c_qkh{i}", [P, 2, 2, TOKENS], F32R) for i in range(2)]
        qkl = [sb(f"c_qkl{i}", [P, 2, 2, TOKENS], F32R) for i in range(2)]
        prob = sb("c_prob", [P, 4, 2, TOKENS])
        probT = [sb(f"c_probT{i}", [P, 2, TOKENS]) for i in range(2)]
        nmax = sb("c_nmax", [P, 4, 2])
        rden = [sb(f"c_rden{i}", [P, 2 * HEADS]) for i in range(2)]
        attn = [sb(f"c_attn{i}", [P, 2 * CHANNELS]) for i in range(2)]
        st = [sb(f"c_st{i}", [P, NORM_GROUPS * 6]) for i in range(2)]
        ident = sb("c_ident", [P, P])
        ps_s = ctx.enter_context(nc.psum_tensor("c_ps_s", [P, 2, 512], F32))
        ps_p = ctx.enter_context(nc.psum_tensor("c_ps_p", [P, 2, 512], F32))
        ps_t = ctx.enter_context(nc.psum_tensor("c_ps_t", [P, 2, 512], F32))
        ps_o = ctx.enter_context(nc.psum_tensor("c_ps_o", [P, 2, 512], F32))

        qk_landed = [sem(f"c_qk_landed{i}") for i in range(2)]
        v_landed = [sem(f"c_v_landed{i}") for i in range(2)]
        cx_landed = [sem(f"c_cx_landed{i}") for i in range(2)]
        x1_stored = [sem(f"c_x1_stored{i}") for i in range(2)]
        st_stored = [sem(f"c_st_stored{i}") for i in range(2)]
        passed = sem("c_passed")
        probs_sb = [sem(f"c_probs_sb{i}") for i in range(2)]
        (id_landed, cleared, qk_staged, v_staged, cx_summed, x1_made, turned, turned_hi, turned_lo, scores,
         maxed, expd, probs_turned, pv, inverted, scaled, bn_done) = (sem("c_" + n) for n in (
             "id_landed", "cleared", "qk_staged", "v_staged", "cx_summed", "x1_made", "turned", "turned_hi",
             "turned_lo", "scores", "maxed", "expd", "probs_turned", "pv", "inverted", "scaled", "bn_done"))
        block = ctx.enter_context(nc.Block())

        def pair(t, w):
            return view(t, 2 * w, [[1, 2], [HD * WH, HEADS], [WH, HD]])

        @block.sync
        def _(sp):
            sp.dma_start(ident[:, :], a["ident"]).then_inc(id_landed, 16)

            def rows(t, i, h):
                return t[:, :, bass.ds(i, 1), h, :].rearrange("g p o n -> p (g o) n")

            def tile(t):
                return t.rearrange("p (g n) -> p g n", g=CG)

            def store(i, h):
                sp.wait_ge(x1_made, i * 16 + ((h + 1) * HW + 2))
                sp.dma_start(rows(x1, i, h), tile(x1t[h][:, :])).then_inc(x1_stored[h], 16)
                sp.wait_ge(bn_done, i * 2 + (h + 1))
                sp.dma_start(stats[:, bass.ds(i, 1), h, :].rearrange("p o n -> p (o n)"), st[h][:, :]).then_inc(st_stored[h], 16)

            def image(i, first):
                for h in range(2):
                    if not first:
                        sp.wait_ge(qk_staged, (i - 1) * 16 + (h + 1) * HW)
                    for s in range(2):
                        sp.dma_start(tile(rqk[h][:, s, :]), rows(qkc[s], i, h)).then_inc(qk_landed[h], 16)
                    if not first:
                        sp.wait_ge(v_staged, (i - 1) * 16 + (h + 1) * HW)
                    sp.dma_start(tile(rv[h][:, :]), rows(qkv[2], i, h)).then_inc(v_landed[h], 16)
                    if not first:
                        sp.wait_ge(x1_made, (i - 1) * 16 + ((h + 1) * HW + 2))
                    sp.dma_start(tile(rcx[h][:, 0, :]), rows(qkc[2], i, h)).then_inc(cx_landed[h], 16)
                    sp.dma_start(tile(rcx[h][:, 1, :]), rows(a["x_tok"], i, h)).then_inc(cx_landed[h], 16)
                    if not first:
                        store(i - 1, h)

            image(0, True)
            with sp.Fori(1, IMAGES) as i:
                image(i, False)
            for h in range(2):
                store(IMAGES - 1, h)
            for h in range(2):
                sp.wait_ge(x1_stored[h], 16 * (IMAGES + 1))
                sp.wait_ge(st_stored[h], 16 * (IMAGES + 1))

        @block.gpsimd
        def _(pool):
            for p in range(2):
                pool.memset(qk[p][:, :, :, :], 0.0).then_inc(cleared, 1)
                pool.memset(vs[p][:, :, :, :], 1.0).then_inc(cleared, 1)
                pool.sem_inc(x1_stored[p], 16)
                pool.sem_inc(st_stored[p], 16)
            pool.sem_inc(x1_made, 2)
            pool.wait_ge(cleared, 4)

            def stage_qk(i, w):
                h, p = w // HW, w % 2
                if w % HW == 0:
                    pool.wait_ge(qk_landed[h], i * 32 + 32)
                if not (isinstance(i, int) and i * 16 + w < 2):
                    pool.wait_ge(turned, i * 16 + (w - 1))
                pool.sem_inc(passed, 1)
                for s in range(2):
                    dst = qk[p][:, s, :, :].rearrange("p b (h d) -> p b h d", h=HEADS)[:, :, :, 0:HD]
                    m = pool.tensor_copy(dst, pair(rqk[h][:, s, :], w % HW))
                m.then_inc(qk_staged, 1)

            def stage_v(i, w):
                h, p = w // HW, w % 2
                if w % HW == 0:
                    pool.wait_ge(v_landed[h], i * 16 + 16)
                if not (isinstance(i, int) and i * 16 + w < 2):
                    pool.wait_ge(pv, i * 64 + (4 * (w - 1) + 2))
                pool.sem_inc(passed, 1)
                pool.tensor_copy(vs[p][:, :, :, 0:HD], pair(rv[h][:, :], w % HW)).then_inc(v_staged, 1)

            def sum_cx(i, w):
                h = w // HW
                if w % HW == 0:
                    pool.wait_ge(cx_landed[h], i * 32 + 32)
                pool.tensor_tensor(pair(rcx[h][:, 0, :], w % HW), pair(rcx[h][:, 0, :], w % HW),
                                   pair(rcx[h][:, 1, :], w % HW), ALU.add).then_inc(cx_summed, 1)

            def finish(i, w):
                h = w // HW
                if w % HW == 0:
                    pool.wait_ge(x1_stored[h], i * 16 + 16)
                    if not (isinstance(i, int) and i == 0):
                        pool.wait_ge(bn_done, i * 2 + (h - 1))
                pool.wait_ge(scaled, i * 16 + (w + 3))
                pool.wait_ge(cx_summed, i * 16 + (w + 1))
                pool.tensor_tensor(pair(x1t[h][:, :], w % HW),
                                   attn[w % 2][:, :].rearrange("p (b h d) -> p b h d", b=2, h=HEADS),
                                   pair(rcx[h][:, 0, :], w % HW), ALU.add).then_inc(x1_made, 1)

            def image(i, first, last):
                for w in range(2 * HW):
                    if w + 2 < 2 * HW:
                        stage_qk(i, w + 2)
                    elif not last:
                        stage_qk(i + 1, w + 2 - 2 * HW)
                    if w + 1 < 2 * HW:
                        stage_v(i, w + 1)
                        sum_cx(i, w + 1)
                    elif not last:
                        stage_v(i + 1, 0)
                        sum_cx(i + 1, 0)
                    if w:
                        finish(i, w - 1)
                    elif not first:
                        finish(i - 1, 2 * HW - 1)

            stage_qk(0, 0)
            stage_qk(0, 1)
            stage_v(0, 0)
            sum_cx(0, 0)
            image(0, True, False)
            with pool.Fori(1, IMAGES - 1) as i:
                image(i, False, False)
            image(IMAGES - 1, False, True)
            finish(IMAGES - 1, 2 * HW - 1)

        @block.tensor
        def _(pe):
            def turn(n, p):
                pe.wait_ge(qk_staged, n + 1)
                if not (isinstance(n, int) and n == 0):
                    pe.wait_ge(turned_lo, n * 2)
                for s in range(2):
                    for two in range(2):
                        for b in range(2):
                            m = pe.transpose(ps_t[:, s, two * TOKENS + b * P:two * TOKENS + (b + 1) * P],
                                             qk[p][:, s, b, two * P:(two + 1) * P], ident[:, :])
                m.then_inc(turned, 1)

            def score(n, h, p):
                if h == 0:
                    pe.wait_ge(turned_lo, n * 2 + 2)
                if not (isinstance(n, int) and n * 4 + h < 2):
                    pe.wait_ge(expd, n * 8 + 2 * (h - 1))
                rows = slice(HP * (h % 2), HP * (h % 2) + HD)
                for b in range(2):
                    q = lambda t: t[p][rows, 0, h // 2, b * P:(b + 1) * P]
                    k = lambda t: t[p][rows, 1, h // 2, :]
                    m = matmul3(pe, ps_s[:, h % 2, b * TOKENS:(b + 1) * TOKENS], q(qkh), q(qkl), k(qkh), k(qkl),
                                start=True, stop=True)
                m.then_inc(scores, 1)

            def turn_probs(n, h):
                pe.wait_ge(expd, n * 8 + 2 * (h + 1))
                pe.wait_ge(probs_sb[h % 2], n * 2 + (h // 2 + 1))
                for kb in range(2):
                    for b in range(2):
                        m = pe.transpose(ps_p[:, h % 2, kb * TOKENS + b * P:kb * TOKENS + (b + 1) * P],
                                         prob[:, h, b, kb * P:(kb + 1) * P], ident[:, :])
                m.then_inc(probs_turned, 1)

            def weigh(n, h, p):
                if h == 0:
                    pe.wait_ge(v_staged, n + 1)
                    pe.wait_ge(scaled, n + 1)
                pe.wait_ge(probs_sb[h % 2], n * 2 + (h // 2 + 2))
                for b in range(2):
                    for kb in range(2):
                        m = pe.matmul(ps_o[:, p, (b * HEADS + h) * HP:(b * HEADS + h) * HP + HD + 1],
                                      probT[h % 2][:, kb, b * P:(b + 1) * P], vs[p][:, kb, h, 0:HD + 1],
                                      start=kb == 0, stop=kb == 1)
                m.then_inc(pv, 1)

            def window(n, p, first, ahead):
                for h in range(HEADS):
                    if h < 2:
                        score(n, h + 2, p)
                    elif ahead >= 1:
                        score(n + 1, h - 2, 1 - p)
                    if h == 2 and ahead >= 2:
                        turn(n + 2, p)
                    turn_probs(n, h)
                    if h:
                        weigh(n, h - 1, p)
                    elif not first:
                        weigh(n - 1, HEADS - 1, 1 - p)

            pe.wait_ge(id_landed, 16)
            pe.sem_inc(probs_turned, 4)
            pe.sem_inc(pv, 2)
            turn(0, 0)
            turn(1, 1)
            score(0, 0, 0)
            score(0, 1, 0)
            window(0, 0, True, 2)
            window(1, 1, False, 2)
            with pe.Fori(1, (WINDOWS - 2) // 2) as m:
                n = m * 2
                window(n, 0, False, 2)
                window(n + 1, 1, False, 2)
            window(WINDOWS - 2, 0, False, 1)
            window(WINDOWS - 1, 1, False, 0)
            weigh(WINDOWS - 1, HEADS - 1, 1)

        @block.scalar
        def _(act):
            def upper(n, p):
                act.wait_ge(turned, n + 1)
                for s, scale in enumerate((SCALE, 1.0)):
                    act.activation(qkh[p][:, s, :, :].rearrange("p a t -> p (a t)"), ps_t[:, s, :], ACT.Copy,
                                   scale=scale).then_inc(turned_hi, 1)

            def take_probs(n, h):
                act.wait_ge(probs_turned, n * 4 + (h + 5))
                act.wait_ge(pv, n * 4 + (h + 1))
                act.activation(probT[1][:, :, :].rearrange("p a t -> p (a t)"), ps_p[:, 1, :], ACT.Copy).then_inc(probs_sb[1], 1)

            def exps(n, h):
                act.wait_ge(maxed, n * 4 + (h + 1))
                act.wait_ge(probs_turned, n * 4 + (h + 1))
                for b in range(2):
                    act.activation(prob[:, h, b, :], ps_s[:, h % 2, b * TOKENS:(b + 1) * TOKENS], ACT.Exp,
                                   bias=nmax[:, h, b:b + 1]).then_inc(expd, 1)

            def window(n, p, ahead):
                for h in range(HEADS):
                    if h < 2:
                        exps(n, h + 2)
                    elif ahead >= 1:
                        exps(n + 1, h - 2)
                    if h == 2 and ahead >= 2:
                        upper(n + 2, p)
                    if h % 2:
                        take_probs(n, h)

            upper(0, 0)
            upper(1, 1)
            exps(0, 0)
            exps(0, 1)
            with act.Fori(0, (WINDOWS - 2) // 2) as m:
                n = m * 2
                window(n, 0, 2)
                window(n + 1, 1, 2)
            window(WINDOWS - 2, 0, 1)
            window(WINDOWS - 1, 1, 0)

        @block.vector
        def _(dve):
            def rowmax(n, h):
                dve.wait_ge(scores, n * 4 + (h + 1))
                dve.tensor_reduce(nmax[:, h, :], ps_s[:, h % 2, :].rearrange("p (b t) -> p b t", b=2), AX.X,
                                  ALU.max, negate=True).then_inc(maxed, 1)

            def lower(n, p):
                for s, scale in enumerate((SCALE, 1.0)):
                    dve.wait_ge(turned_hi, n * 2 + (s + 1))
                    dve.scalar_tensor_tensor(qkl[p][:, s, :, :].rearrange("p a t -> p (a t)"), ps_t[:, s, :], scale,
                                             qkh[p][:, s, :, :].bitcast(F32).rearrange("p a t -> p (a t)"),
                                             ALU.mult, ALU.subtract).then_inc(turned_lo, 1)

            def take_probs(n, h):
                dve.wait_ge(probs_turned, n * 4 + (h + 5))
                dve.wait_ge(pv, n * 4 + (h + 1))
                dve.tensor_copy(probT[0][:, :, :].rearrange("p a t -> p (a t)"), ps_p[:, 0, :]).then_inc(probs_sb[0], 1)

            def scale(n, p):
                dve.wait_ge(pv, n * 4 + 6)
                flat = ps_o[:, p, :]
                dve.reciprocal(rden[p][:, :], view(flat, HD, [[HP, 2 * HEADS]])).then_inc(inverted, 1)
                dve.wait_ge(inverted, n + 1)
                dve.wait_ge(x1_made, n + 1)
                dve.tensor_tensor(attn[p][:, :].rearrange("p (a d) -> p a d", d=HD),
                                  view(flat, 0, [[HP, 2 * HEADS], [1, HD]]),
                                  view(rden[p][:, :], 0, [[1, 2 * HEADS], [0, HD]]), ALU.mult).then_inc(scaled, 1)

            def statistics(i, h, k):
                if k == 0:
                    dve.wait_ge(x1_made, i * 16 + ((h + 1) * HW + 2))
                    dve.wait_ge(st_stored[h], i * 16 + 16)
                for g in range(k * NORM_GROUPS // PARTS, (k + 1) * NORM_GROUPS // PARTS):
                    m = dve.bn_stats(st[h][:, g * 6:g * 6 + 6], x1t[h][:, g * PER_NORM * WH:(g + 1) * PER_NORM * WH])
                if k == PARTS - 1:
                    m.then_inc(bn_done, 1)

            def image(i, first, last):
                for w in range(2 * HW):
                    n, p = i * 16 + w, w % 2
                    end = last and w + 1 == 2 * HW
                    for h in range(HEADS):
                        if h < 2:
                            rowmax(n, h + 2)
                        elif not end:
                            rowmax(n + 1, h - 2)
                        if h % 2 == 0:
                            take_probs(n, h)
                        if h == 1 and not (first and w == 0):
                            scale(n - 1, 1 - p)
                        if h == 2 and not (last and w + 2 >= 2 * HW):
                            lower(n + 2, p)
                    if w > HW:
                        statistics(i, 0, w - HW - 1)
                    elif 0 < w < HW and not first:
                        statistics(i - 1, 1, w - 1)

            dve.sem_inc(probs_sb[0], 1)
            dve.sem_inc(probs_sb[1], 1)
            dve.sem_inc(scaled, 2)
            lower(0, 0)
            lower(1, 1)
            rowmax(0, 0)
            rowmax(0, 1)
            image(0, True, False)
            with dve.Fori(1, IMAGES - 1) as i:
                image(i, False, False)
            image(IMAGES - 1, False, True)
            scale(WINDOWS - 1, 1)
            for k in range(PARTS):
                statistics(IMAGES - 1, 1, k)


def stats1_phase(nc, a, stats, norm):
    G = NORM_GROUPS
    BG = IMAGES * G
    with ExitStack() as ctx:
        sb = lambda n, s, d=F32: ctx.enter_context(nc.sbuf_tensor(n, s, d))
        sem = lambda n: ctx.enter_context(nc.semaphore(n))
        st = sb("d_st", [P, HALVES * G * 6])
        ones = sb("d_ones", [P, P])
        pairs = sb("d_pairs", [P, HALVES, G])
        sums = sb("d_sums", [P, IMAGES, G])
        mean = sb("d_mean", [P, IMAGES, G])
        dev = sb("d_dev", [P, IMAGES, G])
        var = sb("d_var", [P, IMAGES, G])
        rstd = sb("d_rstd", [P, IMAGES, G])
        rows = sb("d_rows", [1, G, PER_NORM, 2, IMAGES])
        ps = ctx.enter_context(nc.psum_tensor("d_ps", [P, 4, 512], F32))
        loaded, oned, steps, summed, rooted, stored = (
            sem(n) for n in ("d_loaded", "d_oned", "d_steps", "d_summed", "d_rooted", "d_stored"))
        block = ctx.enter_context(nc.Block())
        flat = lambda t: t[:, :, :].rearrange("p b g -> p (b g)")

        STEP_DEV = 3 + 4 * 4
        STEP_VAR = STEP_DEV + 1

        @block.sync
        def _(sp):
            sp.dma_start(st[:, :], stats.rearrange("p b h n -> p (b h n)")).then_inc(loaded, 16)
            sp.wait_ge(steps, STEP_VAR + 7)
            sp.dma_start(norm.rearrange("(o c) k b -> o (c k b)", o=1),
                         rows[:, :, :, :, :].rearrange("o g c k b -> o (g c k b)")).then_inc(stored, 16)
            sp.wait_ge(stored, 16)

        @block.gpsimd
        def _(pool):
            pool.memset(ones[:, :], 1.0).then_inc(oned, 1)

        @block.tensor
        def _(pe):
            pe.wait_ge(oned, 1)
            for n, (src, after) in enumerate(((sums, 2), (var, STEP_DEV))):
                pe.wait_ge(steps, after)
                for c in range(2):
                    m = pe.matmul(ps[:, 2 * n + c, :], ones[:, :], flat(src)[:, c * 512:(c + 1) * 512],
                                  start=True, stop=True)
                m.then_inc(summed, 1)

        @block.scalar
        def _(act):
            act.wait_ge(steps, STEP_VAR)
            act.activation(flat(dev), flat(var), ACT.Sqrt).then_inc(rooted, 1)

        @block.vector
        def _(dve):
            done = [0]

            def step(ins):
                done[0] += 1
                ins.then_inc(steps, 1)
                dve.wait_ge(steps, done[0])

            def part(o, h):
                return view(st[:, :], h * G * 6 + o, [[2 * G * 6, IMAGES], [6, G]])

            dve.wait_ge(loaded, 16)
            step(dve.tensor_tensor(pairs[:, :, :], view(st[:, :], 1, [[G * 6, HALVES], [6, G]]),
                                   view(st[:, :], 4, [[G * 6, HALVES], [6, G]]), ALU.add))
            step(dve.tensor_tensor(sums[:, :, :], view(flat(pairs), 0, [[2 * G, IMAGES], [1, G]]),
                                   view(flat(pairs), G, [[2 * G, IMAGES], [1, G]]), ALU.add))
            dve.wait_ge(summed, 1)
            step(dve.tensor_scalar(flat(mean), ps[:, 0:2, :].rearrange("p a n -> p (a n)"),
                                   1.0 / (4 * P), None, ALU.mult))
            each = float(PER_NORM * WH // 2)
            n = 0
            for h in range(2):
                for e in range(2):
                    step(dve.tensor_tensor(dev[:, :, :], part(3 * e + 1, h), mean[:, :, :], ALU.subtract))
                    step(dve.tensor_tensor(dev[:, :, :], dev[:, :, :], dev[:, :, :], ALU.mult))
                    dst = var if n == 0 else dev
                    step(dve.scalar_tensor_tensor(dst[:, :, :], dev[:, :, :], each, part(3 * e + 2, h), ALU.mult, ALU.add))
                    step(dve.tensor_tensor(var[:, :, :], var[:, :, :], dev[:, :, :], ALU.add) if n else
                         dve.tensor_scalar(var[:, :, :], var[:, :, :], 0.0, None, ALU.max))
                    n += 1
            dve.wait_ge(summed, 2)
            step(dve.tensor_scalar(flat(var), ps[:, 2:4, :].rearrange("p a n -> p (a n)"),
                                   1.0 / NORM_COUNT, EPS, ALU.mult, ALU.add))
            dve.wait_ge(rooted, 1)
            step(dve.reciprocal(flat(rstd), flat(dev)))
            newton(dve, step, flat(rstd), flat(var), flat(dev))
            step(dve.tensor_tensor(flat(mean), flat(mean), flat(rstd), ALU.mult))
            for c in range(PER_NORM):
                dve.tensor_copy(rows[:, :, c, 0, :], rstd[0:1, :, :].rearrange("p b g -> p g b"))
                m = dve.tensor_copy(rows[:, :, c, 1, :], mean[0:1, :, :].rearrange("p b g -> p g b"))
            step(m)
            assert done[0] == STEP_VAR + 7


def long_phase(nc, a, x1, norm, kpad, out):
    TILE = IMAGES * 2 * C8 * WH
    N = IMAGES * WP
    TL = HEIGHT * U55
    STEPS = 2 * C8
    with ExitStack() as ctx:
        sb = lambda n, s, d=F32: ctx.enter_context(nc.sbuf_tensor(n, s, d))
        sem = lambda n: ctx.enter_context(nc.semaphore(n))
        raw = [sb(f"e_raw{i}", [P, TILE]) for i in range(2)]
        nrm = [sb(f"e_norm{i}", [P, C8, 2, IMAGES]) for i in range(2)]
        t = [sb(f"e_t{i}", [P, TL]) for i in range(2)]
        th = [sb(f"e_th{i}", [P, TL], F32R) for i in range(2)]
        tl = [sb(f"e_tl{i}", [P, TL], F32R) for i in range(2)]
        xn = sb("e_xn", [P, N])
        xh = [sb(f"e_xh{i}", [P, N], F32R) for i in range(2)]
        xl = [sb(f"e_xl{i}", [P, N], F32R) for i in range(2)]
        res = [sb(f"e_res{i}", [P, N]) for i in range(2)]
        ps = ctx.enter_context(nc.psum_tensor("e_ps", [P, 2, 2, 512], F32))
        landed = [sem(f"e_landed{i}") for i in range(2)]
        t_landed = [sem(f"e_t_landed{i}") for i in range(2)]
        stored = [sem(f"e_stored{i}") for i in range(2)]
        t_free, normed, hi, lo, parts_free, prod, done = (
            sem(n) for n in ("e_t_free", "e_normed", "e_hi", "e_lo", "e_parts_free", "e_prod", "e_done"))
        block = ctx.enter_context(nc.Block())

        def channel(i, c):
            return view(raw[i][:, :], c * WH, [[C8 * WH, 2], [1, WH], [2 * C8 * WH, IMAGES]])

        def in_order(ap):
            return ap.rearrange("p (a w b) -> p a w b", a=2, w=WH)

        def reversed_t(p):
            return view(t[p][:, :], TL - 1, [[-1, U55], [-U55, HEIGHT]])

        @block.sync
        def _(sp):
            for i in range(2):
                sp.sem_inc(stored[i], 16)

            def load(g, i, first=False):
                if not first:
                    sp.wait_ge(done, g * (2 * C8) + (4 - 4 * C8 + 2 * C8))
                src = x1[bass.ds(g, 1), :, :, :, :].rearrange("o p b h n -> (o p) (b h n)")
                sp.dma_start(raw[i][:, :], src).then_inc(landed[i], 16)
                src = norm[bass.ds(g * C8, C8), :, :].rearrange("c k b -> (c k b)")
                sp.dma_start(nrm[i][:, :, :, :].rearrange("p c k b -> p (c k b)"), src.partition_broadcast(P)).then_inc(landed[i], 16)

            def store(g):
                with sp.Fori(0, C8 // 2) as m:
                    c = m * 2
                    for p in range(2):
                        sp.wait_ge(done, g * (2 * C8) + c * 2 + (2 * p + 6))
                        dst = out[bass.ds(g * C8 + c + p, 1), :, :].rearrange("o p n -> (o p) n")
                        sp.dma_start(dst, res[p][:, :]).then_inc(stored[p], 16)

            load(0, 0, True)
            load(1, 1, True)
            with sp.Fori(0, (CG - 2) // 2) as m:
                g = m * 2
                store(g)
                load(g + 2, 0)
                store(g + 1)
                load(g + 3, 1)
            store(CG - 2)
            store(CG - 1)
            for p in range(2):
                sp.wait_ge(stored[p], 16 * (CHANNELS // 2 + 1))

        @block.gpsimd
        def _(pool):
            pool.sem_inc(t_free, 2)
            with pool.Fori(0, CHANNELS // 2) as m:
                c = m * 2
                for p in range(2):
                    pool.wait_ge(t_free, c + (p + 1))
                    row = kpad[bass.ds(c + p, 1), :]
                    src = bass.AP(tensor=row.tensor, offset=row.offset, ap=[[1, PW], [U55, HEIGHT], [1, TL]])
                    pool.dma_start(t[p][:, :], src).then_inc(t_landed[p], 16)

        @block.scalar
        def _(act):
            def split(gg, j):
                p = j % 2
                act.wait_ge(parts_free, gg * STEPS + (j + 1))
                act.wait_ge(t_landed[p], gg * (16 * C8) + 16 * (j // 2 + 1))
                act.activation(th[p][:, :].rearrange("p (u h) -> p u h", u=U55), reversed_t(p), ACT.Copy).then_inc(hi, 1)
                act.wait_ge(normed, gg * (2 * STEPS) + 2 * (j + 1))
                act.activation(xh[p][:, :], xn[:, :], ACT.Copy).then_inc(hi, 1)

            with act.Fori(0, CG // 2) as gg:
                for j in range(STEPS):
                    split(gg, j)

        @block.vector
        def _(dve):
            dve.sem_inc(done, 4)

            def split(gg, j):
                i, c, p = j // C8, j % C8, j % 2
                n = gg * (2 * STEPS) + 2 * j
                if c == 0:
                    dve.wait_ge(landed[i], gg * 32 + 32)
                wide = lambda k: view(nrm[i][:, c, k, :], 0, [[0, 2], [0, WH], [1, IMAGES]])
                dve.tensor_tensor(in_order(xn[:, :]), channel(i, c), wide(0), ALU.mult).then_inc(normed, 1)
                dve.wait_ge(normed, n + 1)
                dve.tensor_tensor(in_order(xn[:, :]), in_order(xn[:, :]), wide(1), ALU.subtract).then_inc(normed, 1)
                dve.wait_ge(hi, n + 1)
                dve.tensor_tensor(tl[p][:, :].rearrange("p (u h) -> p u h", u=U55), reversed_t(p),
                                  th[p][:, :].bitcast(F32).rearrange("p (u h) -> p u h", u=U55), ALU.subtract).then_inc(lo, 1)
                dve.wait_ge(hi, n + 2)
                dve.tensor_tensor(xl[p][:, :], xn[:, :], xh[p][:, :].bitcast(F32), ALU.subtract).then_inc(lo, 1)
                dve.wait_ge(lo, n + 2)
                dve.sem_inc(t_free, 1)

            def take(gg, j):
                i, c, p = j // C8, j % C8, j % 2
                dve.wait_ge(prod, gg * STEPS + (j + 1))
                dve.wait_ge(stored[p], gg * (16 * C8) + 16 * (j // 2 + 1))
                for h in range(2):
                    part = slice(h * 512, (h + 1) * 512)
                    dve.tensor_tensor(res[p][:, part].rearrange("p (w b) -> p w b", w=WH),
                                      ps[:, p, h, :].rearrange("p (w b) -> p w b", w=WH),
                                      view(raw[i][:, :], (h * C8 + c) * WH, [[1, WH], [2 * C8 * WH, IMAGES]]),
                                      ALU.add).then_inc(done, 1)

            def groups(gg, first):
                for j in range(STEPS):
                    split(gg, j)
                    if j:
                        take(gg, j - 1)
                    elif not first:
                        take(gg - 1, STEPS - 1)

            groups(0, True)
            with dve.Fori(1, CG // 2) as gg:
                groups(gg, False)
            take(CG // 2 - 1, STEPS - 1)

        @block.tensor
        def _(pe):
            pe.sem_inc(parts_free, 2)
            order = sorted(range(-FAR55, FAR55 + 1), key=abs)
            with pe.Fori(0, CHANNELS // 2) as m:
                n = m * 2
                for p in range(2):
                    pe.wait_ge(lo, n * 2 + 2 * (p + 1))
                    pe.wait_ge(done, n * 2 + 2 * (p + 1))
                    for d in order:
                        wt = slice((2 * d + 2 * FAR55) * HEIGHT, (2 * d + 2 * FAR55 + 2) * HEIGHT)
                        for h in range(2):
                            w0, w1 = max(d, h * WH), min(WP + d, (h + 1) * WH)
                            o = ps[:, p, h, (w0 - h * WH) * IMAGES:(w1 - h * WH) * IMAGES]
                            src = slice((w0 - d) * IMAGES, (w1 - d) * IMAGES)
                            m = matmul3(pe, o, th[p][:, wt], tl[p][:, wt], xh[p][:, src], xl[p][:, src],
                                        start=d == 0, stop=d == order[-1])
                    m.then_inc(prod, 1)
                    pe.wait_ge(prod, n + (p + 1))
                    pe.sem_inc(parts_free, 1)


def program(nc, a, out, scratch):
    kpad = scratch("kpad", [CHANNELS, LEN55])
    qkv = [scratch(n, [CG, P, IMAGES, 2, C8 * WH]) for n in ("q", "k", "v")]
    qkc = [scratch(n, [CG, P, IMAGES, 2, C8 * WH]) for n in ("q_conv", "k_conv", "cape")]
    x1 = scratch("x1", [CG, P, IMAGES, 2, C8 * WH])
    stats = scratch("stats", [P, IMAGES, 2, NORM_GROUPS * 6])
    norm = scratch("norm", [CHANNELS, 2, IMAGES])
    filter_phase(nc, a, kpad)
    with nc.sbuf_tensor("rstd0", [KP, IMAGES * KC], F32) as rstd, \
            nc.sbuf_tensor("shift0", [KP, IMAGES * KC], F32) as shift:
        stats0_phase(nc, a, rstd, shift)
        project_phase(nc, a, rstd, shift, qkv)
    depthwise_phase(nc, a, qkv, qkc)
    attention_phase(nc, a, qkv, qkc, x1, stats)
    stats1_phase(nc, a, stats, norm)
    long_phase(nc, a, x1, norm, kpad, out)


def kernel(**inputs):
    import numpy as np
    import concourse.bacc as bacc
    from concourse.bass_utils import run_bass_kernel_spmd

    f = {k: np.asarray(v) for k, v in inputs.items()}
    x = f["x"]
    split = x.reshape(IMAGES, CHANNELS, HEIGHT, 2, WH, PW)
    w = np.concatenate([f["L0_conv_w_qk"].reshape(2 * CHANNELS, CHANNELS), f["L0_conv_w_v"].reshape(CHANNELS, CHANNELS)])
    w_qkv = np.zeros((KP + 1, KC, QKV), np.float32)
    w_qkv[:KP] = w.T.reshape(KC, KP, QKV).transpose(1, 0, 2)
    w_qkv[KP, KC - 1] = np.concatenate([f["L0_conv_b_qk"], f["L0_conv_b_v"]])
    w5 = np.zeros((3, CHANNELS, LEN5), np.float32)
    rows = w5[:, :, :(2 * HEIGHT - 1) * U5].reshape(3, CHANNELS, 2 * HEIGHT - 1, U5)
    for s, name in enumerate(("q5", "k5", "cape")):
        r0 = HEIGHT - 1 - PAD5
        rows[s, :, r0:r0 + K5, 1:1 + K5] = f["L0_conv_w_" + name].reshape(CHANNELS, K5, K5)
    chan = np.stack([f["L1_conv_" + n].reshape(KC, KP).T for n in ("deltas", "shift", "bias")], axis=1)
    arrays = {
        "x_ch": split.transpose(0, 1, 3, 4, 5, 2).reshape(IMAGES, CHANNELS, 2, WH * P),
        "x_tok": split.reshape(IMAGES, CG, C8, HEIGHT, 2, WH, PW).transpose(1, 6, 3, 0, 4, 2, 5)
        .reshape(CG, P, IMAGES, 2, C8 * WH),
        "w_qkv": w_qkv,
        "w5": w5,
        "bias5": np.concatenate([f["L0_conv_b_" + n] for n in ("q5", "k5", "cape")]),
        "z": f["L1_conv_z"][0, :, ::-1, ::-1].reshape(EMB, K55 * K55),
        "dist": f["L1_conv_distance_map"][0, 0, ::-1, ::-1].reshape(K55 * K55),
        "w1t": f["L1_conv_W1"].T,
        "w2t": f["L1_conv_W2"].T,
        "w3t": f["L1_conv_W3"].T,
        "hid": np.stack([f["L1_conv_" + n].reshape(HID) for n in ("b1", "f1", "b2", "f2")], axis=1),
        "chan": chan,
        "mask": np.kron(np.eye(KP // PER_NORM), np.ones((PER_NORM, PER_NORM))).astype(np.float32),
        "ident": np.eye(P, dtype=np.float32),
    }
    arrays = {k: np.ascontiguousarray(v) for k, v in arrays.items()}
    nc = bacc.Bacc("TRN2", target_bir_lowering=False, num_devices=1)
    a = {k: nc.dram_tensor(f"in_{k}", v.shape, F32, kind="ExternalInput").ap() for k, v in arrays.items()}
    out = nc.dram_tensor("out", (CHANNELS, P, WP * IMAGES), F32, kind="ExternalOutput").ap()
    program(nc, a, out, lambda name, shape: nc.dram_tensor(name, shape, F32, kind="Internal").ap())
    r = run_bass_kernel_spmd(nc, [{f"in_{k}": v for k, v in arrays.items()}], core_ids=[0])
    y = r.results[0]["out"].reshape(CHANNELS, PW, HEIGHT, WP, IMAGES)
    return np.ascontiguousarray(y.transpose(4, 0, 2, 3, 1).reshape(IMAGES, CHANNELS, HEIGHT, WIDTH))
```

```python
from contextlib import ExitStack

import concourse.bass as bass
from concourse import mybir


F32 = mybir.dt.float32
F32R = mybir.dt.float32r
ALU = mybir.AluOpType
ACT = mybir.ActivationFunctionType
AX = mybir.AxisListType

P = 128
IMAGES, CHANNELS, HEIGHT, WIDTH = 32, 192, 64, 64
PW = 2
WP = WIDTH // PW
WH = WP // 2
HALVES = 2 * IMAGES
C8 = 8
CG = CHANNELS // C8
KC = 2
KP = CHANNELS // KC
QKV = 3 * CHANNELS
NORM_GROUPS = 32
PER_NORM = CHANNELS // NORM_GROUPS
NORM_COUNT = PER_NORM * HEIGHT * WIDTH
EPS = 1e-5
HEADS = 4
HD = CHANNELS // HEADS
HP = 64
TOKENS = 2 * P
WINDOWS = IMAGES * WP // 2
SCALE = HD ** -0.5

K5, PAD5 = 5, 2
K55, PAD55 = 55, 27
HID, EMB = 64, 32


def toeplitz(k, pad):
    far = (pad + 1) // PW
    u = PW * (2 * far + 1)
    return far, u, (2 * HEIGHT - 1) * u + 2


FAR5, U5, LEN5 = toeplitz(K5, PAD5)

FAR55 = (PAD55 + 1) // PW + 1
MID55 = PW * FAR55 + 1
U55 = MID55 + PAD55 + 1
TL55 = (HEIGHT - 1) * U55 + PW * (2 * FAR55 + 1)
LEN55 = 2 * HEIGHT * U55 - U55 + MID55 - PAD55


def view(ap, offset, dims):
    return bass.AP(tensor=ap.tensor, offset=ap.offset + offset, ap=[ap.ap[0], *dims])


def matmul3(pe, out, w_hi, w_lo, x_hi, x_lo, start, stop):
    pe.matmul(out, w_hi, x_hi, start=start, stop=False)
    pe.matmul(out, w_hi, x_lo, start=False, stop=False)
    return pe.matmul(out, w_lo, x_hi, start=False, stop=stop)


def filter_phase(nc, a, kpad):
    inv2pi, magic = 0.15915494309189535, 12582912.0
    c1, c2 = 6.28125, 0.0019353071795864769
    pi = 3.1415925
    n_pix = K55 * K55
    rows = [(r, min(8, K55 - r)) for r in range(0, K55, 8)]
    with ExitStack() as ctx:
        sb = lambda n, s, d=F32: ctx.enter_context(nc.sbuf_tensor(n, s, d))
        sem = lambda n: ctx.enter_context(nc.semaphore(n))
        z = sb("f_z", [EMB, n_pix])
        w1 = sb("f_w1", [EMB, HID])
        w2 = sb("f_w2", [HID, HID])
        w3 = sb("f_w3", [HID, CHANNELS])
        hid = sb("f_hid", [HID, 4])
        chan = sb("f_chan", [KP, 3, KC])
        dist = sb("f_dist", [KP, n_pix])
        slope = sb("f_slope", [KP, KC])
        decay = sb("f_decay", [KP, KC, n_pix])
        arg = sb("f_arg", [HID, n_pix])
        turns = sb("f_turns", [HID, n_pix])
        h1 = sb("f_h1", [HID, n_pix])
        h2 = sb("f_h2", [HID, n_pix])
        padded = sb("f_padded", [KP, KC, LEN55])
        ps = ctx.enter_context(nc.psum_tensor("f_ps", [P, 8, 512], F32))
        loaded, cleared, products, steps, funcs, stored = (
            sem(n) for n in ("f_loaded", "f_cleared", "f_products", "f_steps", "f_funcs", "f_stored"))
        LOADS = 7
        block = ctx.enter_context(nc.Block())

        @block.sync
        def _(sp):
            for dst, src in ((z[:, :], a["z"]), (w1[:, :], a["w1t"]), (w2[:, :], a["w2t"]),
                             (w3[:, :], a["w3t"]), (hid[:, :], a["hid"]), (chan[:, :, :], a["chan"]),
                             (dist[:, :], a["dist"].partition_broadcast(KP))):
                sp.dma_start(dst, src).then_inc(loaded, 16)
            sp.wait_ge(steps, 28)
            for k in range(KC):
                sp.dma_start(kpad[k * KP:(k + 1) * KP, :], padded[:, k, :]).then_inc(stored, 16)
            sp.wait_ge(stored, 16 * KC)

        @block.gpsimd
        def _(pool):
            pool.memset(padded[:, :, :], 0.0).then_inc(cleared, 1)

        @block.tensor
        def _(pe):
            pe.wait_ge(loaded, 16 * LOADS)
            for i, (r, n) in enumerate(rows):
                m = pe.matmul(ps[0:HID, i, 0:n * K55], w1[:, :], z[:, r * K55:(r + n) * K55],
                              start=True, stop=True)
            m.then_inc(products, 1)
            pe.wait_ge(funcs, 3)
            for i, (r, n) in enumerate(rows):
                m = pe.matmul(ps[0:HID, i, 0:n * K55], w2[:, :], h1[:, r * K55:(r + n) * K55],
                              start=True, stop=True)
            m.then_inc(products, 1)
            pe.wait_ge(funcs, 4)
            for k in range(KC):
                if k:
                    pe.wait_ge(steps, 20)
                for i, (r, n) in enumerate(rows):
                    m = pe.matmul(ps[0:KP, i, 0:n * K55], w3[:, k * KP:(k + 1) * KP],
                                  h2[:, r * K55:(r + n) * K55], start=True, stop=True)
                m.then_inc(products, 1)

        @block.scalar
        def _(act):
            act.wait_ge(steps, 1)
            for k in range(KC):
                act.activation(decay[:, k, :], dist[:, :], ACT.Exp, scale=slope[:, k:k + 1]).then_inc(funcs, 1)
            act.wait_ge(steps, 7)
            act.activation(h1[:, :], turns[:, :], ACT.Sin).then_inc(funcs, 1)
            act.wait_ge(steps, 13)
            act.activation(h2[:, :], turns[:, :], ACT.Sin).then_inc(funcs, 1)

        @block.vector
        def _(dve):
            done = [0]

            def step(ins):
                done[0] += 1
                ins.then_inc(steps, 1)
                dve.wait_ge(steps, done[0])

            dve.wait_ge(loaded, 16 * LOADS)
            step(dve.scalar_tensor_tensor(slope[:, :], chan[:, 0, :], -1.0, chan[:, 0, :], ALU.mult, ALU.min))
            for layer in range(2):
                dve.wait_ge(products, layer + 1)
                if layer:
                    dve.wait_ge(funcs, 3)
                for i, (r, n) in enumerate(rows):
                    m = dve.tensor_scalar(arg[:, r * K55:(r + n) * K55], ps[0:HID, i, 0:n * K55],
                                          hid[:, 2 * layer:2 * layer + 1], hid[:, 2 * layer + 1:2 * layer + 2],
                                          ALU.add, ALU.mult)
                step(m)
                step(dve.tensor_scalar(turns[:, :], arg[:, :], inv2pi, magic, ALU.mult, ALU.add))
                step(dve.tensor_scalar(turns[:, :], turns[:, :], magic, None, ALU.subtract))
                step(dve.scalar_tensor_tensor(arg[:, :], turns[:, :], -c1, arg[:, :], ALU.mult, ALU.add))
                step(dve.scalar_tensor_tensor(arg[:, :], turns[:, :], -c2, arg[:, :], ALU.mult, ALU.add))
                step(dve.tensor_scalar(turns[:, :], arg[:, :], pi, -pi, ALU.min, ALU.max))
            dve.wait_ge(cleared, 1)
            for k in range(KC):
                dve.wait_ge(products, 3 + k)
                for i, (r, n) in enumerate(rows):
                    dst = view(padded[:, k, :], (HEIGHT - 1 - PAD55 + r) * U55 + MID55 - PAD55, [[U55, n], [1, K55]])
                    step(dve.scalar_tensor_tensor(
                        dst, decay[:, k, r * K55:(r + n) * K55].rearrange("p (a b) -> p a b", b=K55),
                        chan[:, 1, k:k + 1], ps[0:KP, i, 0:n * K55].rearrange("p (a b) -> p a b", b=K55),
                        ALU.add, ALU.mult))
            centre = (HEIGHT - 1) * U55 + MID55
            assert done[0] == 27, done[0]
            for k in range(KC):
                m = dve.tensor_tensor(padded[:, k, centre:centre + 1], padded[:, k, centre:centre + 1],
                                      chan[:, 2, k:k + 1], ALU.add)
            step(m)


def stats0_phase(nc, a, rstd, shift):
    TILES = IMAGES * KC
    FM = 512
    NS = HEIGHT * WIDTH // FM
    SUB = 2 * NS
    with ExitStack() as ctx:
        sb = lambda n, s, d=F32: ctx.enter_context(nc.sbuf_tensor(n, s, d))
        sem = lambda n: ctx.enter_context(nc.semaphore(n))
        xt = sb("s_x", [KP, 4, HEIGHT * WIDTH])
        st = sb("s_stats", [KP, TILES, NS * 6])
        mask = sb("s_mask", [KP, KP])
        mean = sb("s_mean", [KP, TILES])
        dev = sb("s_dev", [KP, TILES, SUB])
        var = sb("s_var", [KP, TILES])
        t = sb("s_t", [KP, TILES])
        ps = ctx.enter_context(nc.psum_tensor("s_ps", [P, 2, 512], F32))
        landed = [sem(f"s_landed{i}") for i in range(4)]
        used, masked, steps, summed, rooted = (sem(n) for n in ("s_used", "s_masked", "s_steps", "s_summed", "s_rooted"))
        block = ctx.enter_context(nc.Block())

        @block.sync
        def _(sp):
            sp.dma_start(mask[:, :], a["mask"]).then_inc(masked, 16)
            sp.sem_inc(used, 4)
            with sp.Fori(0, IMAGES // 2) as m:
                i = m * 2
                for j in range(4):
                    sp.wait_ge(used, i * 2 + (j + 1))
                    src = a["x_ch"][bass.ds(i + j // 2, 1), (j % 2) * KP:(j % 2 + 1) * KP, :, :]
                    sp.dma_start(xt[:, j, :], src.rearrange("o c w n -> (o c) (w n)")).then_inc(landed[j], 16)

        @block.vector
        def _(dve):
            with dve.Fori(0, IMAGES // 2) as m:
                i = m * 2
                for j in range(4):
                    dve.wait_ge(landed[j], i * 8 + 16)
                    for s in range(NS):
                        m = dve.bn_stats(st[:, bass.ds(i * 2 + j, 1), s * 6:s * 6 + 6], xt[:, j, s * FM:(s + 1) * FM])
                    m.then_inc(used, 1)
            dve.wait_ge(used, TILES + 4)
            done = [0]

            def step(ins):
                done[0] += 1
                ins.then_inc(steps, 1)
                dve.wait_ge(steps, done[0])

            flat = st[:, :, :].rearrange("p t s -> p (t s)")
            part = lambda o: view(flat, o, [[NS * 6, TILES], [3, SUB]])
            wide = lambda v: view(v, 0, [[1, TILES], [0, SUB]])
            step(dve.tensor_reduce(t[:, :], part(1), AX.X, ALU.add))
            dve.wait_ge(summed, 1)
            step(dve.tensor_scalar(mean[:, :], ps[0:KP, 0, 0:TILES], 1.0 / (PER_NORM * SUB), None, ALU.mult))
            step(dve.tensor_tensor(dev[:, :, :], part(1), wide(mean[:, :]), ALU.subtract))
            step(dve.tensor_tensor(dev[:, :, :], dev[:, :, :], dev[:, :, :], ALU.mult))
            step(dve.scalar_tensor_tensor(dev[:, :, :], dev[:, :, :], FM / 2.0, part(2), ALU.mult, ALU.add))
            step(dve.tensor_reduce(t[:, :], dev[:, :, :], AX.X, ALU.add))
            dve.wait_ge(summed, 2)
            step(dve.tensor_scalar(var[:, :], ps[0:KP, 1, 0:TILES], 1.0 / NORM_COUNT, EPS, ALU.mult, ALU.add))
            dve.wait_ge(rooted, 1)
            step(dve.reciprocal(rstd[:, :], t[:, :]))
            newton(dve, step, rstd[:, :], var[:, :], t[:, :])
            step(dve.scalar_tensor_tensor(shift[:, :], mean[:, :], -1.0, rstd[:, :], ALU.mult, ALU.mult))

        @block.tensor
        def _(pe):
            pe.wait_ge(masked, 16)
            for n, after in enumerate((1, 6)):
                pe.wait_ge(steps, after)
                pe.matmul(ps[0:KP, n, 0:TILES], mask[:, :], t[:, :], start=True, stop=True).then_inc(summed, 1)

        @block.scalar
        def _(act):
            act.wait_ge(steps, 7)
            act.activation(t[:, :], var[:, :], ACT.Sqrt).then_inc(rooted, 1)


def newton(dve, step, y, v, t):
    step(dve.tensor_tensor(t, y, y, ALU.mult))
    step(dve.tensor_tensor(t, t, v, ALU.mult))
    step(dve.tensor_scalar(t, t, -0.5, 1.5, ALU.mult, ALU.add))
    step(dve.tensor_tensor(y, y, t, ALU.mult))


def project_phase(nc, a, rstd, shift, qkv):
    PX = WH * P
    NC = QKV // 2
    SLOTS = 4
    with ExitStack() as ctx:
        sb = lambda n, s, d=F32: ctx.enter_context(nc.sbuf_tensor(n, s, d))
        sem = lambda n: ctx.enter_context(nc.semaphore(n))
        x = [sb(f"a_x{i}", [KP, KC, PX]) for i in range(2)]
        xh = [sb(f"a_xh{i}", [KP + 1, KC, PX], F32R) for i in range(2)]
        xl = [sb(f"a_xl{i}", [KP, KC, PX], F32R) for i in range(2)]
        w = sb("a_w", [KP + 1, KC, QKV])
        wh = sb("a_wh", [KP + 1, KC, QKV], F32R)
        wl = sb("a_wl", [KP + 1, KC, QKV], F32R)
        tok = [sb(f"a_tok{i}", [P, QKV, WH]) for i in range(2)]
        ps = ctx.enter_context(nc.psum_tensor("a_ps", [P, SLOTS, 2, 512], F32))
        w_landed, w_split, ones = sem("a_w_landed"), sem("a_w_split"), sem("a_ones")
        x_landed = [sem(f"a_x_landed{i}") for i in range(2)]
        x_free, normed, hi, lo, parts_free, prod, prod_free = (
            sem(n) for n in ("a_x_free", "a_normed", "a_hi", "a_lo", "a_parts_free", "a_prod", "a_prod_free"))
        stored = [sem(f"a_stored{i}") for i in range(2)]
        block = ctx.enter_context(nc.Block())

        @block.sync
        def _(sp):
            sp.dma_start(w[:, :, :], a["w_qkv"]).then_inc(w_landed, 16)
            sp.sem_inc(x_free, 2)
            with sp.Fori(0, IMAGES) as i:
                for h in range(2):
                    sp.wait_ge(x_free, i * 2 + (h + 1))
                    src = a["x_ch"][bass.ds(i, 1), :, h, :]
                    sp.dma_start(x[h][:, :, :], src.rearrange("o (k c) n -> c (o k) n", k=KC)).then_inc(x_landed[h], 16)

        @block.gpsimd
        def _(pool):
            for h in range(2):
                pool.memset(xh[h][KP:KP + 1, :, :].bitcast(F32), 1.0).then_inc(ones, 1)

        @block.vector
        def _(dve):
            dve.wait_ge(w_split, 1)
            dve.tensor_tensor(wl[:, :, :], w[:, :, :], wh[:, :, :].bitcast(F32), ALU.subtract).then_inc(w_split, 1)
            with dve.Fori(0, IMAGES) as i:
                for h in range(2):
                    dve.wait_ge(x_landed[h], i * 16 + 16)
                    for k in range(KC):
                        dve.tensor_scalar(x[h][:, k, :], x[h][:, k, :], rstd[:, bass.ds(i * KC + k, 1)],
                                          shift[:, bass.ds(i * KC + k, 1)], ALU.mult, ALU.add).then_inc(normed, 1)
                    dve.wait_ge(hi, i * 2 + (h + 1))
                    dve.wait_ge(parts_free, i * 2 + (h + 1))
                    m = dve.tensor_tensor(xl[h][:, :, :], x[h][:, :, :], xh[h][0:KP, :, :].bitcast(F32), ALU.subtract)
                    m.then_inc(lo, 1)
                    dve.wait_ge(lo, i * 2 + (h + 1))
                    dve.sem_inc(x_free, 1)

        @block.scalar
        def _(act):
            act.wait_ge(w_landed, 16)
            act.activation(wh[:, :, :], w[:, :, :], ACT.Copy).then_inc(w_split, 1)
            act.sem_inc(prod_free, SLOTS)
            for h in range(2):
                act.sem_inc(stored[h], 48)

            def split(i, h):
                act.wait_ge(normed, i * 4 + 2 * (h + 1))
                act.wait_ge(parts_free, i * 2 + (h + 1))
                act.activation(xh[h][0:KP, :, :], x[h][:, :, :], ACT.Copy).then_inc(hi, 1)

            def take(i, h, n0, n1):
                for n in range(n0, n1):
                    act.wait_ge(prod, i * 32 + (h * WH + n + 1))
                    dst = tok[h][:, :, n].rearrange("p (a c) -> p a c", a=2)
                    act.activation(dst, ps[:, n % SLOTS, :, 0:NC], ACT.Copy).then_inc(prod_free, 1)

            def image(i, last):
                for h in range(2):
                    act.wait_ge(stored[h], i * 48 + 48)
                    take(i, h, 0, WH // 2)
                    if h == 0:
                        split(i, 1)
                    elif not last:
                        split(i + 1, 0)
                    take(i, h, WH // 2, WH)
                    act.wait_ge(prod_free, i * 32 + ((h + 1) * WH + SLOTS))
                    for s in range(3):
                        dst = qkv[s][:, :, bass.ds(i, 1), h, :].rearrange("g p o n -> p (g o) n")
                        src = tok[h][:, s * CHANNELS:(s + 1) * CHANNELS, :].rearrange("p (g c) w -> p g (c w)", c=C8)
                        act.dma_start(dst, src).then_inc(stored[h], 16)

            split(0, 0)
            with act.Fori(0, IMAGES - 1) as i:
                image(i, False)
            image(IMAGES - 1, True)
            for h in range(2):
                act.wait_ge(stored[h], 48 * (IMAGES + 1))

        @block.tensor
        def _(pe):
            pe.sem_inc(parts_free, 2)
            pe.wait_ge(w_split, 2)
            pe.wait_ge(ones, 2)
            with pe.Fori(0, IMAGES) as i:
                for h in range(2):
                    pe.wait_ge(hi, i * 2 + (h + 1))
                    pe.wait_ge(lo, i * 2 + (h + 1))
                    for n in range(WH):
                        pe.wait_ge(prod_free, i * 32 + (h * WH + n + 1))
                        px = slice(n * P, (n + 1) * P)
                        for c in range(2):
                            out = ps[:, n % SLOTS, c, 0:NC]
                            oc = slice(c * NC, (c + 1) * NC)
                            for k in range(KC):
                                r = KP + k
                                pe.matmul(out, xh[h][0:r, k, px], wh[0:r, k, oc], start=k == 0, stop=False)
                                pe.matmul(out, xh[h][0:r, k, px], wl[0:r, k, oc], start=False, stop=False)
                                m = pe.matmul(out, xl[h][:, k, px], wh[0:KP, k, oc], start=False, stop=k == 1)
                        m.then_inc(prod, 1)
                        if n == WH - 1:
                            pe.wait_ge(prod, i * 32 + (h + 1) * WH)
                            pe.sem_inc(parts_free, 1)


def depthwise_phase(nc, a, qkv, qkc):
    TILE = IMAGES * 2 * C8 * WH
    N = IMAGES * WP
    STEPS = 3 * C8
    SLOTS = 3
    RING = 8
    with ExitStack() as ctx:
        sb = lambda n, s, d=F32: ctx.enter_context(nc.sbuf_tensor(n, s, d))
        sem = lambda n: ctx.enter_context(nc.semaphore(n))
        raw = {n: sb(f"b_raw_{n}", [P, TILE]) for n in ("v0", "v1", "q", "k")}
        t5 = [sb(f"b_t{i}", [P, HEIGHT * U5]) for i in range(RING)]
        th = [sb(f"b_th{i}", [P, U5 * HEIGHT], F32R) for i in range(SLOTS)]
        tl = [sb(f"b_tl{i}", [P, U5 * HEIGHT], F32R) for i in range(SLOTS)]
        xh = [sb(f"b_xh{i}", [P, N], F32R) for i in range(SLOTS)]
        xl = [sb(f"b_xl{i}", [P, N], F32R) for i in range(SLOTS)]
        bias = sb("b_bias", [P, CG * STEPS])
        ps = ctx.enter_context(nc.psum_tensor("b_ps", [P, SLOTS, 2, 512], F32))
        landed = {n: sem(f"b_landed_{n}") for n in raw}
        stored = {n: sem(f"b_stored_{n}") for n in raw}
        t_landed = [sem(f"b_t_landed{i}") for i in range(RING)]
        passed, b_landed, hi, lo, prod, done = (sem("b_" + n) for n in ("passed", "b_landed", "hi", "lo", "prod", "done"))
        block = ctx.enter_context(nc.Block())

        def channel(tile, c):
            return view(raw[tile][:, :], c * WH, [[C8 * WH, 2], [1, WH], [2 * C8 * WH, IMAGES]])

        def in_order(ap):
            return ap.rearrange("p (a w b) -> p a w b", a=2, w=WH)

        def toeplitz_rows(tile):
            return view(tile[:, :], HEIGHT * U5 - 1, [[-1, U5], [-U5, HEIGHT]])

        def matrices(tile):
            return tile.rearrange("p (u h) -> p u h", u=U5)

        def place(j):
            return (f"v{j // STEPS}", "q", "k")[j % STEPS // C8], j % C8

        @block.sync
        def _(sp):
            sp.dma_start(bias[:, :], a["bias5"].partition_broadcast(P)).then_inc(b_landed, 16)
            scratch_in = {"v0": qkv[2], "v1": qkv[2], "q": qkv[0], "k": qkv[1]}
            scratch_out = {"v0": qkc[2], "v1": qkc[2], "q": qkc[0], "k": qkc[1]}

            def rows(t, g):
                return t[bass.ds(g, 1), :, :, :, :].rearrange("o p b h n -> (o p) (b h n)")

            def load(n, g):
                sp.dma_start(raw[n][:, :], rows(scratch_in[n], g)).then_inc(landed[n], 16)

            def store(n, g, k):
                sp.wait_ge(done, g * (2 * STEPS) + (2 * C8 * (k + 1) + 2 * SLOTS))
                sp.sem_inc(passed, 1)
                sp.dma_start(rows(scratch_out[n], g), raw[n][:, :]).then_inc(stored[n], 16)

            def group(g, i, m, last):
                v = f"v{i}"
                store(v, g, 0)
                store("q", g, 1)
                if not (last and i == 1):
                    sp.wait_ge(stored["q"], m * 32 + (16 * i + 16))
                    sp.sem_inc(passed, 1)
                    load("q", g + 1)
                store("k", g, 2)
                if not last:
                    sp.wait_ge(stored[v], m * 16 + 16)
                    sp.sem_inc(passed, 1)
                    load(v, g + 2)
                if not (last and i == 1):
                    sp.wait_ge(stored["k"], m * 32 + (16 * i + 16))
                    sp.sem_inc(passed, 1)
                    load("k", g + 1)

            load("v0", 0)
            load("q", 0)
            load("k", 0)
            load("v1", 1)
            with sp.Fori(0, CG // 2 - 1) as m:
                group(m * 2, 0, m, False)
                group(m * 2 + 1, 1, m, False)
            group(CG - 2, 0, CG // 2 - 1, True)
            group(CG - 1, 1, CG // 2 - 1, True)
            for n in raw:
                sp.wait_ge(stored[n], 16 * CG if n in "qk" else 8 * CG)

        @block.gpsimd
        def _(pool):
            def load(n, r):
                row = a["w5"][bass.ds(n, 1), :]
                src = bass.AP(tensor=row.tensor, offset=row.offset, ap=[[1, PW], [U5, HEIGHT], [1, HEIGHT * U5]])
                pool.dma_start(t5[r][:, :], src).then_inc(t_landed[r], 16)

            for r in range(RING):
                load(r, r)
            with pool.Fori(1, CG * STEPS // RING) as m:
                for r in range(RING):
                    pool.wait_ge(lo, m * (2 * RING) + (2 * r + 1 - 2 * RING))
                    pool.sem_inc(passed, 1)
                    load(m * RING + r, r)

        @block.scalar
        def _(act):
            with act.Fori(0, CG // 2) as gg:
                for j in range(2 * STEPS):
                    (tile, c), p, r = place(j), j % SLOTS, j % RING
                    if c == 0:
                        each = 16 if tile[0] == "v" else 32
                        act.wait_ge(landed[tile], gg * each + (16 if tile[0] == "v" else 16 * (j // STEPS + 1)))
                    act.wait_ge(prod, gg * (2 * STEPS) + (j + 1))
                    act.wait_ge(t_landed[r], gg * (16 * 2 * STEPS // RING) + 16 * (j // RING + 1))
                    act.activation(matrices(th[p][:, :]), toeplitz_rows(t5[r]), ACT.Copy).then_inc(hi, 1)
                    act.activation(in_order(xh[p][:, :]), channel(tile, c), ACT.Copy).then_inc(hi, 1)

        @block.vector
        def _(dve):
            dve.sem_inc(done, 2 * SLOTS)
            dve.wait_ge(b_landed, 16)

            def lower(gg, j):
                (tile, c), p, r = place(j), j % SLOTS, j % RING
                n = gg * (4 * STEPS) + 2 * j
                dve.wait_ge(hi, n + 1)
                dve.tensor_tensor(matrices(tl[p][:, :]), toeplitz_rows(t5[r]), matrices(th[p][:, :].bitcast(F32)),
                                  ALU.subtract).then_inc(lo, 1)
                dve.wait_ge(hi, n + 2)
                dve.tensor_tensor(in_order(xl[p][:, :]), channel(tile, c), in_order(xh[p][:, :]).bitcast(F32),
                                  ALU.subtract).then_inc(lo, 1)
                dve.wait_ge(lo, n + 2)

            def take(gg, j):
                (tile, c), p = place(j), j % SLOTS
                dve.wait_ge(prod, gg * (2 * STEPS) + (j + SLOTS + 1))
                own = bias[:, bass.ds(gg * (2 * STEPS) + j, 1)]
                if tile[0] != "v":
                    dve.wait_ge(done, gg * (4 * STEPS) + (2 * (j // STEPS * STEPS + c + 1) + 2 * SLOTS))
                for h in range(2):
                    at = lambda t: view(raw[t][:, :], (h * C8 + c) * WH, [[1, WH], [2 * C8 * WH, IMAGES]])
                    src = ps[:, p, h, :].rearrange("p (w b) -> p w b", w=WH)
                    if tile[0] == "v":
                        dve.tensor_scalar(at(tile), src, own, None, ALU.add).then_inc(done, 1)
                    else:
                        dve.scalar_tensor_tensor(at(tile), src, own, at(f"v{j // STEPS}"), ALU.add, ALU.add).then_inc(done, 1)

            def groups(gg, first):
                for j in range(2 * STEPS):
                    lower(gg, j)
                    if j:
                        take(gg, j - 1)
                    elif not first:
                        take(gg - 1, 2 * STEPS - 1)

            groups(0, True)
            with dve.Fori(1, CG // 2) as gg:
                groups(gg, False)
            take(CG // 2 - 1, 2 * STEPS - 1)

        @block.tensor
        def _(pe):
            pe.sem_inc(prod, SLOTS)
            with pe.Fori(0, CG * STEPS // SLOTS) as m:
                n = m * SLOTS
                for p in range(SLOTS):
                    pe.wait_ge(lo, n * 2 + 2 * (p + 1))
                    pe.wait_ge(done, n * 2 + 2 * (p + 1))
                    for d in (0, -1, 1):
                        wt = slice((2 * d + 2 * FAR5) * HEIGHT, (2 * d + 2 * FAR5 + 2) * HEIGHT)
                        for h in range(2):
                            w0, w1 = max(d, h * WH), min(WP + d, (h + 1) * WH)
                            o = ps[:, p, h, (w0 - h * WH) * IMAGES:(w1 - h * WH) * IMAGES]
                            src = slice((w0 - d) * IMAGES, (w1 - d) * IMAGES)
                            last = matmul3(pe, o, th[p][:, wt], tl[p][:, wt], xh[p][:, src], xl[p][:, src],
                                           start=d == 0, stop=d == 1)
                    last.then_inc(prod, 1)


def attention_phase(nc, a, qkv, qkc, x1, stats):
    HALF = CG * C8 * WH
    HW = WH // 2
    PARTS = HW - 1
    with ExitStack() as ctx:
        sb = lambda n, s, d=F32: ctx.enter_context(nc.sbuf_tensor(n, s, d))
        sem = lambda n: ctx.enter_context(nc.semaphore(n))
        rqk = [sb(f"c_rqk{i}", [P, 2, HALF]) for i in range(2)]
        rv = [sb(f"c_rv{i}", [P, HALF]) for i in range(2)]
        rcx = [sb(f"c_rcx{i}", [P, 2, HALF]) for i in range(2)]
        x1t = [sb(f"c_x1t{i}", [P, HALF]) for i in range(2)]
        qk = [sb(f"c_qk{i}", [P, 2, 2, HEADS * HP]) for i in range(2)]
        vs = [sb(f"c_v{i}", [P, 2, HEADS, HP]) for i in range(2)]
        qkh = [sb(f"c_qkh{i}", [P, 2, 2, TOKENS], F32R) for i in range(2)]
        qkl = [sb(f"c_qkl{i}", [P, 2, 2, TOKENS], F32R) for i in range(2)]
        prob = sb("c_prob", [P, 4, 2, TOKENS])
        probT = [sb(f"c_probT{i}", [P, 2, TOKENS]) for i in range(2)]
        nmax = sb("c_nmax", [P, 4, 2])
        rden = [sb(f"c_rden{i}", [P, 2 * HEADS]) for i in range(2)]
        attn = [sb(f"c_attn{i}", [P, 2 * CHANNELS]) for i in range(2)]
        st = [sb(f"c_st{i}", [P, NORM_GROUPS * 6]) for i in range(2)]
        ident = sb("c_ident", [P, P])
        ps_s = ctx.enter_context(nc.psum_tensor("c_ps_s", [P, 2, 512], F32))
        ps_p = ctx.enter_context(nc.psum_tensor("c_ps_p", [P, 2, 512], F32))
        ps_t = ctx.enter_context(nc.psum_tensor("c_ps_t", [P, 2, 512], F32))
        ps_o = ctx.enter_context(nc.psum_tensor("c_ps_o", [P, 2, 512], F32))

        qk_landed = [sem(f"c_qk_landed{i}") for i in range(2)]
        v_landed = [sem(f"c_v_landed{i}") for i in range(2)]
        cx_landed = [sem(f"c_cx_landed{i}") for i in range(2)]
        x1_stored = [sem(f"c_x1_stored{i}") for i in range(2)]
        st_stored = [sem(f"c_st_stored{i}") for i in range(2)]
        passed = sem("c_passed")
        probs_sb = [sem(f"c_probs_sb{i}") for i in range(2)]
        (id_landed, cleared, qk_staged, v_staged, cx_summed, x1_made, turned, turned_hi, turned_lo, scores,
         maxed, expd, probs_turned, pv, inverted, scaled, bn_done) = (sem("c_" + n) for n in (
             "id_landed", "cleared", "qk_staged", "v_staged", "cx_summed", "x1_made", "turned", "turned_hi",
             "turned_lo", "scores", "maxed", "expd", "probs_turned", "pv", "inverted", "scaled", "bn_done"))
        block = ctx.enter_context(nc.Block())

        def pair(t, w):
            return view(t, 2 * w, [[1, 2], [HD * WH, HEADS], [WH, HD]])

        @block.sync
        def _(sp):
            sp.dma_start(ident[:, :], a["ident"]).then_inc(id_landed, 16)

            def rows(t, i, h):
                return t[:, :, bass.ds(i, 1), h, :].rearrange("g p o n -> p (g o) n")

            def tile(t):
                return t.rearrange("p (g n) -> p g n", g=CG)

            def store(i, h):
                sp.wait_ge(x1_made, i * 16 + ((h + 1) * HW + 2))
                sp.dma_start(rows(x1, i, h), tile(x1t[h][:, :])).then_inc(x1_stored[h], 16)
                sp.wait_ge(bn_done, i * 2 + (h + 1))
                sp.dma_start(stats[:, bass.ds(i, 1), h, :].rearrange("p o n -> p (o n)"), st[h][:, :]).then_inc(st_stored[h], 16)

            def image(i, first):
                for h in range(2):
                    if not first:
                        sp.wait_ge(qk_staged, (i - 1) * 16 + (h + 1) * HW)
                    for s in range(2):
                        sp.dma_start(tile(rqk[h][:, s, :]), rows(qkc[s], i, h)).then_inc(qk_landed[h], 16)
                    if not first:
                        sp.wait_ge(v_staged, (i - 1) * 16 + (h + 1) * HW)
                    sp.dma_start(tile(rv[h][:, :]), rows(qkv[2], i, h)).then_inc(v_landed[h], 16)
                    if not first:
                        sp.wait_ge(x1_made, (i - 1) * 16 + ((h + 1) * HW + 2))
                    sp.dma_start(tile(rcx[h][:, 0, :]), rows(qkc[2], i, h)).then_inc(cx_landed[h], 16)
                    sp.dma_start(tile(rcx[h][:, 1, :]), rows(a["x_tok"], i, h)).then_inc(cx_landed[h], 16)
                    if not first:
                        store(i - 1, h)

            image(0, True)
            with sp.Fori(1, IMAGES) as i:
                image(i, False)
            for h in range(2):
                store(IMAGES - 1, h)
            for h in range(2):
                sp.wait_ge(x1_stored[h], 16 * (IMAGES + 1))
                sp.wait_ge(st_stored[h], 16 * (IMAGES + 1))

        @block.gpsimd
        def _(pool):
            for p in range(2):
                pool.memset(qk[p][:, :, :, :], 0.0).then_inc(cleared, 1)
                pool.memset(vs[p][:, :, :, :], 1.0).then_inc(cleared, 1)
                pool.sem_inc(x1_stored[p], 16)
                pool.sem_inc(st_stored[p], 16)
            pool.sem_inc(x1_made, 2)
            pool.wait_ge(cleared, 4)

            def stage_qk(i, w):
                h, p = w // HW, w % 2
                if w % HW == 0:
                    pool.wait_ge(qk_landed[h], i * 32 + 32)
                if not (isinstance(i, int) and i * 16 + w < 2):
                    pool.wait_ge(turned, i * 16 + (w - 1))
                pool.sem_inc(passed, 1)
                for s in range(2):
                    dst = qk[p][:, s, :, :].rearrange("p b (h d) -> p b h d", h=HEADS)[:, :, :, 0:HD]
                    m = pool.tensor_copy(dst, pair(rqk[h][:, s, :], w % HW))
                m.then_inc(qk_staged, 1)

            def stage_v(i, w):
                h, p = w // HW, w % 2
                if w % HW == 0:
                    pool.wait_ge(v_landed[h], i * 16 + 16)
                if not (isinstance(i, int) and i * 16 + w < 2):
                    pool.wait_ge(pv, i * 64 + (4 * (w - 1) + 2))
                pool.sem_inc(passed, 1)
                pool.tensor_copy(vs[p][:, :, :, 0:HD], pair(rv[h][:, :], w % HW)).then_inc(v_staged, 1)

            def sum_cx(i, w):
                h = w // HW
                if w % HW == 0:
                    pool.wait_ge(cx_landed[h], i * 32 + 32)
                pool.tensor_tensor(pair(rcx[h][:, 0, :], w % HW), pair(rcx[h][:, 0, :], w % HW),
                                   pair(rcx[h][:, 1, :], w % HW), ALU.add).then_inc(cx_summed, 1)

            def finish(i, w):
                h = w // HW
                if w % HW == 0:
                    pool.wait_ge(x1_stored[h], i * 16 + 16)
                    if not (isinstance(i, int) and i == 0):
                        pool.wait_ge(bn_done, i * 2 + (h - 1))
                pool.wait_ge(scaled, i * 16 + (w + 3))
                pool.wait_ge(cx_summed, i * 16 + (w + 1))
                pool.tensor_tensor(pair(x1t[h][:, :], w % HW),
                                   attn[w % 2][:, :].rearrange("p (b h d) -> p b h d", b=2, h=HEADS),
                                   pair(rcx[h][:, 0, :], w % HW), ALU.add).then_inc(x1_made, 1)

            def image(i, first, last):
                for w in range(2 * HW):
                    if w + 2 < 2 * HW:
                        stage_qk(i, w + 2)
                    elif not last:
                        stage_qk(i + 1, w + 2 - 2 * HW)
                    if w + 1 < 2 * HW:
                        stage_v(i, w + 1)
                        sum_cx(i, w + 1)
                    elif not last:
                        stage_v(i + 1, 0)
                        sum_cx(i + 1, 0)
                    if w:
                        finish(i, w - 1)
                    elif not first:
                        finish(i - 1, 2 * HW - 1)

            stage_qk(0, 0)
            stage_qk(0, 1)
            stage_v(0, 0)
            sum_cx(0, 0)
            image(0, True, False)
            with pool.Fori(1, IMAGES - 1) as i:
                image(i, False, False)
            image(IMAGES - 1, False, True)
            finish(IMAGES - 1, 2 * HW - 1)

        @block.tensor
        def _(pe):
            def turn(n, p):
                pe.wait_ge(qk_staged, n + 1)
                if not (isinstance(n, int) and n == 0):
                    pe.wait_ge(turned_lo, n * 2)
                for s in range(2):
                    for two in range(2):
                        for b in range(2):
                            m = pe.transpose(ps_t[:, s, two * TOKENS + b * P:two * TOKENS + (b + 1) * P],
                                             qk[p][:, s, b, two * P:(two + 1) * P], ident[:, :])
                m.then_inc(turned, 1)

            def score(n, h, p):
                if h == 0:
                    pe.wait_ge(turned_lo, n * 2 + 2)
                if not (isinstance(n, int) and n * 4 + h < 2):
                    pe.wait_ge(expd, n * 8 + 2 * (h - 1))
                rows = slice(HP * (h % 2), HP * (h % 2) + HD)
                for b in range(2):
                    q = lambda t: t[p][rows, 0, h // 2, b * P:(b + 1) * P]
                    k = lambda t: t[p][rows, 1, h // 2, :]
                    m = matmul3(pe, ps_s[:, h % 2, b * TOKENS:(b + 1) * TOKENS], q(qkh), q(qkl), k(qkh), k(qkl),
                                start=True, stop=True)
                m.then_inc(scores, 1)

            def turn_probs(n, h):
                pe.wait_ge(expd, n * 8 + 2 * (h + 1))
                pe.wait_ge(probs_sb[h % 2], n * 2 + (h // 2 + 1))
                for kb in range(2):
                    for b in range(2):
                        m = pe.transpose(ps_p[:, h % 2, kb * TOKENS + b * P:kb * TOKENS + (b + 1) * P],
                                         prob[:, h, b, kb * P:(kb + 1) * P], ident[:, :])
                m.then_inc(probs_turned, 1)

            def weigh(n, h, p):
                if h == 0:
                    pe.wait_ge(v_staged, n + 1)
                    pe.wait_ge(scaled, n + 1)
                pe.wait_ge(probs_sb[h % 2], n * 2 + (h // 2 + 2))
                for b in range(2):
                    for kb in range(2):
                        m = pe.matmul(ps_o[:, p, (b * HEADS + h) * HP:(b * HEADS + h) * HP + HD + 1],
                                      probT[h % 2][:, kb, b * P:(b + 1) * P], vs[p][:, kb, h, 0:HD + 1],
                                      start=kb == 0, stop=kb == 1)
                m.then_inc(pv, 1)

            def window(n, p, first, ahead):
                for h in range(HEADS):
                    if h < 2:
                        score(n, h + 2, p)
                    elif ahead >= 1:
                        score(n + 1, h - 2, 1 - p)
                    if h == 2 and ahead >= 2:
                        turn(n + 2, p)
                    turn_probs(n, h)
                    if h:
                        weigh(n, h - 1, p)
                    elif not first:
                        weigh(n - 1, HEADS - 1, 1 - p)

            pe.wait_ge(id_landed, 16)
            pe.sem_inc(probs_turned, 4)
            pe.sem_inc(pv, 2)
            turn(0, 0)
            turn(1, 1)
            score(0, 0, 0)
            score(0, 1, 0)
            window(0, 0, True, 2)
            window(1, 1, False, 2)
            with pe.Fori(1, (WINDOWS - 2) // 2) as m:
                n = m * 2
                window(n, 0, False, 2)
                window(n + 1, 1, False, 2)
            window(WINDOWS - 2, 0, False, 1)
            window(WINDOWS - 1, 1, False, 0)
            weigh(WINDOWS - 1, HEADS - 1, 1)

        @block.scalar
        def _(act):
            def upper(n, p):
                act.wait_ge(turned, n + 1)
                for s, scale in enumerate((SCALE, 1.0)):
                    act.activation(qkh[p][:, s, :, :].rearrange("p a t -> p (a t)"), ps_t[:, s, :], ACT.Copy,
                                   scale=scale).then_inc(turned_hi, 1)

            def take_probs(n, h):
                act.wait_ge(probs_turned, n * 4 + (h + 5))
                act.wait_ge(pv, n * 4 + (h + 1))
                act.activation(probT[1][:, :, :].rearrange("p a t -> p (a t)"), ps_p[:, 1, :], ACT.Copy).then_inc(probs_sb[1], 1)

            def exps(n, h):
                act.wait_ge(maxed, n * 4 + (h + 1))
                act.wait_ge(probs_turned, n * 4 + (h + 1))
                for b in range(2):
                    act.activation(prob[:, h, b, :], ps_s[:, h % 2, b * TOKENS:(b + 1) * TOKENS], ACT.Exp,
                                   bias=nmax[:, h, b:b + 1]).then_inc(expd, 1)

            def window(n, p, ahead):
                for h in range(HEADS):
                    if h < 2:
                        exps(n, h + 2)
                    elif ahead >= 1:
                        exps(n + 1, h - 2)
                    if h == 2 and ahead >= 2:
                        upper(n + 2, p)
                    if h % 2:
                        take_probs(n, h)

            upper(0, 0)
            upper(1, 1)
            exps(0, 0)
            exps(0, 1)
            with act.Fori(0, (WINDOWS - 2) // 2) as m:
                n = m * 2
                window(n, 0, 2)
                window(n + 1, 1, 2)
            window(WINDOWS - 2, 0, 1)
            window(WINDOWS - 1, 1, 0)

        @block.vector
        def _(dve):
            def rowmax(n, h):
                dve.wait_ge(scores, n * 4 + (h + 1))
                dve.tensor_reduce(nmax[:, h, :], ps_s[:, h % 2, :].rearrange("p (b t) -> p b t", b=2), AX.X,
                                  ALU.max, negate=True).then_inc(maxed, 1)

            def lower(n, p):
                for s, scale in enumerate((SCALE, 1.0)):
                    dve.wait_ge(turned_hi, n * 2 + (s + 1))
                    dve.scalar_tensor_tensor(qkl[p][:, s, :, :].rearrange("p a t -> p (a t)"), ps_t[:, s, :], scale,
                                             qkh[p][:, s, :, :].bitcast(F32).rearrange("p a t -> p (a t)"),
                                             ALU.mult, ALU.subtract).then_inc(turned_lo, 1)

            def take_probs(n, h):
                dve.wait_ge(probs_turned, n * 4 + (h + 5))
                dve.wait_ge(pv, n * 4 + (h + 1))
                dve.tensor_copy(probT[0][:, :, :].rearrange("p a t -> p (a t)"), ps_p[:, 0, :]).then_inc(probs_sb[0], 1)

            def scale(n, p):
                dve.wait_ge(pv, n * 4 + 6)
                flat = ps_o[:, p, :]
                dve.reciprocal(rden[p][:, :], view(flat, HD, [[HP, 2 * HEADS]])).then_inc(inverted, 1)
                dve.wait_ge(inverted, n + 1)
                dve.wait_ge(x1_made, n + 1)
                dve.tensor_tensor(attn[p][:, :].rearrange("p (a d) -> p a d", d=HD),
                                  view(flat, 0, [[HP, 2 * HEADS], [1, HD]]),
                                  view(rden[p][:, :], 0, [[1, 2 * HEADS], [0, HD]]), ALU.mult).then_inc(scaled, 1)

            def statistics(i, h, k):
                if k == 0:
                    dve.wait_ge(x1_made, i * 16 + ((h + 1) * HW + 2))
                    dve.wait_ge(st_stored[h], i * 16 + 16)
                for g in range(k * NORM_GROUPS // PARTS, (k + 1) * NORM_GROUPS // PARTS):
                    m = dve.bn_stats(st[h][:, g * 6:g * 6 + 6], x1t[h][:, g * PER_NORM * WH:(g + 1) * PER_NORM * WH])
                if k == PARTS - 1:
                    m.then_inc(bn_done, 1)

            def image(i, first, last):
                for w in range(2 * HW):
                    n, p = i * 16 + w, w % 2
                    end = last and w + 1 == 2 * HW
                    for h in range(HEADS):
                        if h < 2:
                            rowmax(n, h + 2)
                        elif not end:
                            rowmax(n + 1, h - 2)
                        if h % 2 == 0:
                            take_probs(n, h)
                        if h == 1 and not (first and w == 0):
                            scale(n - 1, 1 - p)
                        if h == 2 and not (last and w + 2 >= 2 * HW):
                            lower(n + 2, p)
                    if w > HW:
                        statistics(i, 0, w - HW - 1)
                    elif 0 < w < HW and not first:
                        statistics(i - 1, 1, w - 1)

            dve.sem_inc(probs_sb[0], 1)
            dve.sem_inc(probs_sb[1], 1)
            dve.sem_inc(scaled, 2)
            lower(0, 0)
            lower(1, 1)
            rowmax(0, 0)
            rowmax(0, 1)
            image(0, True, False)
            with dve.Fori(1, IMAGES - 1) as i:
                image(i, False, False)
            image(IMAGES - 1, False, True)
            scale(WINDOWS - 1, 1)
            for k in range(PARTS):
                statistics(IMAGES - 1, 1, k)


def stats1_phase(nc, a, stats, norm):
    G = NORM_GROUPS
    BG = IMAGES * G
    with ExitStack() as ctx:
        sb = lambda n, s, d=F32: ctx.enter_context(nc.sbuf_tensor(n, s, d))
        sem = lambda n: ctx.enter_context(nc.semaphore(n))
        st = sb("d_st", [P, HALVES * G * 6])
        ones = sb("d_ones", [P, P])
        pairs = sb("d_pairs", [P, HALVES, G])
        sums = sb("d_sums", [P, IMAGES, G])
        mean = sb("d_mean", [P, IMAGES, G])
        dev = sb("d_dev", [P, IMAGES, G])
        var = sb("d_var", [P, IMAGES, G])
        rstd = sb("d_rstd", [P, IMAGES, G])
        rows = sb("d_rows", [1, G, PER_NORM, 2, IMAGES])
        ps = ctx.enter_context(nc.psum_tensor("d_ps", [P, 4, 512], F32))
        loaded, oned, steps, summed, rooted, stored = (
            sem(n) for n in ("d_loaded", "d_oned", "d_steps", "d_summed", "d_rooted", "d_stored"))
        block = ctx.enter_context(nc.Block())
        flat = lambda t: t[:, :, :].rearrange("p b g -> p (b g)")

        STEP_DEV = 3 + 4 * 4
        STEP_VAR = STEP_DEV + 1

        @block.sync
        def _(sp):
            sp.dma_start(st[:, :], stats.rearrange("p b h n -> p (b h n)")).then_inc(loaded, 16)
            sp.wait_ge(steps, STEP_VAR + 7)
            sp.dma_start(norm.rearrange("(o c) k b -> o (c k b)", o=1),
                         rows[:, :, :, :, :].rearrange("o g c k b -> o (g c k b)")).then_inc(stored, 16)
            sp.wait_ge(stored, 16)

        @block.gpsimd
        def _(pool):
            pool.memset(ones[:, :], 1.0).then_inc(oned, 1)

        @block.tensor
        def _(pe):
            pe.wait_ge(oned, 1)
            for n, (src, after) in enumerate(((sums, 2), (var, STEP_DEV))):
                pe.wait_ge(steps, after)
                for c in range(2):
                    m = pe.matmul(ps[:, 2 * n + c, :], ones[:, :], flat(src)[:, c * 512:(c + 1) * 512],
                                  start=True, stop=True)
                m.then_inc(summed, 1)

        @block.scalar
        def _(act):
            act.wait_ge(steps, STEP_VAR)
            act.activation(flat(dev), flat(var), ACT.Sqrt).then_inc(rooted, 1)

        @block.vector
        def _(dve):
            done = [0]

            def step(ins):
                done[0] += 1
                ins.then_inc(steps, 1)
                dve.wait_ge(steps, done[0])

            def part(o, h):
                return view(st[:, :], h * G * 6 + o, [[2 * G * 6, IMAGES], [6, G]])

            dve.wait_ge(loaded, 16)
            step(dve.tensor_tensor(pairs[:, :, :], view(st[:, :], 1, [[G * 6, HALVES], [6, G]]),
                                   view(st[:, :], 4, [[G * 6, HALVES], [6, G]]), ALU.add))
            step(dve.tensor_tensor(sums[:, :, :], view(flat(pairs), 0, [[2 * G, IMAGES], [1, G]]),
                                   view(flat(pairs), G, [[2 * G, IMAGES], [1, G]]), ALU.add))
            dve.wait_ge(summed, 1)
            step(dve.tensor_scalar(flat(mean), ps[:, 0:2, :].rearrange("p a n -> p (a n)"),
                                   1.0 / (4 * P), None, ALU.mult))
            each = float(PER_NORM * WH // 2)
            n = 0
            for h in range(2):
                for e in range(2):
                    step(dve.tensor_tensor(dev[:, :, :], part(3 * e + 1, h), mean[:, :, :], ALU.subtract))
                    step(dve.tensor_tensor(dev[:, :, :], dev[:, :, :], dev[:, :, :], ALU.mult))
                    dst = var if n == 0 else dev
                    step(dve.scalar_tensor_tensor(dst[:, :, :], dev[:, :, :], each, part(3 * e + 2, h), ALU.mult, ALU.add))
                    step(dve.tensor_tensor(var[:, :, :], var[:, :, :], dev[:, :, :], ALU.add) if n else
                         dve.tensor_scalar(var[:, :, :], var[:, :, :], 0.0, None, ALU.max))
                    n += 1
            dve.wait_ge(summed, 2)
            step(dve.tensor_scalar(flat(var), ps[:, 2:4, :].rearrange("p a n -> p (a n)"),
                                   1.0 / NORM_COUNT, EPS, ALU.mult, ALU.add))
            dve.wait_ge(rooted, 1)
            step(dve.reciprocal(flat(rstd), flat(dev)))
            newton(dve, step, flat(rstd), flat(var), flat(dev))
            step(dve.tensor_tensor(flat(mean), flat(mean), flat(rstd), ALU.mult))
            for c in range(PER_NORM):
                dve.tensor_copy(rows[:, :, c, 0, :], rstd[0:1, :, :].rearrange("p b g -> p g b"))
                m = dve.tensor_copy(rows[:, :, c, 1, :], mean[0:1, :, :].rearrange("p b g -> p g b"))
            step(m)
            assert done[0] == STEP_VAR + 7


def long_phase(nc, a, x1, norm, kpad, out):
    TILE = IMAGES * 2 * C8 * WH
    N = IMAGES * WH
    FAR = (FAR55 - 1) // 2
    TAPS = 2 * FAR + 1
    UNITS = 3
    STEPS = 2 * C8
    NORMS = 5
    with ExitStack() as ctx:
        sb = lambda n, s, d=F32: ctx.enter_context(nc.sbuf_tensor(n, s, d))
        sem = lambda n: ctx.enter_context(nc.semaphore(n))
        raw = [sb(f"e_raw{i}", [P, TILE]) for i in range(2)]
        nrm = [sb(f"e_norm{i}", [P, C8, 2, IMAGES]) for i in range(2)]
        t = [sb(f"e_t{i}", [P, TL55]) for i in range(2)]
        g = sb("e_g", [P, TL55 - PW])
        th = [sb(f"e_th{s}", [P, TAPS * P], F32R) for s in range(UNITS)]
        tl = [sb(f"e_tl{s}", [P, TAPS * P], F32R) for s in range(UNITS)]
        xn = [sb(f"e_xn{e}", [P, N]) for e in range(2)]
        xs = sb("e_xs", [P, N])
        xh = [sb(f"e_xh{s}", [P, N], F32R) for s in range(UNITS)]
        xl = [sb(f"e_xl{s}", [P, N], F32R) for s in range(UNITS)]
        res = [sb(f"e_res{i}", [P, 2, N]) for i in range(2)]
        ps = ctx.enter_context(nc.psum_tensor("e_ps", [P, 2, 4, 512], F32))
        landed = [sem(f"e_landed{i}") for i in range(2)]
        t_landed = [sem(f"e_t_landed{i}") for i in range(2)]
        stored = [sem(f"e_stored{i}") for i in range(2)]
        g_made, normed, hi, lo, prod, taken, done, passed = (
            sem("e_" + n) for n in ("g_made", "normed", "hi", "lo", "prod", "taken", "done", "passed"))
        block = ctx.enter_context(nc.Block())

        def blocks(i, c, e):
            return view(raw[i][:, :], c * WH + e, [[C8 * WH, 2], [2, WH // 2], [2 * C8 * WH, IMAGES]])

        def in_order(ap):
            return ap.rearrange("p (a w b) -> p a w b", a=2, w=WH // 2)

        def matrices(p, s):
            src, first = ((t[p], PW), (g, PW), (g, 2 * PW))[s]
            return view(src[:, :], TL55 - 1 - first, [[-2 * PW, TAPS], [-1, PW], [-U55, HEIGHT]])

        def taps(ap):
            return ap.rearrange("p (d u h) -> p d u h", d=TAPS, u=PW)

        @block.sync
        def _(sp):
            for i in range(2):
                sp.sem_inc(stored[i], 16)

            def load(g, i, first=False):
                if not first:
                    sp.wait_ge(done, g * (2 * C8) + (4 - 4 * C8 + 2 * C8))
                src = x1[bass.ds(g, 1), :, :, :, :].rearrange("o p b h n -> (o p) (b h n)")
                sp.dma_start(raw[i][:, :], src).then_inc(landed[i], 16)
                src = norm[bass.ds(g * C8, C8), :, :].rearrange("c k b -> (c k b)")
                sp.dma_start(nrm[i][:, :, :, :].rearrange("p c k b -> p (c k b)"), src.partition_broadcast(P)).then_inc(landed[i], 16)

            def store(g):
                with sp.Fori(0, C8 // 2) as m:
                    c = m * 2
                    for p in range(2):
                        sp.wait_ge(done, g * (2 * C8) + c * 2 + (2 * p + 6))
                        dst = out[bass.ds(g * C8 + c + p, 1), :, :].rearrange("o p n -> (o p) n")
                        sp.dma_start(dst, res[p][:, :, :].rearrange("p e n -> p (e n)")).then_inc(stored[p], 16)

            load(0, 0, True)
            load(1, 1, True)
            with sp.Fori(0, (CG - 2) // 2) as m:
                g = m * 2
                store(g)
                load(g + 2, 0)
                store(g + 1)
                load(g + 3, 1)
            store(CG - 2)
            store(CG - 1)
            for p in range(2):
                sp.wait_ge(stored[p], 16 * (CHANNELS // 2 + 1))

        @block.gpsimd
        def _(pool):
            def load(c, p):
                row = kpad[bass.ds(c, 1), :]
                src = bass.AP(tensor=row.tensor, offset=row.offset, ap=[[1, PW], [U55, HEIGHT], [1, TL55]])
                pool.dma_start(t[p][:, :], src).then_inc(t_landed[p], 16)

            def differences(c, p, first=False):
                pool.wait_ge(t_landed[p], (c - p) * 8 + 16)
                if not first:
                    pool.wait_ge(lo, c * (2 * UNITS))
                pool.sem_inc(passed, 1)
                pool.tensor_tensor(g[:, :], t[p][:, 0:TL55 - PW], t[p][:, PW:TL55], ALU.subtract).then_inc(g_made, 1)

            def refill(c, p):
                pool.wait_ge(g_made, c + 1)
                pool.wait_ge(lo, c * (2 * UNITS) + 2)
                pool.sem_inc(passed, 1)
                load(c + 2, p)

            for p in range(2):
                load(p, p)
            for p in range(2):
                differences(p, p, first=p == 0)
                refill(p, p)
            with pool.Fori(1, CHANNELS // 2 - 1) as m:
                c = m * 2
                for p in range(2):
                    differences(c + p, p)
                    refill(c + p, p)
            for p in range(2):
                differences(CHANNELS - 2 + p, p)

        @block.scalar
        def _(act):
            with act.Fori(0, CG // 2) as gg:
                for j in range(STEPS):
                    p = j % 2
                    for s in range(UNITS):
                        act.wait_ge(prod, gg * (UNITS * STEPS) + (UNITS * j + s + 1))
                        if s == 0:
                            act.wait_ge(t_landed[p], gg * (16 * C8) + 16 * (j // 2 + 1))
                        if s == 1:
                            act.wait_ge(g_made, gg * STEPS + (j + 1))
                        act.activation(taps(th[s][:, :]), matrices(p, s), ACT.Copy).then_inc(hi, 1)
                        if s == 0:
                            act.wait_ge(normed, gg * (NORMS * STEPS) + NORMS * (j + 1))
                        act.activation(xh[s][:, :], (xs, xn[1], xn[0])[s][:, :], ACT.Copy).then_inc(hi, 1)

        @block.vector
        def _(dve):
            dve.sem_inc(done, 4)

            def normalise(gg, j):
                i, c = j // C8, j % C8
                n = gg * (NORMS * STEPS) + NORMS * j
                if c == 0:
                    dve.wait_ge(landed[i], gg * 32 + 32)
                wide = lambda k: view(nrm[i][:, c, k, :], 0, [[0, 2], [0, WH // 2], [1, IMAGES]])
                for e in range(2):
                    dve.tensor_tensor(in_order(xn[e][:, :]), blocks(i, c, e), wide(0), ALU.mult).then_inc(normed, 1)
                for e in range(2):
                    dve.wait_ge(normed, n + (e + 1))
                    dve.tensor_tensor(in_order(xn[e][:, :]), in_order(xn[e][:, :]), wide(1), ALU.subtract).then_inc(normed, 1)
                dve.wait_ge(normed, n + 4)
                dve.tensor_tensor(xs[:, :], xn[0][:, :], xn[1][:, :], ALU.add).then_inc(normed, 1)
                dve.wait_ge(normed, n + 5)

            def lower(gg, j, s):
                n = gg * (2 * UNITS * STEPS) + 2 * (UNITS * j + s)
                dve.wait_ge(hi, n + 1)
                dve.tensor_tensor(taps(tl[s][:, :]), matrices(j % 2, s), taps(th[s][:, :].bitcast(F32)),
                                  ALU.subtract).then_inc(lo, 1)
                dve.wait_ge(hi, n + 2)
                dve.tensor_tensor(xl[s][:, :], (xs, xn[1], xn[0])[s][:, :], xh[s][:, :].bitcast(F32),
                                  ALU.subtract).then_inc(lo, 1)

            def take(gg, j):
                i, c, p = j // C8, j % C8, j % 2
                dve.wait_ge(prod, gg * (UNITS * STEPS) + UNITS * (j + 2))
                dve.wait_ge(stored[p], gg * (16 * C8) + 16 * (j // 2 + 1))
                for e in range(2):
                    dve.tensor_tensor(in_order(res[p][:, e, :]), in_order(ps[:, p, 0, :]), blocks(i, c, e),
                                      ALU.add).then_inc(taken, 1)
                for e, op in enumerate((ALU.subtract, ALU.add)):
                    dve.wait_ge(taken, gg * (2 * STEPS) + (2 * j + e + 1))
                    dve.tensor_tensor(res[p][:, e, :], res[p][:, e, :], ps[:, p, 1 + e, :], op).then_inc(done, 1)

            def groups(gg, first):
                for j in range(STEPS):
                    normalise(gg, j)
                    for s in range(UNITS):
                        lower(gg, j, s)
                    dve.wait_ge(lo, gg * (2 * UNITS * STEPS) + 2 * UNITS * (j + 1))
                    if j:
                        take(gg, j - 1)
                    elif not first:
                        take(gg - 1, STEPS - 1)

            groups(0, True)
            with dve.Fori(1, CG // 2) as gg:
                groups(gg, False)
            take(CG // 2 - 1, STEPS - 1)

        @block.tensor
        def _(pe):
            pe.sem_inc(prod, UNITS)
            order = sorted(range(-FAR, FAR + 1), key=abs)
            with pe.Fori(0, CHANNELS // 2) as m:
                n = m * 2
                for p in range(2):
                    pe.wait_ge(done, n * 2 + 2 * (p + 1))
                    for s in range(UNITS):
                        pe.wait_ge(lo, n * (2 * UNITS) + 2 * (UNITS * p + s + 1))
                        for d in order:
                            wt = slice((d + FAR) * P, (d + FAR + 1) * P)
                            w0, w1 = max(d, 0), WH + min(d, 0)
                            src = slice((w0 - d) * IMAGES, (w1 - d) * IMAGES)
                            m = matmul3(pe, ps[:, p, s, w0 * IMAGES:w1 * IMAGES], th[s][:, wt], tl[s][:, wt],
                                        xh[s][:, src], xl[s][:, src], start=d == 0, stop=d == order[-1])
                        m.then_inc(prod, 1)


def program(nc, a, out, scratch):
    kpad = scratch("kpad", [CHANNELS, LEN55])
    qkv = [scratch(n, [CG, P, IMAGES, 2, C8 * WH]) for n in ("q", "k", "v")]
    qkc = [scratch(n, [CG, P, IMAGES, 2, C8 * WH]) for n in ("q_conv", "k_conv", "cape")]
    x1 = scratch("x1", [CG, P, IMAGES, 2, C8 * WH])
    stats = scratch("stats", [P, IMAGES, 2, NORM_GROUPS * 6])
    norm = scratch("norm", [CHANNELS, 2, IMAGES])
    filter_phase(nc, a, kpad)
    with nc.sbuf_tensor("rstd0", [KP, IMAGES * KC], F32) as rstd, \
            nc.sbuf_tensor("shift0", [KP, IMAGES * KC], F32) as shift:
        stats0_phase(nc, a, rstd, shift)
        project_phase(nc, a, rstd, shift, qkv)
    depthwise_phase(nc, a, qkv, qkc)
    attention_phase(nc, a, qkv, qkc, x1, stats)
    stats1_phase(nc, a, stats, norm)
    long_phase(nc, a, x1, norm, kpad, out)


def kernel(**inputs):
    import numpy as np
    import concourse.bacc as bacc
    from concourse.bass_utils import run_bass_kernel_spmd

    f = {k: np.asarray(v) for k, v in inputs.items()}
    x = f["x"]
    split = x.reshape(IMAGES, CHANNELS, HEIGHT, 2, WH, PW)
    w = np.concatenate([f["L0_conv_w_qk"].reshape(2 * CHANNELS, CHANNELS), f["L0_conv_w_v"].reshape(CHANNELS, CHANNELS)])
    w_qkv = np.zeros((KP + 1, KC, QKV), np.float32)
    w_qkv[:KP] = w.T.reshape(KC, KP, QKV).transpose(1, 0, 2)
    w_qkv[KP, KC - 1] = np.concatenate([f["L0_conv_b_qk"], f["L0_conv_b_v"]])
    w5 = np.zeros((CG, 3, C8, LEN5), np.float32)
    rows = w5[:, :, :, :(2 * HEIGHT - 1) * U5].reshape(CG, 3, C8, 2 * HEIGHT - 1, U5)
    names = ("cape", "q5", "k5")
    for s, name in enumerate(names):
        r0 = HEIGHT - 1 - PAD5
        rows[:, s, :, r0:r0 + K5, 1:1 + K5] = f["L0_conv_w_" + name].reshape(CG, C8, K5, K5)
    chan = np.stack([f["L1_conv_" + n].reshape(KC, KP).T for n in ("deltas", "shift", "bias")], axis=1)
    arrays = {
        "x_ch": split.transpose(0, 1, 3, 4, 5, 2).reshape(IMAGES, CHANNELS, 2, WH * P),
        "x_tok": split.reshape(IMAGES, CG, C8, HEIGHT, 2, WH, PW).transpose(1, 6, 3, 0, 4, 2, 5)
        .reshape(CG, P, IMAGES, 2, C8 * WH),
        "w_qkv": w_qkv,
        "w5": w5.reshape(CG * 3 * C8, LEN5),
        "bias5": np.stack([f["L0_conv_b_" + n].reshape(CG, C8) for n in names], axis=1).reshape(CG * 3 * C8),
        "z": f["L1_conv_z"][0, :, ::-1, ::-1].reshape(EMB, K55 * K55),
        "dist": f["L1_conv_distance_map"][0, 0, ::-1, ::-1].reshape(K55 * K55),
        "w1t": f["L1_conv_W1"].T,
        "w2t": f["L1_conv_W2"].T,
        "w3t": f["L1_conv_W3"].T,
        "hid": np.stack([f["L1_conv_" + n].reshape(HID) for n in ("b1", "f1", "b2", "f2")], axis=1),
        "chan": chan,
        "mask": np.kron(np.eye(KP // PER_NORM), np.ones((PER_NORM, PER_NORM))).astype(np.float32),
        "ident": np.eye(P, dtype=np.float32),
    }
    arrays = {k: np.ascontiguousarray(v) for k, v in arrays.items()}
    nc = bacc.Bacc("TRN2", target_bir_lowering=False, num_devices=1)
    a = {k: nc.dram_tensor(f"in_{k}", v.shape, F32, kind="ExternalInput").ap() for k, v in arrays.items()}
    out = nc.dram_tensor("out", (CHANNELS, P, WP * IMAGES), F32, kind="ExternalOutput").ap()
    program(nc, a, out, lambda name, shape: nc.dram_tensor(name, shape, F32, kind="Internal").ap())
    r = run_bass_kernel_spmd(nc, [{f"in_{k}": v for k, v in arrays.items()}], core_ids=[0])
    y = r.results[0]["out"].reshape(CHANNELS, PW, HEIGHT, 2, WH, IMAGES)
    return np.ascontiguousarray(y.transpose(5, 0, 2, 4, 3, 1).reshape(IMAGES, CHANNELS, HEIGHT, WIDTH))
```

```python
from contextlib import ExitStack

import concourse.bass as bass
from concourse import mybir


F32 = mybir.dt.float32
F32R = mybir.dt.float32r
ALU = mybir.AluOpType
ACT = mybir.ActivationFunctionType
AX = mybir.AxisListType

P = 128
IMAGES, CHANNELS, HEIGHT, WIDTH = 32, 192, 64, 64
PW = 2
WP = WIDTH // PW
WH = WP // 2
HALVES = 2 * IMAGES
C8 = 8
CG = CHANNELS // C8
KC = 2
KP = CHANNELS // KC
QKV = 3 * CHANNELS
NORM_GROUPS = 32
PER_NORM = CHANNELS // NORM_GROUPS
NORM_COUNT = PER_NORM * HEIGHT * WIDTH
EPS = 1e-5
HEADS = 4
HD = CHANNELS // HEADS
HP = 64
TOKENS = 2 * P
WINDOWS = IMAGES * WP // 2
SCALE = HD ** -0.5

K5, PAD5 = 5, 2
K55, PAD55 = 55, 27
HID, EMB = 64, 32


def toeplitz(k, pad):
    far = (pad + 1) // PW
    u = PW * (2 * far + 1)
    return far, u, (2 * HEIGHT - 1) * u + 2


FAR5, U5, LEN5 = toeplitz(K5, PAD5)

FAR55 = (PAD55 + 1) // PW + 1
MID55 = PW * FAR55 + 1
U55 = MID55 + PAD55 + 1
TL55 = (HEIGHT - 1) * U55 + PW * (2 * FAR55 + 1)
LEN55 = 2 * HEIGHT * U55 - U55 + MID55 - PAD55


def view(ap, offset, dims):
    return bass.AP(tensor=ap.tensor, offset=ap.offset + offset, ap=[ap.ap[0], *dims])


def matmul3(pe, out, w_hi, w_lo, x_hi, x_lo, start, stop):
    pe.matmul(out, w_hi, x_hi, start=start, stop=False)
    pe.matmul(out, w_hi, x_lo, start=False, stop=False)
    return pe.matmul(out, w_lo, x_hi, start=False, stop=stop)


def filter_phase(nc, a, kpad):
    inv2pi, magic = 0.15915494309189535, 12582912.0
    c1, c2 = 6.28125, 0.0019353071795864769
    pi = 3.1415925
    n_pix = K55 * K55
    rows = [(r, min(8, K55 - r)) for r in range(0, K55, 8)]
    with ExitStack() as ctx:
        sb = lambda n, s, d=F32: ctx.enter_context(nc.sbuf_tensor(n, s, d))
        sem = lambda n: ctx.enter_context(nc.semaphore(n))
        z = sb("f_z", [EMB, n_pix])
        w1 = sb("f_w1", [EMB, HID])
        w2 = sb("f_w2", [HID, HID])
        w3 = sb("f_w3", [HID, CHANNELS])
        hid = sb("f_hid", [HID, 4])
        chan = sb("f_chan", [KP, 3, KC])
        dist = sb("f_dist", [KP, n_pix])
        slope = sb("f_slope", [KP, KC])
        decay = sb("f_decay", [KP, KC, n_pix])
        arg = sb("f_arg", [HID, n_pix])
        turns = sb("f_turns", [HID, n_pix])
        h1 = sb("f_h1", [HID, n_pix])
        h2 = sb("f_h2", [HID, n_pix])
        padded = sb("f_padded", [KP, KC, LEN55])
        ps = ctx.enter_context(nc.psum_tensor("f_ps", [P, 8, 512], F32))
        loaded, cleared, products, steps, funcs, stored = (
            sem(n) for n in ("f_loaded", "f_cleared", "f_products", "f_steps", "f_funcs", "f_stored"))
        LOADS = 7
        block = ctx.enter_context(nc.Block())

        @block.sync
        def _(sp):
            for dst, src in ((z[:, :], a["z"]), (w1[:, :], a["w1t"]), (w2[:, :], a["w2t"]),
                             (w3[:, :], a["w3t"]), (hid[:, :], a["hid"]), (chan[:, :, :], a["chan"]),
                             (dist[:, :], a["dist"].partition_broadcast(KP))):
                sp.dma_start(dst, src).then_inc(loaded, 16)
            sp.wait_ge(steps, 28)
            for k in range(KC):
                sp.dma_start(kpad[k * KP:(k + 1) * KP, :], padded[:, k, :]).then_inc(stored, 16)
            sp.wait_ge(stored, 16 * KC)

        @block.gpsimd
        def _(pool):
            pool.memset(padded[:, :, :], 0.0).then_inc(cleared, 1)

        @block.tensor
        def _(pe):
            pe.wait_ge(loaded, 16 * LOADS)
            for i, (r, n) in enumerate(rows):
                m = pe.matmul(ps[0:HID, i, 0:n * K55], w1[:, :], z[:, r * K55:(r + n) * K55],
                              start=True, stop=True)
            m.then_inc(products, 1)
            pe.wait_ge(funcs, 3)
            for i, (r, n) in enumerate(rows):
                m = pe.matmul(ps[0:HID, i, 0:n * K55], w2[:, :], h1[:, r * K55:(r + n) * K55],
                              start=True, stop=True)
            m.then_inc(products, 1)
            pe.wait_ge(funcs, 4)
            for k in range(KC):
                if k:
                    pe.wait_ge(steps, 20)
                for i, (r, n) in enumerate(rows):
                    m = pe.matmul(ps[0:KP, i, 0:n * K55], w3[:, k * KP:(k + 1) * KP],
                                  h2[:, r * K55:(r + n) * K55], start=True, stop=True)
                m.then_inc(products, 1)

        @block.scalar
        def _(act):
            act.wait_ge(steps, 1)
            for k in range(KC):
                act.activation(decay[:, k, :], dist[:, :], ACT.Exp, scale=slope[:, k:k + 1]).then_inc(funcs, 1)
            act.wait_ge(steps, 7)
            act.activation(h1[:, :], turns[:, :], ACT.Sin).then_inc(funcs, 1)
            act.wait_ge(steps, 13)
            act.activation(h2[:, :], turns[:, :], ACT.Sin).then_inc(funcs, 1)

        @block.vector
        def _(dve):
            done = [0]

            def step(ins):
                done[0] += 1
                ins.then_inc(steps, 1)
                dve.wait_ge(steps, done[0])

            dve.wait_ge(loaded, 16 * LOADS)
            step(dve.scalar_tensor_tensor(slope[:, :], chan[:, 0, :], -1.0, chan[:, 0, :], ALU.mult, ALU.min))
            for layer in range(2):
                dve.wait_ge(products, layer + 1)
                if layer:
                    dve.wait_ge(funcs, 3)
                for i, (r, n) in enumerate(rows):
                    m = dve.tensor_scalar(arg[:, r * K55:(r + n) * K55], ps[0:HID, i, 0:n * K55],
                                          hid[:, 2 * layer:2 * layer + 1], hid[:, 2 * layer + 1:2 * layer + 2],
                                          ALU.add, ALU.mult)
                step(m)
                step(dve.tensor_scalar(turns[:, :], arg[:, :], inv2pi, magic, ALU.mult, ALU.add))
                step(dve.tensor_scalar(turns[:, :], turns[:, :], magic, None, ALU.subtract))
                step(dve.scalar_tensor_tensor(arg[:, :], turns[:, :], -c1, arg[:, :], ALU.mult, ALU.add))
                step(dve.scalar_tensor_tensor(arg[:, :], turns[:, :], -c2, arg[:, :], ALU.mult, ALU.add))
                step(dve.tensor_scalar(turns[:, :], arg[:, :], pi, -pi, ALU.min, ALU.max))
            dve.wait_ge(cleared, 1)
            for k in range(KC):
                dve.wait_ge(products, 3 + k)
                for i, (r, n) in enumerate(rows):
                    dst = view(padded[:, k, :], (HEIGHT - 1 - PAD55 + r) * U55 + MID55 - PAD55, [[U55, n], [1, K55]])
                    step(dve.scalar_tensor_tensor(
                        dst, decay[:, k, r * K55:(r + n) * K55].rearrange("p (a b) -> p a b", b=K55),
                        chan[:, 1, k:k + 1], ps[0:KP, i, 0:n * K55].rearrange("p (a b) -> p a b", b=K55),
                        ALU.add, ALU.mult))
            centre = (HEIGHT - 1) * U55 + MID55
            assert done[0] == 27, done[0]
            for k in range(KC):
                m = dve.tensor_tensor(padded[:, k, centre:centre + 1], padded[:, k, centre:centre + 1],
                                      chan[:, 2, k:k + 1], ALU.add)
            step(m)


def newton(dve, step, y, v, t):
    step(dve.tensor_tensor(t, y, y, ALU.mult))
    step(dve.tensor_tensor(t, t, v, ALU.mult))
    step(dve.tensor_scalar(t, t, -0.5, 1.5, ALU.mult, ALU.add))
    step(dve.tensor_tensor(y, y, t, ALU.mult))


def project_phase(nc, a, qkv):
    PX = WH * P
    NC = QKV // 2
    REST = CHANNELS - P
    BIAS_HI, BIAS_LO = 96, REST
    SLOTS = 3
    PAIRS = WH // 2
    slot = lambda k: k % SLOTS if k < 4 * PAIRS - 2 else k - (4 * PAIRS - 2)
    FM = 512
    CHUNKS = PX // FM
    PARTS = 2 * 2 * CHUNKS
    STEPS = 16
    with ExitStack() as ctx:
        sb = lambda n, s, d=F32: ctx.enter_context(nc.sbuf_tensor(n, s, d))
        sem = lambda n: ctx.enter_context(nc.semaphore(n))
        x_first = [[sb(f"a_x_first{i}{h}", [P, PX]) for h in range(2)] for i in range(2)]
        x_rest = [sb(f"a_x_rest{i}", [P, PX]) for i in range(2)]
        first_hi = [sb(f"a_first_hi{h}", [P, PX], F32R) for h in range(2)]
        first_lo = [sb(f"a_first_lo{h}", [P, PX], F32R) for h in range(2)]
        rest_both = [sb(f"a_rest_both{h}", [P, PX], F32R) for h in range(2)]
        rest_hi = [sb(f"a_rest_hi{h}", [BIAS_HI + 1, PX], F32R) for h in range(2)]
        tok = [[sb(f"a_tok{h}{c}", [P, NC, WH]) for c in range(2)] for h in range(2)]
        w_hi = sb("a_w_hi", [P, QKV], F32R)
        w_lo = sb("a_w_lo", [P, QKV], F32R)
        w_rest = sb("a_w_rest", [P, QKV], F32R)
        w_rest_lo = sb("a_w_rest_lo", [BIAS_HI + 1, QKV], F32R)
        mask = sb("a_mask", [P, 2, 2, P])
        st = sb("a_st", [P, 3, CHUNKS * 6])
        dev = sb("a_dev", [P, 3, 2 * CHUNKS])
        t, mean, var, rstd, shift = (sb("a_" + n, [P, 2]) for n in ("t", "mean", "var", "rstd", "shift"))
        ps = ctx.enter_context(nc.psum_tensor("a_ps", [P, SLOTS, 2, 512], F32))
        ps_sums = ctx.enter_context(nc.psum_tensor("a_ps_sums", [P, 512], F32))
        sums = lambda o: ps_sums[:, o:o + 1]
        w_src = tok[1][1][:, 0:3 * QKV // WH, :].rearrange("p a b -> p (a b)")
        src = [w_src[:, n * QKV:(n + 1) * QKV] for n in range(3)]
        w_landed, w_split, ones = sem("a_w_landed"), sem("a_w_split"), sem("a_ones")
        x_landed = [sem(f"a_x_landed{i}") for i in range(2)]
        stored = [sem(f"a_stored{i}") for i in range(4)]
        steps, summed, rooted, normed, hi, copied, lo, prod, prod_free, bn, passed = (sem("a_" + n) for n in (
            "steps", "summed", "rooted", "normed", "hi", "copied", "lo", "prod", "prod_free", "bn", "passed"))
        block = ctx.enter_context(nc.Block())

        @block.sync
        def _(sp):
            def load(i, par):
                for h in range(2):
                    sp.dma_start(x_first[par][h][:, :], a["x_ch"][bass.ds(i, 1), 0:P, h, :].rearrange("o c n -> (o c) n")
                                 ).then_inc(x_landed[par], 16)
                    sp.dma_start(x_rest[par][h * REST:(h + 1) * REST, :],
                                 a["x_ch"][bass.ds(i, 1), P:CHANNELS, h, :].rearrange("o c n -> (o c) n")
                                 ).then_inc(x_landed[par], 16)

            def image(i, par, more):
                if more:
                    sp.wait_ge(lo, i * 4 + 4)
                    sp.sem_inc(passed, 1)
                    load(i + 2, par)
                for h in range(2):
                    for c in range(2):
                        u = 2 * h + c
                        sp.wait_ge(prod_free, i * 32 + (PAIRS * (u + 1) + SLOTS))
                        sp.sem_inc(passed, 1)
                        out = [(0, 0, CHANNELS), (1, 0, NC - CHANNELS)] if c == 0 else \
                            [(1, NC - CHANNELS, CHANNELS), (2, 0, CHANNELS)]
                        o = 0
                        for s, c0, c1 in out:
                            dst = qkv[s][c0 // C8:c1 // C8, :, bass.ds(i, 1), h, :].rearrange("g p o n -> p (g o) n")
                            piece = tok[h][c][:, o:o + c1 - c0, :].rearrange("p (g c) w -> p g (c w)", c=C8)
                            sp.dma_start(dst, piece).then_inc(stored[u], 16)
                            o += c1 - c0

            for n, w in enumerate(("w_first", "w_rest", "w_bias")):
                sp.dma_start(src[n], a[w]).then_inc(w_landed, 16)
            sp.dma_start(mask[:, :, :, :], a["mask"]).then_inc(w_landed, 16)
            for par in range(2):
                load(par, par)
            with sp.Fori(0, IMAGES // 2 - 1) as m:
                for par in range(2):
                    image(m * 2 + par, par, True)
            for par in range(2):
                image(IMAGES - 2 + par, par, False)
            for u in range(4):
                sp.wait_ge(stored[u], 32 * (IMAGES + 1))

        @block.gpsimd
        def _(pool):
            for u in range(4):
                pool.sem_inc(stored[u], 32)
            for h in range(2):
                pool.memset(rest_hi[h][REST:BIAS_HI + 1, :].bitcast(F32), 1.0).then_inc(ones, 1)
            with pool.Fori(0, IMAGES) as i:
                for h in range(2):
                    pool.wait_ge(hi, i * 4 + (2 * h + 1))
                    pool.sem_inc(passed, 1)
                    pool.tensor_copy(rest_hi[h][0:REST, :], rest_both[h][h * REST:(h + 1) * REST, :]).then_inc(copied, 1)

        @block.vector
        def _(dve):
            dve.wait_ge(w_split, 2)
            dve.tensor_tensor(w_lo[:, :], src[0], w_hi[:, :].bitcast(F32), ALU.subtract).then_inc(w_split, 1)
            dve.tensor_tensor(w_rest_lo[:, :], src[2][0:BIAS_HI + 1, :], w_rest_lo[:, :].bitcast(F32), ALU.subtract).then_inc(w_split, 1)

            def statistics(m, par, i):
                done = [0]

                def step(ins):
                    done[0] += 1
                    ins.then_inc(steps, 1)
                    dve.wait_ge(steps, i * STEPS + done[0])

                part = lambda o, n0, n1: view(st[:, n0, :], o, [[3, 2 * CHUNKS * (n1 - n0)]])
                flat = lambda n0, n1: dev[:, n0:n1, :].rearrange("p a b -> p (a b)")

                def reduce(source):
                    dve.tensor_reduce(t[:, 0:1], source(0, 2), AX.X, ALU.add)
                    step(dve.tensor_reduce(t[:, 1:2], source(2, 3), AX.X, ALU.add))

                dve.wait_ge(x_landed[par], m * 64 + 64)
                for n, tile in enumerate((x_first[par][0], x_first[par][1], x_rest[par])):
                    for k in range(CHUNKS):
                        last = dve.bn_stats(st[:, n, k * 6:k * 6 + 6], tile[:, k * FM:(k + 1) * FM])
                last.then_inc(bn, 1)
                dve.wait_ge(bn, i + 1)
                reduce(lambda n0, n1: part(1, n0, n1))
                dve.wait_ge(summed, i * 2 + 1)
                for k in range(2):
                    step(dve.tensor_scalar(mean[:, k:k + 1], sums(k), 1.0 / (PER_NORM * PARTS), None, ALU.mult))
                for k, (n0, n1) in enumerate(((0, 2), (2, 3))):
                    step(dve.tensor_scalar(flat(n0, n1), part(1, n0, n1), mean[:, k:k + 1], None, ALU.subtract))
                step(dve.tensor_tensor(flat(0, 3), flat(0, 3), flat(0, 3), ALU.mult))
                step(dve.scalar_tensor_tensor(flat(0, 3), flat(0, 3), FM / 2.0, part(2, 0, 3), ALU.mult, ALU.add))
                reduce(flat)
                assert done[0] == 8
                dve.wait_ge(summed, i * 2 + 2)
                for k in range(2):
                    step(dve.tensor_scalar(var[:, k:k + 1], sums(k + 2), 1.0 / NORM_COUNT, EPS, ALU.mult, ALU.add))
                dve.wait_ge(rooted, i + 1)
                step(dve.reciprocal(rstd[:, :], t[:, :]))
                newton(dve, step, rstd[:, :], var[:, :], t[:, :])
                step(dve.scalar_tensor_tensor(shift[:, :], mean[:, :], -1.0, rstd[:, :], ALU.mult, ALU.mult))
                assert done[0] == STEPS

            def split(i, par, h):
                tiles = ([(x_rest[par], 1)] if h == 0 else []) + [(x_first[par][h], 0)]
                for tile, k in tiles:
                    dve.tensor_scalar(tile[:, :], tile[:, :], rstd[:, k:k + 1], shift[:, k:k + 1],
                                      ALU.mult, ALU.add).then_inc(normed, 1)
                dve.wait_ge(hi, i * 4 + (2 * h + 1))
                own = slice(h * REST, (h + 1) * REST)
                other = slice((1 - h) * REST, (2 - h) * REST)
                dve.tensor_tensor(rest_both[h][other, :], x_rest[par][own, :], rest_both[h][own, :].bitcast(F32),
                                  ALU.subtract).then_inc(lo, 1)
                dve.wait_ge(hi, i * 4 + (2 * h + 2))
                dve.tensor_tensor(first_lo[h][:, :], x_first[par][h][:, :], first_hi[h][:, :].bitcast(F32),
                                  ALU.subtract).then_inc(lo, 1)

            statistics(0, 0, 0)
            split(0, 0, 0)
            with dve.Fori(0, IMAGES // 2 - 1) as m:
                i = m * 2
                split(i, 0, 1)
                statistics(m, 1, i + 1)
                split(i + 1, 1, 0)
                split(i + 1, 1, 1)
                statistics(m + 1, 0, i + 2)
                split(i + 2, 0, 0)
            i = IMAGES - 2
            split(i, 0, 1)
            statistics(IMAGES // 2 - 1, 1, i + 1)
            split(i + 1, 1, 0)
            split(i + 1, 1, 1)

        @block.scalar
        def _(act):
            act.wait_ge(w_landed, 64)
            act.activation(w_hi[:, :], src[0], ACT.Copy)
            act.activation(w_rest[:, :], src[1], ACT.Copy).then_inc(w_split, 1)
            act.activation(w_rest_lo[:, :], src[2][0:BIAS_HI + 1, :], ACT.Copy).then_inc(w_split, 1)
            act.wait_ge(w_split, 4)
            act.activation(w_rest_lo[BIAS_HI:BIAS_HI + 1, :], src[2][BIAS_HI:BIAS_HI + 1, :], ACT.Copy).then_inc(w_split, 1)
            act.sem_inc(prod_free, SLOTS)

            def root(i):
                act.wait_ge(steps, i * STEPS + 10)
                act.activation(t[:, :], var[:, :], ACT.Sqrt).then_inc(rooted, 1)

            def split_rest(i, par, h):
                act.wait_ge(prod, i * 32 + 16 * (h + 1))
                act.wait_ge(normed, i * 3 + 1)
                own = slice(h * REST, (h + 1) * REST)
                act.activation(rest_both[h][own, :], x_rest[par][own, :], ACT.Copy).then_inc(hi, 1)

            def split_first(i, par, h):
                act.wait_ge(normed, i * 3 + (2 + h))
                act.activation(first_hi[h][:, :], x_first[par][h][:, :], ACT.Copy).then_inc(hi, 1)

            def take(i, k):
                u, n = k // PAIRS, k % PAIRS
                if n == 0:
                    act.wait_ge(stored[u], i * 32 + 32)
                act.wait_ge(prod, i * 32 + (k + 33))
                dst = view(tok[u // 2][u % 2][:, :, :].rearrange("p a b -> p (a b)"), 2 * n, [[1, 2], [WH, NC]])
                act.activation(dst, ps[:, slot(k), :, 0:NC], ACT.Copy).then_inc(prod_free, 1)

            def image(i, par, last):
                for k in range(4 * PAIRS):
                    take(i, k)
                    if k == 1:
                        split_rest(i, par, 1)
                    if k == 3:
                        split_first(i, par, 1)
                    if not last and k == 2 * PAIRS + 2:
                        root(i + 1)
                    if not last and k == 2 * PAIRS + 6:
                        split_rest(i + 1, 1 - par, 0)
                    if not last and k == 3 * PAIRS:
                        split_first(i + 1, 1 - par, 0)

            root(0)
            split_rest(0, 0, 0)
            split_first(0, 0, 0)
            with act.Fori(0, IMAGES // 2 - 1) as m:
                for par in range(2):
                    image(m * 2 + par, par, False)
            image(IMAGES - 2, 0, False)
            image(IMAGES - 1, 1, True)

        @block.tensor
        def _(pe):
            def group_sums(i, n):
                pe.wait_ge(steps, i * STEPS + (1, 8)[n])
                for o in range(2):
                    for k in range(2):
                        m = pe.matmul(sums(2 * n + o), mask[:, k, o, :], t[:, k:k + 1], start=k == 0, stop=k == 1)
                m.then_inc(summed, 1)

            def image(i, last):
                for h in range(2):
                    pe.wait_ge(lo, i * 4 + 2 * (h + 1))
                    pe.wait_ge(copied, i * 2 + (h + 1))
                    for c in range(2):
                        for n in range(PAIRS):
                            k = (2 * h + c) * PAIRS + n
                            if not last and k == 2 * PAIRS - 2:
                                group_sums(i + 1, 0)
                            if not last and k == 2 * PAIRS + 1:
                                group_sums(i + 1, 1)
                            pe.wait_ge(prod_free, i * 32 + (k + 2 if k < 2 else k + 1))
                            oc = slice(c * NC, (c + 1) * NC)
                            for b in range(2):
                                out = ps[:, slot(k), b, 0:NC]
                                px = slice((2 * n + b) * P, (2 * n + b + 1) * P)
                                pe.matmul(out, first_hi[h][:, px], w_hi[:, oc], start=True, stop=False)
                                pe.matmul(out, first_hi[h][:, px], w_lo[:, oc], start=False, stop=False)
                                pe.matmul(out, first_lo[h][:, px], w_hi[:, oc], start=False, stop=False)
                                pe.matmul(out, rest_both[h][:, px], w_rest[:, oc], start=False, stop=False)
                                m = pe.matmul(out, rest_hi[h][:, px], w_rest_lo[:, oc], start=False, stop=True)
                            m.then_inc(prod, 1)

            pe.sem_inc(prod, 32)
            pe.wait_ge(w_landed, 64)
            for n in range(2):
                group_sums(0, n)
            pe.wait_ge(w_split, 5)
            pe.wait_ge(ones, 2)
            with pe.Fori(0, IMAGES - 1) as i:
                image(i, False)
            image(IMAGES - 1, True)


def depthwise_phase(nc, a, qkv, qkc):
    TILE = IMAGES * 2 * C8 * WH
    N = IMAGES * WP
    STEPS = 3 * C8
    SLOTS = 3
    RING = 8
    with ExitStack() as ctx:
        sb = lambda n, s, d=F32: ctx.enter_context(nc.sbuf_tensor(n, s, d))
        sem = lambda n: ctx.enter_context(nc.semaphore(n))
        raw = {n: sb(f"b_raw_{n}", [P, TILE]) for n in ("v0", "v1", "q", "k")}
        t5 = [sb(f"b_t{i}", [P, HEIGHT * U5]) for i in range(RING)]
        th = [sb(f"b_th{i}", [P, U5 * HEIGHT], F32R) for i in range(SLOTS)]
        tl = [sb(f"b_tl{i}", [P, U5 * HEIGHT], F32R) for i in range(SLOTS)]
        xh = [sb(f"b_xh{i}", [P, N], F32R) for i in range(SLOTS)]
        xl = [sb(f"b_xl{i}", [P, N], F32R) for i in range(SLOTS)]
        bias = sb("b_bias", [P, CG * STEPS])
        ps = ctx.enter_context(nc.psum_tensor("b_ps", [P, SLOTS, 2, 512], F32))
        landed = {n: sem(f"b_landed_{n}") for n in raw}
        stored = {n: sem(f"b_stored_{n}") for n in raw}
        t_landed = [sem(f"b_t_landed{i}") for i in range(RING)]
        passed, b_landed, hi, lo, prod, done = (sem("b_" + n) for n in ("passed", "b_landed", "hi", "lo", "prod", "done"))
        block = ctx.enter_context(nc.Block())

        def channel(tile, c):
            return view(raw[tile][:, :], c * WH, [[C8 * WH, 2], [1, WH], [2 * C8 * WH, IMAGES]])

        def in_order(ap):
            return ap.rearrange("p (a w b) -> p a w b", a=2, w=WH)

        def toeplitz_rows(tile):
            return view(tile[:, :], HEIGHT * U5 - 1, [[-1, U5], [-U5, HEIGHT]])

        def matrices(tile):
            return tile.rearrange("p (u h) -> p u h", u=U5)

        def place(j):
            return (f"v{j // STEPS}", "q", "k")[j % STEPS // C8], j % C8

        @block.sync
        def _(sp):
            sp.dma_start(bias[:, :], a["bias5"].partition_broadcast(P)).then_inc(b_landed, 16)
            scratch_in = {"v0": qkv[2], "v1": qkv[2], "q": qkv[0], "k": qkv[1]}
            scratch_out = {"v0": qkc[2], "v1": qkc[2], "q": qkc[0], "k": qkc[1]}

            def rows(t, g):
                return t[bass.ds(g, 1), :, :, :, :].rearrange("o p b h n -> (o p) (b h n)")

            def load(n, g):
                sp.dma_start(raw[n][:, :], rows(scratch_in[n], g)).then_inc(landed[n], 16)

            def store(n, g, k):
                sp.wait_ge(done, g * (2 * STEPS) + (2 * C8 * (k + 1) + 2 * SLOTS))
                sp.sem_inc(passed, 1)
                sp.dma_start(rows(scratch_out[n], g), raw[n][:, :]).then_inc(stored[n], 16)

            def group(g, i, m, last):
                v = f"v{i}"
                store(v, g, 0)
                store("q", g, 1)
                if not (last and i == 1):
                    sp.wait_ge(stored["q"], m * 32 + (16 * i + 16))
                    sp.sem_inc(passed, 1)
                    load("q", g + 1)
                store("k", g, 2)
                if not last:
                    sp.wait_ge(stored[v], m * 16 + 16)
                    sp.sem_inc(passed, 1)
                    load(v, g + 2)
                if not (last and i == 1):
                    sp.wait_ge(stored["k"], m * 32 + (16 * i + 16))
                    sp.sem_inc(passed, 1)
                    load("k", g + 1)

            load("v0", 0)
            sp.wait_ge(t_landed[RING - 1], 16)
            load("q", 0)
            load("k", 0)
            load("v1", 1)
            with sp.Fori(0, CG // 2 - 1) as m:
                group(m * 2, 0, m, False)
                group(m * 2 + 1, 1, m, False)
            group(CG - 2, 0, CG // 2 - 1, True)
            group(CG - 1, 1, CG // 2 - 1, True)
            for n in raw:
                sp.wait_ge(stored[n], 16 * CG if n in "qk" else 8 * CG)

        @block.gpsimd
        def _(pool):
            def load(n, r):
                row = a["w5"][bass.ds(n, 1), :]
                src = bass.AP(tensor=row.tensor, offset=row.offset, ap=[[1, PW], [U5, HEIGHT], [1, HEIGHT * U5]])
                pool.dma_start(t5[r][:, :], src).then_inc(t_landed[r], 16)

            for r in range(RING):
                load(r, r)
            with pool.Fori(1, CG * STEPS // RING) as m:
                for r in range(RING):
                    pool.wait_ge(lo, m * (2 * RING) + (2 * r + 1 - 2 * RING))
                    pool.sem_inc(passed, 1)
                    load(m * RING + r, r)

        @block.scalar
        def _(act):
            with act.Fori(0, CG // 2) as gg:
                for j in range(2 * STEPS):
                    (tile, c), p, r = place(j), j % SLOTS, j % RING
                    if c == 0:
                        each = 16 if tile[0] == "v" else 32
                        act.wait_ge(landed[tile], gg * each + (16 if tile[0] == "v" else 16 * (j // STEPS + 1)))
                    act.wait_ge(prod, gg * (2 * STEPS) + (j + 1))
                    act.wait_ge(t_landed[r], gg * (16 * 2 * STEPS // RING) + 16 * (j // RING + 1))
                    act.activation(matrices(th[p][:, :]), toeplitz_rows(t5[r]), ACT.Copy).then_inc(hi, 1)
                    act.activation(in_order(xh[p][:, :]), channel(tile, c), ACT.Copy).then_inc(hi, 1)

        @block.vector
        def _(dve):
            dve.sem_inc(done, 2 * SLOTS)
            dve.wait_ge(b_landed, 16)

            def lower(gg, j):
                (tile, c), p, r = place(j), j % SLOTS, j % RING
                n = gg * (4 * STEPS) + 2 * j
                dve.wait_ge(hi, n + 1)
                dve.tensor_tensor(matrices(tl[p][:, :]), toeplitz_rows(t5[r]), matrices(th[p][:, :].bitcast(F32)),
                                  ALU.subtract).then_inc(lo, 1)
                dve.wait_ge(hi, n + 2)
                dve.tensor_tensor(in_order(xl[p][:, :]), channel(tile, c), in_order(xh[p][:, :]).bitcast(F32),
                                  ALU.subtract).then_inc(lo, 1)
                dve.wait_ge(lo, n + 2)

            def take(gg, j):
                (tile, c), p = place(j), j % SLOTS
                dve.wait_ge(prod, gg * (2 * STEPS) + (j + SLOTS + 1))
                own = bias[:, bass.ds(gg * (2 * STEPS) + j, 1)]
                if tile[0] != "v":
                    dve.wait_ge(done, gg * (4 * STEPS) + (2 * (j // STEPS * STEPS + c + 1) + 2 * SLOTS))
                for h in range(2):
                    at = lambda t: view(raw[t][:, :], (h * C8 + c) * WH, [[1, WH], [2 * C8 * WH, IMAGES]])
                    src = ps[:, p, h, :].rearrange("p (w b) -> p w b", w=WH)
                    if tile[0] == "v":
                        dve.tensor_scalar(at(tile), src, own, None, ALU.add).then_inc(done, 1)
                    else:
                        dve.scalar_tensor_tensor(at(tile), src, own, at(f"v{j // STEPS}"), ALU.add, ALU.add).then_inc(done, 1)

            def groups(gg, first):
                for j in range(2 * STEPS):
                    lower(gg, j)
                    if j:
                        take(gg, j - 1)
                    elif not first:
                        take(gg - 1, 2 * STEPS - 1)

            groups(0, True)
            with dve.Fori(1, CG // 2) as gg:
                groups(gg, False)
            take(CG // 2 - 1, 2 * STEPS - 1)

        @block.tensor
        def _(pe):
            pe.sem_inc(prod, SLOTS)
            with pe.Fori(0, CG * STEPS // SLOTS) as m:
                n = m * SLOTS
                for p in range(SLOTS):
                    pe.wait_ge(lo, n * 2 + 2 * (p + 1))
                    pe.wait_ge(done, n * 2 + 2 * (p + 1))
                    for d in (0, -1, 1):
                        wt = slice((2 * d + 2 * FAR5) * HEIGHT, (2 * d + 2 * FAR5 + 2) * HEIGHT)
                        for h in range(2):
                            w0, w1 = max(d, h * WH), min(WP + d, (h + 1) * WH)
                            o = ps[:, p, h, (w0 - h * WH) * IMAGES:(w1 - h * WH) * IMAGES]
                            src = slice((w0 - d) * IMAGES, (w1 - d) * IMAGES)
                            last = matmul3(pe, o, th[p][:, wt], tl[p][:, wt], xh[p][:, src], xl[p][:, src],
                                           start=d == 0, stop=d == 1)
                    last.then_inc(prod, 1)


def attention_phase(nc, a, qkv, qkc, x1, stats):
    HALF = CG * C8 * WH
    HW = WH // 2
    PARTS = HW - 2
    with ExitStack() as ctx:
        sb = lambda n, s, d=F32: ctx.enter_context(nc.sbuf_tensor(n, s, d))
        sem = lambda n: ctx.enter_context(nc.semaphore(n))
        rqk = [sb(f"c_rqk{i}", [P, 2, HALF]) for i in range(2)]
        rv = [sb(f"c_rv{i}", [P, HALF]) for i in range(2)]
        rcx = [sb(f"c_rcx{i}", [P, 2, HALF]) for i in range(2)]
        x1t = [sb(f"c_x1t{i}", [P, HALF]) for i in range(2)]
        qk = [sb(f"c_qk{i}", [P, 2, 2, HEADS * HP]) for i in range(2)]
        vs = [sb(f"c_v{i}", [P, 2, HEADS, HP]) for i in range(2)]
        q_both = [[sb(f"c_q_both{i}{e}", [P, 2 * TOKENS], F32R) for e in range(2)] for i in range(2)]
        k_hi = [[sb(f"c_k_hi{i}{e}", [P, 2 * TOKENS], F32R) for e in range(2)] for i in range(2)]
        k_lo = [sb(f"c_k_lo{i}", [P, 2 * TOKENS], F32R) for i in range(2)]
        prob = sb("c_prob", [P, 4, 2, TOKENS])
        probT = [sb(f"c_probT{i}", [P, 2, TOKENS]) for i in range(2)]
        nmax = sb("c_nmax", [P, 4, 2])
        rden = [sb(f"c_rden{i}", [P, 2 * HEADS]) for i in range(2)]
        attn = [sb(f"c_attn{i}", [P, 2 * CHANNELS]) for i in range(2)]
        st = [sb(f"c_st{i}", [P, NORM_GROUPS * 6]) for i in range(2)]
        ident = sb("c_ident", [P, P])
        ps_s = ctx.enter_context(nc.psum_tensor("c_ps_s", [P, 2, 512], F32))
        ps_p = ctx.enter_context(nc.psum_tensor("c_ps_p", [P, 2, 512], F32))
        ps_t = ctx.enter_context(nc.psum_tensor("c_ps_t", [P, 2, 512], F32))
        ps_o = ctx.enter_context(nc.psum_tensor("c_ps_o", [P, 2, 512], F32))

        qk_landed = [sem(f"c_qk_landed{i}") for i in range(2)]
        v_landed = [sem(f"c_v_landed{i}") for i in range(2)]
        cx_landed = [sem(f"c_cx_landed{i}") for i in range(2)]
        x1_stored = [sem(f"c_x1_stored{i}") for i in range(2)]
        st_stored = [sem(f"c_st_stored{i}") for i in range(2)]
        passed = sem("c_passed")
        probs_sb = [sem(f"c_probs_sb{i}") for i in range(2)]
        (id_landed, cleared, qk_staged, v_staged, cx_summed, x1_made, turned, turned_hi, turned_lo, scores,
         maxed, expd, probs_turned, pv, inverted, scaled, bn_done) = (sem("c_" + n) for n in (
             "id_landed", "cleared", "qk_staged", "v_staged", "cx_summed", "x1_made", "turned", "turned_hi",
             "turned_lo", "scores", "maxed", "expd", "probs_turned", "pv", "inverted", "scaled", "bn_done"))
        block = ctx.enter_context(nc.Block())

        def own(e):
            return slice(HP * e, HP * (e + 1))

        def pair(t, w):
            return view(t, 2 * w, [[1, 2], [HD * WH, HEADS], [WH, HD]])

        @block.sync
        def _(sp):
            sp.dma_start(ident[:, :], a["ident"]).then_inc(id_landed, 16)

            def rows(t, i, h):
                return t[:, :, bass.ds(i, 1), h, :].rearrange("g p o n -> p (g o) n")

            def tile(t):
                return t.rearrange("p (g n) -> p g n", g=CG)

            def store(i, h):
                sp.wait_ge(x1_made, i * 16 + ((h + 1) * HW + 2))
                sp.dma_start(rows(x1, i, h), tile(x1t[h][:, :])).then_inc(x1_stored[h], 16)
                sp.wait_ge(bn_done, i * 2 + (h + 1))
                sp.dma_start(stats[:, bass.ds(i, 1), h, :].rearrange("p o n -> p (o n)"), st[h][:, :]).then_inc(st_stored[h], 16)

            def image(i, first):
                for h in range(2):
                    if not first:
                        sp.wait_ge(qk_staged, (i - 1) * 16 + (h + 1) * HW)
                    for s in range(2):
                        sp.dma_start(tile(rqk[h][:, s, :]), rows(qkc[s], i, h)).then_inc(qk_landed[h], 16)
                    if not first:
                        sp.wait_ge(v_staged, (i - 1) * 16 + (h + 1) * HW)
                    sp.dma_start(tile(rv[h][:, :]), rows(qkv[2], i, h)).then_inc(v_landed[h], 16)
                    if not first:
                        sp.wait_ge(x1_made, (i - 1) * 16 + ((h + 1) * HW + 2))
                    sp.dma_start(tile(rcx[h][:, 0, :]), rows(qkc[2], i, h)).then_inc(cx_landed[h], 16)
                    sp.dma_start(tile(rcx[h][:, 1, :]), rows(a["x_tok"], i, h)).then_inc(cx_landed[h], 16)
                    if not first:
                        store(i - 1, h)

            image(0, True)
            with sp.Fori(1, IMAGES) as i:
                image(i, False)
            for h in range(2):
                store(IMAGES - 1, h)
            for h in range(2):
                sp.wait_ge(x1_stored[h], 16 * (IMAGES + 1))
                sp.wait_ge(st_stored[h], 16 * (IMAGES + 1))

        @block.gpsimd
        def _(pool):
            for p in range(2):
                pool.memset(qk[p][:, :, :, :], 0.0).then_inc(cleared, 1)
                pool.memset(vs[p][:, :, :, :], 1.0).then_inc(cleared, 1)
                pool.sem_inc(x1_stored[p], 16)
                pool.sem_inc(st_stored[p], 16)
            pool.sem_inc(x1_made, 2)
            pool.wait_ge(cleared, 4)

            def stage_qk(i, w):
                h, p = w // HW, w % 2
                if w % HW == 0:
                    pool.wait_ge(qk_landed[h], i * 32 + 32)
                if not (isinstance(i, int) and i * 16 + w < 2):
                    pool.wait_ge(turned, i * 16 + (w - 1))
                pool.sem_inc(passed, 1)
                for s in range(2):
                    dst = qk[p][:, s, :, :].rearrange("p b (h d) -> p b h d", h=HEADS)[:, :, :, 0:HD]
                    m = pool.tensor_copy(dst, pair(rqk[h][:, s, :], w % HW))
                m.then_inc(qk_staged, 1)

            def stage_v(i, w):
                h, p = w // HW, w % 2
                if w % HW == 0:
                    pool.wait_ge(v_landed[h], i * 16 + 16)
                if not (isinstance(i, int) and i * 16 + w < 2):
                    pool.wait_ge(pv, i * 64 + (4 * (w - 1) + 2))
                pool.sem_inc(passed, 1)
                pool.tensor_copy(vs[p][:, :, :, 0:HD], pair(rv[h][:, :], w % HW)).then_inc(v_staged, 1)

            def sum_cx(i, w):
                h = w // HW
                if w % HW == 0:
                    pool.wait_ge(cx_landed[h], i * 32 + 32)
                pool.tensor_tensor(pair(rcx[h][:, 0, :], w % HW), pair(rcx[h][:, 0, :], w % HW),
                                   pair(rcx[h][:, 1, :], w % HW), ALU.add).then_inc(cx_summed, 1)

            def finish(i, w):
                h = w // HW
                if w % HW == 0:
                    pool.wait_ge(x1_stored[h], i * 16 + 16)
                    if not (isinstance(i, int) and i == 0):
                        pool.wait_ge(bn_done, i * 2 + (h - 1))
                pool.wait_ge(scaled, i * 16 + (w + 3))
                pool.wait_ge(cx_summed, i * 16 + (w + 1))
                pool.tensor_tensor(pair(x1t[h][:, :], w % HW),
                                   attn[w % 2][:, :].rearrange("p (b h d) -> p b h d", b=2, h=HEADS),
                                   pair(rcx[h][:, 0, :], w % HW), ALU.add).then_inc(x1_made, 1)

            def image(i, first, last):
                for w in range(2 * HW):
                    if w + 2 < 2 * HW:
                        stage_qk(i, w + 2)
                    elif not last:
                        stage_qk(i + 1, w + 2 - 2 * HW)
                    if w + 1 < 2 * HW:
                        stage_v(i, w + 1)
                        sum_cx(i, w + 1)
                    elif not last:
                        stage_v(i + 1, 0)
                        sum_cx(i + 1, 0)
                    if w:
                        finish(i, w - 1)
                    elif not first:
                        finish(i - 1, 2 * HW - 1)

            stage_qk(0, 0)
            stage_qk(0, 1)
            stage_v(0, 0)
            sum_cx(0, 0)
            image(0, True, False)
            with pool.Fori(1, IMAGES - 1) as i:
                image(i, False, False)
            image(IMAGES - 1, False, True)
            finish(IMAGES - 1, 2 * HW - 1)

        @block.tensor
        def _(pe):
            def turn(n, p):
                pe.wait_ge(qk_staged, n + 1)
                if not (isinstance(n, int) and n == 0):
                    pe.wait_ge(turned_lo, n * 4)
                for s in range(2):
                    for two in range(2):
                        for b in range(2):
                            m = pe.transpose(ps_t[:, s, two * TOKENS + b * P:two * TOKENS + (b + 1) * P],
                                             qk[p][:, s, b, two * P:(two + 1) * P], ident[:, :])
                m.then_inc(turned, 1)

            def score(n, h, p):
                if h == 0:
                    pe.wait_ge(turned_lo, n * 4 + 4)
                if not (isinstance(n, int) and n * 4 + h < 2):
                    pe.wait_ge(expd, n * 8 + 2 * (h - 1))
                e, keys = h % 2, slice(h // 2 * TOKENS, (h // 2 + 1) * TOKENS)
                rows = slice(HP * e, HP * e + HD)
                for b in range(2):
                    out = ps_s[:, e, b * TOKENS:(b + 1) * TOKENS]
                    queries = slice(h // 2 * TOKENS + b * P, h // 2 * TOKENS + (b + 1) * P)
                    pe.matmul(out, q_both[p][e][:, queries], k_hi[p][e][:, keys], start=True, stop=False)
                    m = pe.matmul(out, q_both[p][e][rows, queries], k_lo[p][rows, keys], start=False, stop=True)
                m.then_inc(scores, 1)

            def turn_probs(n, h):
                pe.wait_ge(expd, n * 8 + 2 * (h + 1))
                pe.wait_ge(probs_sb[h % 2], n * 2 + (h // 2 + 1))
                for kb in range(2):
                    for b in range(2):
                        m = pe.transpose(ps_p[:, h % 2, kb * TOKENS + b * P:kb * TOKENS + (b + 1) * P],
                                         prob[:, h, b, kb * P:(kb + 1) * P], ident[:, :])
                m.then_inc(probs_turned, 1)

            def weigh(n, h, p):
                if h == 0:
                    pe.wait_ge(v_staged, n + 1)
                    pe.wait_ge(scaled, n + 1)
                pe.wait_ge(probs_sb[h % 2], n * 2 + (h // 2 + 2))
                for b in range(2):
                    for kb in range(2):
                        m = pe.matmul(ps_o[:, p, (b * HEADS + h) * HP:(b * HEADS + h) * HP + HD + 1],
                                      probT[h % 2][:, kb, b * P:(b + 1) * P], vs[p][:, kb, h, 0:HD + 1],
                                      start=kb == 0, stop=kb == 1)
                m.then_inc(pv, 1)

            def window(n, p, first, ahead):
                for h in range(HEADS):
                    if h < 2:
                        score(n, h + 2, p)
                    elif ahead >= 1:
                        score(n + 1, h - 2, 1 - p)
                    turn_probs(n, h)
                    if h:
                        weigh(n, h - 1, p)
                    elif not first:
                        weigh(n - 1, HEADS - 1, 1 - p)
                    if h == 1 and ahead >= 2:
                        turn(n + 2, p)

            pe.wait_ge(id_landed, 16)
            pe.sem_inc(probs_turned, 4)
            pe.sem_inc(pv, 2)
            turn(0, 0)
            turn(1, 1)
            score(0, 0, 0)
            score(0, 1, 0)
            window(0, 0, True, 2)
            window(1, 1, False, 2)
            with pe.Fori(1, (WINDOWS - 2) // 2) as m:
                n = m * 2
                window(n, 0, False, 2)
                window(n + 1, 1, False, 2)
            window(WINDOWS - 2, 0, False, 1)
            window(WINDOWS - 1, 1, False, 0)
            weigh(WINDOWS - 1, HEADS - 1, 1)

        @block.scalar
        def _(act):
            def upper_q(n, p):
                act.wait_ge(turned, n + 1)
                for e in range(2):
                    act.activation(q_both[p][e][own(e), :], ps_t[own(e), 0, :], ACT.Copy, scale=SCALE).then_inc(turned_hi, 1)

            def upper_k(n, p, e):
                for rows in (own(e), own(1 - e)):
                    act.activation(k_hi[p][e][rows, :], ps_t[own(e), 1, :], ACT.Copy).then_inc(turned_hi, 1)

            def take_probs(n, h):
                act.wait_ge(probs_turned, n * 4 + (h + 5))
                act.wait_ge(pv, n * 4 + (h + 1))
                act.activation(probT[1][:, :, :].rearrange("p a t -> p (a t)"), ps_p[:, 1, :], ACT.Copy).then_inc(probs_sb[1], 1)

            def exps(n, h):
                act.wait_ge(maxed, n * 4 + (h + 1))
                act.wait_ge(probs_turned, n * 4 + (h + 1))
                for b in range(2):
                    act.activation(prob[:, h, b, :], ps_s[:, h % 2, b * TOKENS:(b + 1) * TOKENS], ACT.Exp,
                                   bias=nmax[:, h, b:b + 1]).then_inc(expd, 1)

            def window(n, p, ahead):
                for h in range(HEADS):
                    if h == 2 and ahead >= 2:
                        upper_q(n + 2, p)
                    if h % 2:
                        take_probs(n, h)
                    if h < 2:
                        exps(n, h + 2)
                    elif ahead >= 1:
                        exps(n + 1, h - 2)
                    if h >= 2 and ahead >= 2:
                        upper_k(n + 2, p, h - 2)

            for n in range(2):
                upper_q(n, n)
                for e in range(2):
                    upper_k(n, n, e)
            exps(0, 0)
            exps(0, 1)
            with act.Fori(0, (WINDOWS - 2) // 2) as m:
                n = m * 2
                window(n, 0, 2)
                window(n + 1, 1, 2)
            window(WINDOWS - 2, 0, 1)
            window(WINDOWS - 1, 1, 0)

        @block.vector
        def _(dve):
            def rowmax(n, h):
                dve.wait_ge(scores, n * 4 + (h + 1))
                dve.tensor_reduce(nmax[:, h, :], ps_s[:, h % 2, :].rearrange("p (b t) -> p b t", b=2), AX.X,
                                  ALU.max, negate=True).then_inc(maxed, 1)

            def lower_q(n, p, e):
                dve.wait_ge(turned_hi, n * 6 + 2)
                dve.scalar_tensor_tensor(q_both[p][e][own(1 - e), :], ps_t[own(e), 0, :], SCALE,
                                         q_both[p][e][own(e), :].bitcast(F32), ALU.mult, ALU.subtract).then_inc(turned_lo, 1)

            def lower_k(n, p, e):
                dve.wait_ge(turned_hi, n * 6 + 6)
                dve.tensor_tensor(k_lo[p][own(e), :], ps_t[own(e), 1, :], k_hi[p][e][own(e), :].bitcast(F32),
                                  ALU.subtract).then_inc(turned_lo, 1)

            def take_probs(n, h):
                dve.wait_ge(probs_turned, n * 4 + (h + 5))
                dve.wait_ge(pv, n * 4 + (h + 1))
                dve.tensor_copy(probT[0][:, :, :].rearrange("p a t -> p (a t)"), ps_p[:, 0, :]).then_inc(probs_sb[0], 1)

            def scale(n, p):
                dve.wait_ge(pv, n * 4 + 6)
                flat = ps_o[:, p, :]
                dve.reciprocal(rden[p][:, :], view(flat, HD, [[HP, 2 * HEADS]])).then_inc(inverted, 1)
                dve.wait_ge(inverted, n + 1)
                dve.wait_ge(x1_made, n + 1)
                dve.tensor_tensor(attn[p][:, :].rearrange("p (a d) -> p a d", d=HD),
                                  view(flat, 0, [[HP, 2 * HEADS], [1, HD]]),
                                  view(rden[p][:, :], 0, [[1, 2 * HEADS], [0, HD]]), ALU.mult).then_inc(scaled, 1)

            def statistics(i, h, k):
                if k == 0:
                    dve.wait_ge(x1_made, i * 16 + ((h + 1) * HW + 2))
                    dve.wait_ge(st_stored[h], i * 16 + 16)
                for g in range(k * NORM_GROUPS // PARTS, (k + 1) * NORM_GROUPS // PARTS):
                    m = dve.bn_stats(st[h][:, g * 6:g * 6 + 6], x1t[h][:, g * PER_NORM * WH:(g + 1) * PER_NORM * WH])
                if k == PARTS - 1:
                    m.then_inc(bn_done, 1)

            def image(i, first, last):
                for w in range(2 * HW):
                    n, p = i * 16 + w, w % 2
                    end = last and w + 1 == 2 * HW
                    for h in range(HEADS):
                        if h < 2:
                            rowmax(n, h + 2)
                        elif not end:
                            rowmax(n + 1, h - 2)
                        if h % 2 == 0:
                            take_probs(n, h)
                        if h == 0 and not end:
                            for e in range(2):
                                lower_k(n + 1, 1 - p, e)
                        if h == 1 and not (first and w == 0):
                            scale(n - 1, 1 - p)
                        if h >= 2 and not (last and w + 2 >= 2 * HW):
                            lower_q(n + 2, p, h - 2)
                        if h == 3 and w >= HW + 2:
                            statistics(i, 0, w - HW - 2)
                        elif h == 3 and 2 <= w < HW and not first:
                            statistics(i - 1, 1, w - 2)

            dve.sem_inc(probs_sb[0], 1)
            dve.sem_inc(probs_sb[1], 1)
            dve.sem_inc(scaled, 2)
            for e in range(2):
                lower_q(0, 0, e)
            for e in range(2):
                lower_k(0, 0, e)
            for e in range(2):
                lower_q(1, 1, e)
            rowmax(0, 0)
            rowmax(0, 1)
            image(0, True, False)
            with dve.Fori(1, IMAGES - 1) as i:
                image(i, False, False)
            image(IMAGES - 1, False, True)
            scale(WINDOWS - 1, 1)
            for k in range(PARTS):
                statistics(IMAGES - 1, 1, k)


def stats1_phase(nc, a, stats, norm):
    G = NORM_GROUPS
    BG = IMAGES * G
    with ExitStack() as ctx:
        sb = lambda n, s, d=F32: ctx.enter_context(nc.sbuf_tensor(n, s, d))
        sem = lambda n: ctx.enter_context(nc.semaphore(n))
        st = sb("d_st", [P, HALVES * G * 6])
        ones = sb("d_ones", [P, P])
        pairs = sb("d_pairs", [P, HALVES, G])
        sums = sb("d_sums", [P, IMAGES, G])
        mean = sb("d_mean", [P, IMAGES, G])
        dev = sb("d_dev", [P, IMAGES, G])
        var = sb("d_var", [P, IMAGES, G])
        rstd = sb("d_rstd", [P, IMAGES, G])
        rows = sb("d_rows", [1, G, PER_NORM, 2, IMAGES])
        ps = ctx.enter_context(nc.psum_tensor("d_ps", [P, 4, 512], F32))
        loaded, oned, steps, summed, rooted, stored = (
            sem(n) for n in ("d_loaded", "d_oned", "d_steps", "d_summed", "d_rooted", "d_stored"))
        block = ctx.enter_context(nc.Block())
        flat = lambda t: t[:, :, :].rearrange("p b g -> p (b g)")

        STEP_DEV = 3 + 4 * 4
        STEP_VAR = STEP_DEV + 1

        @block.sync
        def _(sp):
            sp.dma_start(st[:, :], stats.rearrange("p b h n -> p (b h n)")).then_inc(loaded, 16)
            sp.wait_ge(steps, STEP_VAR + 7)
            sp.dma_start(norm.rearrange("(o c) k b -> o (c k b)", o=1),
                         rows[:, :, :, :, :].rearrange("o g c k b -> o (g c k b)")).then_inc(stored, 16)
            sp.wait_ge(stored, 16)

        @block.gpsimd
        def _(pool):
            pool.memset(ones[:, :], 1.0).then_inc(oned, 1)

        @block.tensor
        def _(pe):
            pe.wait_ge(oned, 1)
            for n, (src, after) in enumerate(((sums, 2), (var, STEP_DEV))):
                pe.wait_ge(steps, after)
                for c in range(2):
                    m = pe.matmul(ps[:, 2 * n + c, :], ones[:, :], flat(src)[:, c * 512:(c + 1) * 512],
                                  start=True, stop=True)
                m.then_inc(summed, 1)

        @block.scalar
        def _(act):
            act.wait_ge(steps, STEP_VAR)
            act.activation(flat(dev), flat(var), ACT.Sqrt).then_inc(rooted, 1)

        @block.vector
        def _(dve):
            done = [0]

            def step(ins):
                done[0] += 1
                ins.then_inc(steps, 1)
                dve.wait_ge(steps, done[0])

            def part(o, h):
                return view(st[:, :], h * G * 6 + o, [[2 * G * 6, IMAGES], [6, G]])

            dve.wait_ge(loaded, 16)
            step(dve.tensor_tensor(pairs[:, :, :], view(st[:, :], 1, [[G * 6, HALVES], [6, G]]),
                                   view(st[:, :], 4, [[G * 6, HALVES], [6, G]]), ALU.add))
            step(dve.tensor_tensor(sums[:, :, :], view(flat(pairs), 0, [[2 * G, IMAGES], [1, G]]),
                                   view(flat(pairs), G, [[2 * G, IMAGES], [1, G]]), ALU.add))
            dve.wait_ge(summed, 1)
            step(dve.tensor_scalar(flat(mean), ps[:, 0:2, :].rearrange("p a n -> p (a n)"),
                                   1.0 / (4 * P), None, ALU.mult))
            each = float(PER_NORM * WH // 2)
            n = 0
            for h in range(2):
                for e in range(2):
                    step(dve.tensor_tensor(dev[:, :, :], part(3 * e + 1, h), mean[:, :, :], ALU.subtract))
                    step(dve.tensor_tensor(dev[:, :, :], dev[:, :, :], dev[:, :, :], ALU.mult))
                    dst = var if n == 0 else dev
                    step(dve.scalar_tensor_tensor(dst[:, :, :], dev[:, :, :], each, part(3 * e + 2, h), ALU.mult, ALU.add))
                    step(dve.tensor_tensor(var[:, :, :], var[:, :, :], dev[:, :, :], ALU.add) if n else
                         dve.tensor_scalar(var[:, :, :], var[:, :, :], 0.0, None, ALU.max))
                    n += 1
            dve.wait_ge(summed, 2)
            step(dve.tensor_scalar(flat(var), ps[:, 2:4, :].rearrange("p a n -> p (a n)"),
                                   1.0 / NORM_COUNT, EPS, ALU.mult, ALU.add))
            dve.wait_ge(rooted, 1)
            step(dve.reciprocal(flat(rstd), flat(dev)))
            newton(dve, step, flat(rstd), flat(var), flat(dev))
            step(dve.tensor_tensor(flat(mean), flat(mean), flat(rstd), ALU.mult))
            for c in range(PER_NORM):
                dve.tensor_copy(rows[:, :, c, 0, :], rstd[0:1, :, :].rearrange("p b g -> p g b"))
                m = dve.tensor_copy(rows[:, :, c, 1, :], mean[0:1, :, :].rearrange("p b g -> p g b"))
            step(m)
            assert done[0] == STEP_VAR + 7


def long_phase(nc, a, x1, norm, kpad, out):
    TILE = IMAGES * 2 * C8 * WH
    N = IMAGES * WH
    FAR = (FAR55 - 1) // 2
    TAPS = 2 * FAR + 1
    UNITS = 3
    STEPS = 2 * C8
    NORMS = 5
    with ExitStack() as ctx:
        sb = lambda n, s, d=F32: ctx.enter_context(nc.sbuf_tensor(n, s, d))
        sem = lambda n: ctx.enter_context(nc.semaphore(n))
        raw = [sb(f"e_raw{i}", [P, TILE]) for i in range(2)]
        nrm = [sb(f"e_norm{i}", [P, C8, 2, IMAGES]) for i in range(2)]
        t = [sb(f"e_t{i}", [P, TL55]) for i in range(2)]
        g = sb("e_g", [P, TL55 - PW])
        th = [sb(f"e_th{s}", [P, TAPS * P], F32R) for s in range(UNITS)]
        tl = [sb(f"e_tl{s}", [P, TAPS * P], F32R) for s in range(UNITS)]
        xn = [sb(f"e_xn{e}", [P, N]) for e in range(2)]
        xs = sb("e_xs", [P, N])
        xh = [sb(f"e_xh{s}", [P, N], F32R) for s in range(UNITS)]
        xl = [sb(f"e_xl{s}", [P, N], F32R) for s in range(UNITS)]
        res = [sb(f"e_res{i}", [P, 2, N]) for i in range(2)]
        ps = ctx.enter_context(nc.psum_tensor("e_ps", [P, 2, 4, 512], F32))
        landed = [sem(f"e_landed{i}") for i in range(2)]
        t_landed = [sem(f"e_t_landed{i}") for i in range(2)]
        stored = [sem(f"e_stored{i}") for i in range(2)]
        g_made, normed, hi, lo, prod, taken, done, passed = (
            sem("e_" + n) for n in ("g_made", "normed", "hi", "lo", "prod", "taken", "done", "passed"))
        block = ctx.enter_context(nc.Block())

        def blocks(i, c, e):
            return view(raw[i][:, :], c * WH + e, [[C8 * WH, 2], [2, WH // 2], [2 * C8 * WH, IMAGES]])

        def in_order(ap):
            return ap.rearrange("p (a w b) -> p a w b", a=2, w=WH // 2)

        def matrices(p, s):
            src, first = ((t[p], PW), (g, PW), (g, 2 * PW))[s]
            return view(src[:, :], TL55 - 1 - first, [[-2 * PW, TAPS], [-1, PW], [-U55, HEIGHT]])

        def taps(ap):
            return ap.rearrange("p (d u h) -> p d u h", d=TAPS, u=PW)

        @block.sync
        def _(sp):
            for i in range(2):
                sp.sem_inc(stored[i], 16)

            def load(g, i, first=False):
                if not first:
                    sp.wait_ge(done, g * (2 * C8) + (4 - 4 * C8 + 2 * C8))
                src = x1[bass.ds(g, 1), :, :, :, :].rearrange("o p b h n -> (o p) (b h n)")
                sp.dma_start(raw[i][:, :], src).then_inc(landed[i], 16)
                src = norm[bass.ds(g * C8, C8), :, :].rearrange("c k b -> (c k b)")
                sp.dma_start(nrm[i][:, :, :, :].rearrange("p c k b -> p (c k b)"), src.partition_broadcast(P)).then_inc(landed[i], 16)

            def store(g):
                with sp.Fori(0, C8 // 2) as m:
                    c = m * 2
                    for p in range(2):
                        sp.wait_ge(done, g * (2 * C8) + c * 2 + (2 * p + 6))
                        dst = out[bass.ds(g * C8 + c + p, 1), :, :].rearrange("o p n -> (o p) n")
                        sp.dma_start(dst, res[p][:, :, :].rearrange("p e n -> p (e n)")).then_inc(stored[p], 16)

            load(0, 0, True)
            load(1, 1, True)
            with sp.Fori(0, (CG - 2) // 2) as m:
                g = m * 2
                store(g)
                load(g + 2, 0)
                store(g + 1)
                load(g + 3, 1)
            store(CG - 2)
            store(CG - 1)
            for p in range(2):
                sp.wait_ge(stored[p], 16 * (CHANNELS // 2 + 1))

        @block.gpsimd
        def _(pool):
            def load(c, p):
                row = kpad[bass.ds(c, 1), :]
                src = bass.AP(tensor=row.tensor, offset=row.offset, ap=[[1, PW], [U55, HEIGHT], [1, TL55]])
                pool.dma_start(t[p][:, :], src).then_inc(t_landed[p], 16)

            def differences(c, p, first=False):
                pool.wait_ge(t_landed[p], (c - p) * 8 + 16)
                if not first:
                    pool.wait_ge(lo, c * (2 * UNITS))
                pool.sem_inc(passed, 1)
                pool.tensor_tensor(g[:, :], t[p][:, 0:TL55 - PW], t[p][:, PW:TL55], ALU.subtract).then_inc(g_made, 1)

            def refill(c, p):
                pool.wait_ge(g_made, c + 1)
                pool.wait_ge(lo, c * (2 * UNITS) + 2)
                pool.sem_inc(passed, 1)
                load(c + 2, p)

            for p in range(2):
                load(p, p)
            for p in range(2):
                differences(p, p, first=p == 0)
                refill(p, p)
            with pool.Fori(1, CHANNELS // 2 - 1) as m:
                c = m * 2
                for p in range(2):
                    differences(c + p, p)
                    refill(c + p, p)
            for p in range(2):
                differences(CHANNELS - 2 + p, p)

        @block.scalar
        def _(act):
            with act.Fori(0, CG // 2) as gg:
                for j in range(STEPS):
                    p = j % 2
                    for s in range(UNITS):
                        act.wait_ge(prod, gg * (UNITS * STEPS) + (UNITS * j + s + 1))
                        if s == 0:
                            act.wait_ge(t_landed[p], gg * (16 * C8) + 16 * (j // 2 + 1))
                        if s == 1:
                            act.wait_ge(g_made, gg * STEPS + (j + 1))
                        act.activation(taps(th[s][:, :]), matrices(p, s), ACT.Copy).then_inc(hi, 1)
                        if s == 0:
                            act.wait_ge(normed, gg * (NORMS * STEPS) + NORMS * (j + 1))
                        act.activation(xh[s][:, :], (xs, xn[1], xn[0])[s][:, :], ACT.Copy).then_inc(hi, 1)

        @block.vector
        def _(dve):
            dve.sem_inc(done, 4)

            def normalise(gg, j):
                i, c = j // C8, j % C8
                n = gg * (NORMS * STEPS) + NORMS * j
                if c == 0:
                    dve.wait_ge(landed[i], gg * 32 + 32)
                wide = lambda k: view(nrm[i][:, c, k, :], 0, [[0, 2], [0, WH // 2], [1, IMAGES]])
                for e in range(2):
                    dve.tensor_tensor(in_order(xn[e][:, :]), blocks(i, c, e), wide(0), ALU.mult).then_inc(normed, 1)
                for e in range(2):
                    dve.wait_ge(normed, n + (e + 1))
                    dve.tensor_tensor(in_order(xn[e][:, :]), in_order(xn[e][:, :]), wide(1), ALU.subtract).then_inc(normed, 1)
                dve.wait_ge(normed, n + 4)
                dve.tensor_tensor(xs[:, :], xn[0][:, :], xn[1][:, :], ALU.add).then_inc(normed, 1)
                dve.wait_ge(normed, n + 5)

            def lower(gg, j, s):
                n = gg * (2 * UNITS * STEPS) + 2 * (UNITS * j + s)
                dve.wait_ge(hi, n + 1)
                dve.tensor_tensor(taps(tl[s][:, :]), matrices(j % 2, s), taps(th[s][:, :].bitcast(F32)),
                                  ALU.subtract).then_inc(lo, 1)
                dve.wait_ge(hi, n + 2)
                dve.tensor_tensor(xl[s][:, :], (xs, xn[1], xn[0])[s][:, :], xh[s][:, :].bitcast(F32),
                                  ALU.subtract).then_inc(lo, 1)

            def take(gg, j):
                i, c, p = j // C8, j % C8, j % 2
                dve.wait_ge(prod, gg * (UNITS * STEPS) + UNITS * (j + 2))
                dve.wait_ge(stored[p], gg * (16 * C8) + 16 * (j // 2 + 1))
                for e in range(2):
                    dve.tensor_tensor(in_order(res[p][:, e, :]), in_order(ps[:, p, 0, :]), blocks(i, c, e),
                                      ALU.add).then_inc(taken, 1)
                for e, op in enumerate((ALU.subtract, ALU.add)):
                    dve.wait_ge(taken, gg * (2 * STEPS) + (2 * j + e + 1))
                    dve.tensor_tensor(res[p][:, e, :], res[p][:, e, :], ps[:, p, 1 + e, :], op).then_inc(done, 1)

            def groups(gg, first):
                for j in range(STEPS):
                    normalise(gg, j)
                    for s in range(UNITS):
                        lower(gg, j, s)
                    dve.wait_ge(lo, gg * (2 * UNITS * STEPS) + 2 * UNITS * (j + 1))
                    if j:
                        take(gg, j - 1)
                    elif not first:
                        take(gg - 1, STEPS - 1)

            groups(0, True)
            with dve.Fori(1, CG // 2) as gg:
                groups(gg, False)
            take(CG // 2 - 1, STEPS - 1)

        @block.tensor
        def _(pe):
            pe.sem_inc(prod, UNITS)
            order = sorted(range(-FAR, FAR + 1), key=abs)
            with pe.Fori(0, CHANNELS // 2) as m:
                n = m * 2
                for p in range(2):
                    pe.wait_ge(done, n * 2 + 2 * (p + 1))
                    for s in range(UNITS):
                        pe.wait_ge(lo, n * (2 * UNITS) + 2 * (UNITS * p + s + 1))
                        for d in order:
                            wt = slice((d + FAR) * P, (d + FAR + 1) * P)
                            w0, w1 = max(d, 0), WH + min(d, 0)
                            src = slice((w0 - d) * IMAGES, (w1 - d) * IMAGES)
                            m = matmul3(pe, ps[:, p, s, w0 * IMAGES:w1 * IMAGES], th[s][:, wt], tl[s][:, wt],
                                        xh[s][:, src], xl[s][:, src], start=d == 0, stop=d == order[-1])
                        m.then_inc(prod, 1)


def program(nc, a, out, scratch):
    kpad = scratch("kpad", [CHANNELS, LEN55])
    qkv = [scratch(n, [CG, P, IMAGES, 2, C8 * WH]) for n in ("q", "k", "v")]
    qkc = [scratch(n, [CG, P, IMAGES, 2, C8 * WH]) for n in ("q_conv", "k_conv", "cape")]
    x1 = scratch("x1", [CG, P, IMAGES, 2, C8 * WH])
    stats = scratch("stats", [P, IMAGES, 2, NORM_GROUPS * 6])
    norm = scratch("norm", [CHANNELS, 2, IMAGES])
    filter_phase(nc, a, kpad)
    project_phase(nc, a, qkv)
    depthwise_phase(nc, a, qkv, qkc)
    attention_phase(nc, a, qkv, qkc, x1, stats)
    stats1_phase(nc, a, stats, norm)
    long_phase(nc, a, x1, norm, kpad, out)


def kernel(**inputs):
    import numpy as np
    import concourse.bacc as bacc
    from concourse.bass_utils import run_bass_kernel_spmd

    f = {k: np.asarray(v) for k, v in inputs.items()}
    x = f["x"]
    split = x.reshape(IMAGES, CHANNELS, HEIGHT, 2, WH, PW)
    w = np.concatenate([f["L0_conv_w_qk"].reshape(2 * CHANNELS, CHANNELS), f["L0_conv_w_v"].reshape(CHANNELS, CHANNELS)])
    rest = w.T[P:]
    w_bias = np.zeros((P, QKV), np.float32)
    w_bias[:CHANNELS - P] = rest
    w_bias[[CHANNELS - P, 96]] = np.concatenate([f["L0_conv_b_qk"], f["L0_conv_b_v"]])
    channels = (np.arange(P), P + np.arange(P) % (CHANNELS - P))
    mask = np.stack([np.stack([(k[:, None] // PER_NORM == o[None] // PER_NORM) for o in channels], 1)
                     for k in channels], 1).astype(np.float32)
    w5 = np.zeros((CG, 3, C8, LEN5), np.float32)
    rows = w5[:, :, :, :(2 * HEIGHT - 1) * U5].reshape(CG, 3, C8, 2 * HEIGHT - 1, U5)
    names = ("cape", "q5", "k5")
    for s, name in enumerate(names):
        r0 = HEIGHT - 1 - PAD5
        rows[:, s, :, r0:r0 + K5, 1:1 + K5] = f["L0_conv_w_" + name].reshape(CG, C8, K5, K5)
    chan = np.stack([f["L1_conv_" + n].reshape(KC, KP).T for n in ("deltas", "shift", "bias")], axis=1)
    arrays = {
        "x_ch": split.transpose(0, 1, 3, 4, 5, 2).reshape(IMAGES, CHANNELS, 2, WH * P),
        "x_tok": split.reshape(IMAGES, CG, C8, HEIGHT, 2, WH, PW).transpose(1, 6, 3, 0, 4, 2, 5)
        .reshape(CG, P, IMAGES, 2, C8 * WH),
        "w_first": w.T[:P],
        "w_rest": np.concatenate([rest, rest]),
        "w_bias": w_bias,
        "w5": w5.reshape(CG * 3 * C8, LEN5),
        "bias5": np.stack([f["L0_conv_b_" + n].reshape(CG, C8) for n in names], axis=1).reshape(CG * 3 * C8),
        "z": f["L1_conv_z"][0, :, ::-1, ::-1].reshape(EMB, K55 * K55),
        "dist": f["L1_conv_distance_map"][0, 0, ::-1, ::-1].reshape(K55 * K55),
        "w1t": f["L1_conv_W1"].T,
        "w2t": f["L1_conv_W2"].T,
        "w3t": f["L1_conv_W3"].T,
        "hid": np.stack([f["L1_conv_" + n].reshape(HID) for n in ("b1", "f1", "b2", "f2")], axis=1),
        "chan": chan,
        "mask": mask,
        "ident": np.eye(P, dtype=np.float32),
    }
    arrays = {k: np.ascontiguousarray(v) for k, v in arrays.items()}
    nc = bacc.Bacc("TRN2", target_bir_lowering=False, num_devices=1)
    a = {k: nc.dram_tensor(f"in_{k}", v.shape, F32, kind="ExternalInput").ap() for k, v in arrays.items()}
    out = nc.dram_tensor("out", (CHANNELS, P, WP * IMAGES), F32, kind="ExternalOutput").ap()
    program(nc, a, out, lambda name, shape: nc.dram_tensor(name, shape, F32, kind="Internal").ap())
    r = run_bass_kernel_spmd(nc, [{f"in_{k}": v for k, v in arrays.items()}], core_ids=[0])
    y = r.results[0]["out"].reshape(CHANNELS, PW, HEIGHT, 2, WH, IMAGES)
    return np.ascontiguousarray(y.transpose(5, 0, 2, 4, 3, 1).reshape(IMAGES, CHANNELS, HEIGHT, WIDTH))
```
